# Optimizing a Trainium2 kernel written in Bass

```python
import numpy as np
import jax
import jax.numpy as jnp

def _softmax(x, axis=-1):
    return jax.nn.softmax(x, axis=axis)

def _gelu(x):
    return jax.nn.gelu(x, approximate=True)

def _silu(x):
    return jax.nn.silu(x)

def _sigmoid(x):
    return jax.nn.sigmoid(x)

def _layernorm(x, axis=-1, eps=1e-05):
    m = jnp.mean(x, axis=axis, keepdims=True)
    v = jnp.var(x, axis=axis, keepdims=True)
    return (x - m) / jnp.sqrt(v + eps)

def _scatter_add(tgt, idx, src, axis=0):
    return tgt.at[idx].add(src)

def _segment_sum(src, seg, n):
    return jax.ops.segment_sum(src, seg, n)
kernel_name = 'mk_gnn_preln_d4_gnn_r64_fc6e2d'

def setup_inputs(seed: int=0):
    np.random.seed(seed)
    _w = jnp.asarray

    def _rec_inputs():
        import jax
        import jax.numpy as jnp
        _gk = jax.random.key(seed)
        x = -0.000202 + 1 * jax.random.normal(jax.random.fold_in(_gk, 1), (50000, 128), jnp.float32)
        src = jax.random.randint(jax.random.fold_in(_gk, 2), (12500,), 0, 50000, jnp.int32)
        dst = jax.random.randint(jax.random.fold_in(_gk, 3), (12500,), 0, 50000, jnp.int32)
        _o = jnp.argsort(dst, stable=True)
        src = src[_o]
        dst = dst[_o]
        edge_attr_128 = -8.16379e-05 + 0.999858 * jax.random.normal(jax.random.fold_in(_gk, 12), (12500, 128), jnp.float32)
        edge_weight = jax.random.uniform(jax.random.fold_in(_gk, 15), (12500,), jnp.float32, 0.0, 1)
        return (x, src, dst, edge_attr_128, edge_weight)
    x, src, dst, edge_attr_128, edge_weight = _rec_inputs()

    def _L0_gnn_setup():
        import jax, jax.numpy as jnp
        import numpy as np
        N_NODES = 50000
        N_EDGES = 12500
        D = 128
        N_LAYERS = 3

        def _sage_layer(x, src, dst, inv_deg, Wl, bl, Wr):
            msg = x[src]
            agg = jax.ops.segment_sum(msg, dst, num_segments=N_NODES) * inv_deg
            return agg @ Wl.T + bl + x @ Wr.T
        key = jax.random.key(seed)
        k = jax.random.split(key, 6)
        x = jax.random.normal(k[0], (N_NODES, D), dtype=jnp.float32)
        edge_index = jax.random.randint(k[1], (2, N_EDGES), 0, N_NODES, dtype=jnp.int64)
        scale = 1.0 / np.sqrt(D)
        W_l = jax.random.uniform(k[2], (N_LAYERS, D, D), jnp.float32, -scale, scale)
        b_l = jax.random.uniform(k[3], (N_LAYERS, D), jnp.float32, -scale, scale)
        W_r = jax.random.uniform(k[4], (N_LAYERS, D, D), jnp.float32, -scale, scale)
        return {'x': x, 'edge_index': edge_index, 'W_l': W_l, 'b_l': b_l, 'W_r': W_r}
    _L0_gnn_all = _L0_gnn_setup()
    _L0_gnn_in = {k: v for k, v in _L0_gnn_all.items() if k in ('W_l', 'b_l', 'W_r')}
    del _L0_gnn_all

    def _L1_gnn_setup():
        import jax, jax.numpy as jnp
        import numpy as np
        N = 100000
        E = 10000
        D = 128

        def _weighted_mean_agg(ft, w, src, dst, n_nodes):
            m = ft[src] * w[:, None]
            msum = jax.ops.segment_sum(m, dst, num_segments=n_nodes)
            wsum = jax.ops.segment_sum(w, dst, num_segments=n_nodes)
            safe = jnp.where(wsum > 0, wsum, 1.0)
            return jnp.where((wsum > 0)[:, None], msum / safe[:, None], 0.0)
        key = jax.random.key(seed)
        ks = jax.random.split(key, 10)
        s = 1.0 / np.sqrt(D)
        feat = jax.random.normal(ks[0], (N, D), jnp.float32)
        w = jax.random.uniform(ks[1], (E,), jnp.float32)
        src = jax.random.randint(ks[2], (E,), 0, N, dtype=jnp.int32)
        dst = jax.random.randint(ks[3], (E,), 0, N, dtype=jnp.int32)
        W1 = jax.random.uniform(ks[4], (D, D), jnp.float32, -s, s)
        W2 = jax.random.uniform(ks[5], (D, D), jnp.float32, -s, s)
        sg = 1.0 / np.sqrt(D)
        w_ih = jax.random.uniform(ks[6], (3 * D, 2 * D), jnp.float32, -sg, sg)
        w_hh = jax.random.uniform(ks[7], (3 * D, D), jnp.float32, -sg, sg)
        b_ih = jax.random.uniform(ks[8], (3 * D,), jnp.float32, -sg, sg)
        b_hh = jax.random.uniform(ks[9], (3 * D,), jnp.float32, -sg, sg)
        return {'feat': feat, 'w': w, 'src': src, 'dst': dst, 'W1': W1, 'W2': W2, 'w_ih': w_ih, 'w_hh': w_hh, 'b_ih': b_ih, 'b_hh': b_hh}
    _L1_gnn_all = _L1_gnn_setup()
    _L1_gnn_in = {k: v for k, v in _L1_gnn_all.items() if k in ('W1', 'W2', 'w_ih', 'w_hh', 'b_ih', 'b_hh')}
    del _L1_gnn_all

    def _L2_gnn_setup():
        import jax, jax.numpy as jnp
        import numpy as np
        N_NODES = 50000
        N_EDGES = 12500
        D = 128
        BN_EPS = 0.001
        key = jax.random.key(seed)
        ks = jax.random.split(key, 13)
        s = 1.0 / np.sqrt(D)
        return {'node_features': jax.random.normal(ks[0], (N_NODES, D), jnp.float32), 'edge_features': jax.random.normal(ks[1], (N_EDGES, D), jnp.float32), 'W_node': jax.random.normal(ks[2], (D, D), jnp.float32) * s, 'b_node': jax.random.normal(ks[3], (D,), jnp.float32) * 0.01, 'W_gate': jax.random.normal(ks[4], (D, D), jnp.float32) * s, 'b_gate': jax.random.normal(ks[5], (D,), jnp.float32) * 0.01, 'W_filt': jax.random.normal(ks[6], (D, D), jnp.float32) * s, 'b_filt': jax.random.normal(ks[7], (D,), jnp.float32) * 0.01, 'bn_gamma': jax.random.uniform(ks[8], (D,), jnp.float32, 0.5, 1.5), 'bn_beta': jax.random.normal(ks[9], (D,), jnp.float32) * 0.1, 'bn_mean': jax.random.normal(ks[10], (D,), jnp.float32) * 0.1, 'bn_var': jax.random.uniform(ks[11], (D,), jnp.float32, 0.5, 1.5), 'edge_indices': jax.random.randint(ks[12], (N_EDGES, 2), 0, N_NODES, jnp.int32)}
    _L2_gnn_all = _L2_gnn_setup()
    _L2_gnn_in = {k: v for k, v in _L2_gnn_all.items() if k in ('W_node', 'b_node', 'W_gate', 'b_gate', 'W_filt', 'b_filt', 'bn_gamma', 'bn_beta', 'bn_mean', 'bn_var')}
    del _L2_gnn_all

    def _L3_gnn_setup():
        import jax, jax.numpy as jnp
        import numpy as np
        NUM_NODES = 100000
        NUM_EDGES = 25000
        IN_DIM = 128
        OUT_DIM = 128
        key = jax.random.key(seed)
        k_x, k_e, k_wn, k_bn, k_ws, k_bs = jax.random.split(key, 6)
        x = jax.random.normal(k_x, (NUM_NODES, IN_DIM), dtype=jnp.float32)
        edge_index = jax.random.randint(k_e, (2, NUM_EDGES), 0, NUM_NODES, dtype=jnp.int64)
        s = 1.0 / np.sqrt(IN_DIM)
        W_neigh = jax.random.uniform(k_wn, (OUT_DIM, IN_DIM), dtype=jnp.float32, minval=-s, maxval=s)
        b_neigh = jax.random.uniform(k_bn, (OUT_DIM,), dtype=jnp.float32, minval=-s, maxval=s)
        W_self = jax.random.uniform(k_ws, (OUT_DIM, IN_DIM), dtype=jnp.float32, minval=-s, maxval=s)
        b_self = jax.random.uniform(k_bs, (OUT_DIM,), dtype=jnp.float32, minval=-s, maxval=s)
        return {'x': x, 'edge_index': edge_index, 'W_neigh': W_neigh, 'b_neigh': b_neigh, 'W_self': W_self, 'b_self': b_self}
    _L3_gnn_all = _L3_gnn_setup()
    _L3_gnn_in = {k: v for k, v in _L3_gnn_all.items() if k in ('W_neigh', 'b_neigh', 'W_self', 'b_self')}
    del _L3_gnn_all
    return {'x': x, 'src': src, 'dst': dst, 'edge_attr_128': edge_attr_128, 'edge_weight': edge_weight, 'L0_gnn_W_l': _L0_gnn_in['W_l'], 'L0_gnn_b_l': _L0_gnn_in['b_l'], 'L0_gnn_W_r': _L0_gnn_in['W_r'], 'L1_gnn_W1': _L1_gnn_in['W1'], 'L1_gnn_W2': _L1_gnn_in['W2'], 'L1_gnn_w_ih': _L1_gnn_in['w_ih'], 'L1_gnn_w_hh': _L1_gnn_in['w_hh'], 'L1_gnn_b_ih': _L1_gnn_in['b_ih'], 'L1_gnn_b_hh': _L1_gnn_in['b_hh'], 'L2_gnn_W_node': _L2_gnn_in['W_node'], 'L2_gnn_b_node': _L2_gnn_in['b_node'], 'L2_gnn_W_gate': _L2_gnn_in['W_gate'], 'L2_gnn_b_gate': _L2_gnn_in['b_gate'], 'L2_gnn_W_filt': _L2_gnn_in['W_filt'], 'L2_gnn_b_filt': _L2_gnn_in['b_filt'], 'L2_gnn_bn_gamma': _L2_gnn_in['bn_gamma'], 'L2_gnn_bn_beta': _L2_gnn_in['bn_beta'], 'L2_gnn_bn_mean': _L2_gnn_in['bn_mean'], 'L2_gnn_bn_var': _L2_gnn_in['bn_var'], 'L3_gnn_W_neigh': _L3_gnn_in['W_neigh'], 'L3_gnn_b_neigh': _L3_gnn_in['b_neigh'], 'L3_gnn_W_self': _L3_gnn_in['W_self'], 'L3_gnn_b_self': _L3_gnn_in['b_self']}

def reference(x, src, dst, edge_attr_128, edge_weight, L0_gnn_W_l, L0_gnn_b_l, L0_gnn_W_r, L1_gnn_W1, L1_gnn_W2, L1_gnn_w_ih, L1_gnn_w_hh, L1_gnn_b_ih, L1_gnn_b_hh, L2_gnn_W_node, L2_gnn_b_node, L2_gnn_W_gate, L2_gnn_b_gate, L2_gnn_W_filt, L2_gnn_b_filt, L2_gnn_bn_gamma, L2_gnn_bn_beta, L2_gnn_bn_mean, L2_gnn_bn_var, L3_gnn_W_neigh, L3_gnn_b_neigh, L3_gnn_W_self, L3_gnn_b_self):
    import jax
    import jax.numpy as jnp

    def _L0_gnn_ref(x, edge_index, W_l, b_l, W_r):
        import jax, jax.numpy as jnp
        import numpy as np
        N_NODES = 50000
        N_EDGES = 12500
        D = 128
        N_LAYERS = 3

        def _sage_layer(x, src, dst, inv_deg, Wl, bl, Wr):
            msg = x[src]
            agg = jax.ops.segment_sum(msg, dst, num_segments=N_NODES) * inv_deg
            return agg @ Wl.T + bl + x @ Wr.T
        src = edge_index[0]
        dst = edge_index[1]
        deg = jax.ops.segment_sum(jnp.ones((src.shape[0],), x.dtype), dst, num_segments=N_NODES)
        inv_deg = (1.0 / jnp.maximum(deg, 1.0))[:, None]
        h = x
        for i in range(N_LAYERS):
            h = _sage_layer(h, src, dst, inv_deg, W_l[i], b_l[i], W_r[i])
            if i < N_LAYERS - 1:
                h = jax.nn.relu(h)
        return h

    def _L1_gnn_ref(feat, w, src, dst, W1, W2, w_ih, w_hh, b_ih, b_hh):
        import jax, jax.numpy as jnp
        import numpy as np
        N = 100000
        E = 10000
        D = 128

        def _weighted_mean_agg(ft, w, src, dst, n_nodes):
            m = ft[src] * w[:, None]
            msum = jax.ops.segment_sum(m, dst, num_segments=n_nodes)
            wsum = jax.ops.segment_sum(w, dst, num_segments=n_nodes)
            safe = jnp.where(wsum > 0, wsum, 1.0)
            return jnp.where((wsum > 0)[:, None], msum / safe[:, None], 0.0)
        n = feat.shape[0]
        neigh1 = _weighted_mean_agg(feat, w, src, dst, n)
        neigh2 = _weighted_mean_agg(feat, w, dst, src, n)
        hn = jnp.concatenate([neigh1 @ W1.T, neigh2 @ W2.T], axis=1)
        gi = hn @ w_ih.T + b_ih
        gh = feat @ w_hh.T + b_hh
        i_r, i_z, i_n = jnp.split(gi, 3, axis=1)
        h_r, h_z, h_n = jnp.split(gh, 3, axis=1)
        r = jax.nn.sigmoid(i_r + h_r)
        z = jax.nn.sigmoid(i_z + h_z)
        nn_ = jnp.tanh(i_n + r * h_n)
        return nn_ + z * (feat - nn_)

    def _L2_gnn_ref(node_features, edge_features, W_node, b_node, W_gate, b_gate, W_filt, b_filt, bn_gamma, bn_beta, bn_mean, bn_var, edge_indices):
        import jax, jax.numpy as jnp
        import numpy as np
        N_NODES = 50000
        N_EDGES = 12500
        D = 128
        BN_EPS = 0.001
        n = node_features.shape[0]
        node_hidden = node_features @ W_node + b_node
        gate = jax.nn.sigmoid(edge_features @ W_gate + b_gate)
        filt = edge_features @ W_filt + b_filt
        neighbors = jnp.take(node_hidden, edge_indices[:, 1], axis=0)
        messages = gate * filt * neighbors
        seg = edge_indices[:, 0]
        sums = jax.ops.segment_sum(messages, seg, num_segments=n)
        counts = jax.ops.segment_sum(jnp.ones((seg.shape[0],), jnp.float32), seg, num_segments=n)[:, None]
        aggregated = jnp.where(counts > 0, sums / jnp.maximum(counts, 1.0), 0.0)
        out = node_hidden + aggregated
        out = (out - bn_mean) * jax.lax.rsqrt(bn_var + BN_EPS) * bn_gamma + bn_beta
        return jax.nn.relu(out)

    def _L3_gnn_ref(x, edge_index, W_neigh, b_neigh, W_self, b_self):
        import jax, jax.numpy as jnp
        import numpy as np
        NUM_NODES = 100000
        NUM_EDGES = 25000
        IN_DIM = 128
        OUT_DIM = 128
        src, dst = (edge_index[0], edge_index[1])
        msgs = x[src]
        neigh = jax.ops.segment_sum(msgs, dst, num_segments=x.shape[0])
        neigh_proj = neigh @ W_neigh.T + b_neigh
        self_proj = x @ W_self.T + b_self
        return neigh_proj + self_proj
    edge_index = jnp.stack([src, dst])
    edge_index_t = jnp.stack([src, dst], axis=1)
    h = jnp.maximum(_layernorm(x, axis=-1), 0.0)
    x = x + _L0_gnn_ref(h, edge_index, L0_gnn_W_l, L0_gnn_b_l, L0_gnn_W_r)
    h = jnp.maximum(_layernorm(x, axis=-1), 0.0)
    x = x + _L1_gnn_ref(h, edge_weight, src, dst, L1_gnn_W1, L1_gnn_W2, L1_gnn_w_ih, L1_gnn_w_hh, L1_gnn_b_ih, L1_gnn_b_hh)
    h = jnp.maximum(_layernorm(x, axis=-1), 0.0)
    x = x + _L2_gnn_ref(h, edge_attr_128, L2_gnn_W_node, L2_gnn_b_node, L2_gnn_W_gate, L2_gnn_b_gate, L2_gnn_W_filt, L2_gnn_b_filt, L2_gnn_bn_gamma, L2_gnn_bn_beta, L2_gnn_bn_mean, L2_gnn_bn_var, edge_index_t)
    h = jnp.maximum(_layernorm(x, axis=-1), 0.0)
    x = x + _L3_gnn_ref(h, edge_index, L3_gnn_W_neigh, L3_gnn_b_neigh, L3_gnn_W_self, L3_gnn_b_self)
    return x

_drawn_inputs = setup_inputs


def setup_inputs(seed=0):
    import zlib

    import numpy as np

    out = dict(_drawn_inputs(seed))
    spreads = {}
    factors = {'edge_weight': 64.0,
     'L1_gnn_b_hh': 4.587,
     'L2_gnn_b_node': 8.0,
     'L2_gnn_b_gate': 64.0,
     'L2_gnn_b_filt': 51.542}
    for name, (base, spread) in spreads.items():
        noise = np.random.default_rng([zlib.crc32(name.encode()), seed]).standard_normal(out[name].shape)
        drawn = base * np.exp(spread * noise) if base else spread * noise
        out[name] = jnp.asarray(drawn.astype(out[name].dtype))
    for name, factor in factors.items():
        out[name] = (out[name] * factor).astype(out[name].dtype)
    return out
```

```python
from contextlib import ExitStack

import concourse.bass as bass
from concourse import mybir

F32 = mybir.dt.float32
BF16 = mybir.dt.bfloat16
I32 = mybir.dt.int32
ALU = mybir.AluOpType
ACT = mybir.ActivationFunctionType

P = 128
D = 128
N_NODES = 50000
N_EDGES = 12500
TILES = 100
SLOTS = TILES * P
PAD_NODE = N_NODES
EDGE_ROWS = N_EDGES // TILES
LANES = 4
LN_EPS = 1e-5
BN_EPS = 1e-3

ND, NU = 125, 2
GROUP = ND * NU
ROUNDS = N_NODES // (GROUP * LANES)
SPLIT = 112

(B_HN, B_R, B_Z, B_IN, B_L0, B_L1, B_L2, B_NODE_MSG, B_NODE, B_OUT, B_ZERO, B_GATE, B_FILT, B_SHIFT) = range(14)
NBIAS = 14


class Semaphores:

    def __init__(self, nc):
        self.nc, self.all = nc, []

    def __call__(self, name):
        self.all.append(self.nc.alloc_semaphore(name))
        return self.all[-1]

    def __enter__(self):
        return self

    def __exit__(self, *error):
        if error[0] is None:
            self.nc.clear_and_free_semaphores(self.all)
            self.nc.all_engine_barrier()


def rounds(eng, stages, mine, n, lanes=LANES):
    k = len(stages)
    late = [l * k // lanes for l in range(lanes)]

    def one(j, first=False, last=False):
        for slot in range(k):
            for l in range(lanes):
                s = slot - late[l]
                if s >= 0 and not last and stages[s] in mine:
                    mine[stages[s]](l, j)
                elif s < 0 and not first and stages[s + k] in mine:
                    mine[stages[s + k]](l, j - 1)

    one(0, first=True)
    one(1)
    with eng.Fori(2, n) as j:
        one(j)
    one(n, last=True)


def count(names, j, name):
    return j * len(names) + names.index(name) + 1


def again(j):
    return not (isinstance(j, int) and j == 0)


def bc(ap, n):
    return ap.unsqueeze(1).to_broadcast([ap.shape[0], n, ap.shape[1]])


def col(ap, n):
    return ap.unsqueeze(2).to_broadcast([ap.shape[0], ap.shape[1], n])


class Chip:
    pass


def allocate(nc, ctx):
    c = Chip()

    def sb(name, shape, dt):
        return ctx.enter_context(nc.sbuf_tensor(name, shape, dt))

    c.ident = sb("ident", [P, P], F32)
    c.identb = sb("identb", [P, P], BF16)
    c.wrT = sb("wrT", [P, 3, 2 * D], F32)
    c.whhT = sb("whhT", [P, 3, D], F32)
    c.wfwd = sb("wfwd", [P, 3, D], F32)
    c.wrev = sb("wrev", [P, 3, D], F32)
    c.wnode = sb("wnode", [P, D], F32)
    c.wgf = sb("wgf", [P, 2, D], F32)
    c.wout = sb("wout", [P, 2, D], F32)
    c.bcol = sb("bcol", [P, 2], F32)
    c.bias = sb("bias", [P, NBIAS, D], F32)
    c.bias3 = sb("bias3", [3, NBIAS, D], BF16)
    c.ones3 = sb("ones3", [3, P], BF16)
    c.eps = sb("eps", [P, 4], F32)
    c.minus = sb("minus", [P, 4], F32)
    c.power = sb("power", [P, P], F32)
    return c


def phase_setup(nc, c, a):
    with ExitStack() as ctx:
        def sb(name, shape, dt):
            return ctx.enter_context(nc.sbuf_tensor(name, shape, dt))

        sem = ctx.enter_context(Semaphores(nc))
        raw = sb("raw", [P, 17, D], F32)
        rows = sb("rows", [P, 18, D], F32)
        w12 = sb("w12", [P, 2, D], F32)
        wihT = sb("wihT", [P, 2, 3, D], F32)
        scale = sb("scale", [P, D], F32)
        rstd = sb("bn_rstd", [P, D], F32)
        shifted = sb("shifted", [P, D], F32)
        part = [sb(f"part{i}", [1, NBIAS * D], BF16) for i in range(3)]
        rest = [sb(f"rest{i}", [1, NBIAS * D], F32) for i in range(2)]
        turned = ctx.enter_context(nc.psum_tensor("turned", [P, 17, P], F32))
        folded = ctx.enter_context(nc.psum_tensor("folded", [P, 2, 512], F32))
        loaded = sem("loaded")
        zeroed = sem("zeroed")
        ones_set = sem("ones_set")
        ident_made = sem("ident_made")
        turns_done = sem("turns_done")
        turned_copied = sem("turned_copied")
        folds_done = sem("folds_done")
        folds_copied = sem("folds_copied")
        vec = sem("vec")
        rstd_made = sem("rstd_made")
        parts_placed = sem("parts_placed")
        block = ctx.enter_context(nc.Block())
        IH, HH, NODE, GATE, FILT, GAMMA, BETA, MEAN, VAR, NEIGH, SELF = 3, 6, 9, 10, 11, 12, 13, 14, 15, 16, 17
        loads = []
        for i in range(3):
            loads.append((raw[:, i, :], a["L0_gnn_W_l"][i]))
            loads.append((raw[:, 3 + i, :], a["L0_gnn_W_r"][i]))
            loads.append((raw[:, 6 + i, :], a["L1_gnn_w_hh"][i * D:(i + 1) * D, :]))
            for h in range(2):
                loads.append((raw[:, 9 + 3 * h + i, :], a["L1_gnn_w_ih"][i * D:(i + 1) * D, h * D:(h + 1) * D]))
        loads.append((raw[:, 15, :], a["L3_gnn_W_self"]))
        loads.append((raw[:, 16, :], a["L3_gnn_W_neigh"]))
        loads.append((w12[:, 0, :], a["L1_gnn_W1"]))
        loads.append((w12[:, 1, :], a["L1_gnn_W2"]))
        loads.append((c.wnode[:, :], a["L2_gnn_W_node"]))
        loads.append((c.wgf[:, 0, :], a["L2_gnn_W_gate"]))
        loads.append((c.wgf[:, 1, :], a["L2_gnn_W_filt"]))
        vectors = [a["L0_gnn_b_l"][i] for i in range(3)]
        for v in ("L1_gnn_b_ih", "L1_gnn_b_hh"):
            vectors += [a[v][i * D:(i + 1) * D] for i in range(3)]
        vectors += [a["L2_gnn_" + v] for v in ("b_node", "b_gate", "b_filt", "bn_gamma", "bn_beta", "bn_mean", "bn_var")]
        vectors += [a["L3_gnn_b_neigh"], a["L3_gnn_b_self"]]
        for i, v in enumerate(vectors):
            loads.append((rows[:, i, :], v.partition_broadcast(P)))
        for i in range(2):
            loads.append((c.bcol[:, i:i + 1], a["L0_gnn_b_l"][i].rearrange("(p x) -> p x", x=1)))

        @block.sync
        def _(sp):
            for out, src in loads:
                sp.dma_start(out, src).then_inc(loaded, 16)
            sp.wait_ge(vec, 22)
            for i in range(3):
                sp.dma_start(c.bias3[i:i + 1, :, :].rearrange("a b d -> a (b d)"), part[i][:, :]).then_inc(parts_placed, 16)
            sp.wait_ge(parts_placed, 48)

        @block.gpsimd
        def _(pool):
            pool.memset(c.ident[:, :], 0.0).then_inc(zeroed, 1)
            pool.memset(c.ones3[:, :], 1.0).then_inc(ones_set, 1)
            pool.wait_ge(zeroed, 1)
            pool.affine_select(out=c.ident[:, :], in_=c.ident[:, :], compare_op=ALU.not_equal, fill=1.0,
                               base=0, pattern=[[-1, P]], channel_multiplier=1).then_inc(ident_made, 1)
            pool.memset(c.power[:, :], -0.5).then_inc(zeroed, 1)
            pool.memset(c.eps[:, :], LN_EPS)
            pool.memset(c.minus[:, :], -1.0)
            pool.wait_ge(loaded, 16 * len(loads))
            pool.tensor_scalar(scale[:, :], rows[:, VAR, :], BN_EPS, None, ALU.add).then_inc(zeroed, 1)
            pool.wait_ge(zeroed, 3)
            pool.tensor_tensor(rstd[:, :], scale[:, :], c.power[:, :], ALU.pow).then_inc(rstd_made, 1)

        @block.tensor
        def _(pe):
            pe.wait_ge(ident_made, 1)
            pe.wait_ge(loaded, 16 * len(loads))
            for i in range(17):
                pe.transpose(turned[:, i, :], raw[:, i, :], c.ident[:, :]).then_inc(turns_done, 1)
            pe.wait_ge(turned_copied, 17)
            for h in range(2):
                pe.matmul(folded[:, h, 0:3 * D], w12[:, h, :], wihT[:, h, :, :].rearrange("p g d -> p (g d)"),
                          start=True, stop=True).then_inc(folds_done, 1)

        @block.scalar
        def _(act):
            place = [c.wrT[:, i, D:2 * D] for i in range(3)] + [c.wrT[:, i, 0:D] for i in range(3)]
            place += [c.whhT[:, i, :] for i in (1, 2, 0)]
            place += [wihT[:, h, i, :] for h in range(2) for i in range(3)]
            place += [c.wout[:, 0, :], c.wout[:, 1, :]]
            for i, out in enumerate(place):
                act.wait_ge(turns_done, 17)
                nc.scalar.activation(out, turned[:, i, :], ACT.Copy).then_inc(turned_copied, 1)
            for h, out in enumerate((c.wfwd, c.wrev)):
                act.wait_ge(folds_done, 2)
                nc.scalar.activation(out[:, :, :], folded[:, h, 0:3 * D].rearrange("p (g d) -> p g d", g=3),
                                     ACT.Copy).then_inc(folds_copied, 1)

        @block.vector
        def _(dve):
            dve.wait_ge(ident_made, 1)
            nc.vector.tensor_copy(c.identb[:, :], c.ident[:, :]).then_inc(vec, 1)
            dve.wait_ge(loaded, 16 * len(loads))
            b = c.bias
            for out, row in ((B_HN, HH + 2), (B_IN, IH + 2), (B_L0, 0), (B_L1, 1), (B_L2, 2), (B_GATE, GATE), (B_FILT, FILT)):
                nc.vector.tensor_copy(b[:, out, :], rows[:, row, :]).then_inc(vec, 1)
            nc.vector.memset(b[:, B_ZERO, :], 0.0)
            for out, x, y in ((B_R, IH, HH), (B_Z, IH + 1, HH + 1), (B_OUT, NEIGH, SELF)):
                nc.vector.tensor_tensor(b[:, out, :], rows[:, x, :], rows[:, y, :], ALU.add).then_inc(vec, 1)
            dve.wait_ge(rstd_made, 1)
            nc.vector.tensor_tensor(scale[:, :], rstd[:, :], rows[:, GAMMA, :], ALU.mult).then_inc(vec, 1)
            dve.wait_ge(vec, 12)
            nc.vector.tensor_tensor(c.wnode[:, :], c.wnode[:, :], scale[:, :], ALU.mult).then_inc(vec, 1)
            nc.vector.tensor_tensor(b[:, B_NODE_MSG, :], rows[:, NODE, :], scale[:, :], ALU.mult).then_inc(vec, 1)
            nc.vector.tensor_tensor(shifted[:, :], rows[:, MEAN, :], scale[:, :], ALU.mult).then_inc(vec, 1)
            dve.wait_ge(vec, 15)
            nc.vector.tensor_tensor(b[:, B_SHIFT, :], rows[:, BETA, :], shifted[:, :], ALU.subtract).then_inc(vec, 1)
            dve.wait_ge(vec, 16)
            nc.vector.tensor_tensor(b[:, B_NODE, :], b[:, B_NODE_MSG, :], b[:, B_SHIFT, :], ALU.add).then_inc(vec, 1)
            dve.wait_ge(vec, 17)
            whole = b[0:1, :, :].rearrange("a b d -> a (b d)")
            nc.vector.tensor_copy(part[0][:, :], whole).then_inc(vec, 1)
            dve.wait_ge(vec, 18)
            nc.vector.tensor_tensor(rest[0][:, :], whole, part[0][:, :], ALU.subtract).then_inc(vec, 1)
            dve.wait_ge(vec, 19)
            nc.vector.tensor_copy(part[1][:, :], rest[0][:, :]).then_inc(vec, 1)
            dve.wait_ge(vec, 20)
            nc.vector.tensor_tensor(rest[1][:, :], rest[0][:, :], part[1][:, :], ALU.subtract).then_inc(vec, 1)
            dve.wait_ge(vec, 21)
            nc.vector.tensor_copy(part[2][:, :], rest[1][:, :]).then_inc(vec, 1)


def phase_dense(nc, c, x_dram, out_dram):
    x_view = x_dram.rearrange("(g p u) d -> g p u d", p=ND, u=NU)
    out_view = out_dram.rearrange("(g p u) d -> g p u d", p=ND, u=NU)
    LN = ("0", "1", "2", "3")
    PE = ["h0T", "h1T", "h2T", "h3", "h4T", "gates", "h5T", "node", "h6T", "self"]
    AC = ["h0", "h1T", "h4", "rz", "n", "h5", "h5T", "h6", "h6T"]
    DV = (["stats0", "mean0", "h0T", "h2T", "x1", "stats1", "mean1", "h4T", "r hn", "n in", "z mix", "x2", "stats2", "mean2",
           "x3", "stats3", "mean3", "out"])
    PO = ["var0", "rstd0", "m0", "shift0", "var1", "rstd1", "m1", "shift1", "h4 - n", "n + x1",
          "var2", "rstd2", "m2", "shift2", "var3", "rstd3", "m3", "shift3"]
    STAGES = ["load", "ln0", "rstd0", "h0", "h0T", "h0T copy", "h1T", "h1T relu", "h2T", "h2T relu", "h3", "ln1", "rstd1", "h4", "h4T",
              "h4T copy", "gates", "rz", "n in", "n", "mix", "ln2", "rstd2", "h5", "h5T", "h5T copy", "node", "ln3", "rstd3", "h6", "h6T",
              "h6T copy", "self", "out", "store"]
    with ExitStack() as ctx:
        def sb(name, shape, dt=F32):
            return [ctx.enter_context(nc.sbuf_tensor(f"{name}{l}", shape, dt)) for l in range(LANES)]

        semaphore = ctx.enter_context(Semaphores(nc))

        def sems(name):
            return [semaphore(f"{name}{l}") for l in range(LANES)]

        x = sb("x", [ND, NU, D])
        x1 = sb("x1", [ND, NU, D])
        x2 = sb("x2", [ND, NU, D])
        x3 = sb("x3", [ND, NU, D])
        y = sb("y", [ND, NU, D])
        h = sb("h", [ND, NU, D])
        h4 = sb("h4", [ND, NU, D])
        hT = sb("hT", [P, GROUP])
        gT = sb("gT", [P, GROUP])
        rz = sb("rz", [ND, NU, 2 * D])
        u = sb("u", [ND, NU, D])
        n = sb("n", [ND, NU, D])
        apart = sb("apart", [ND, NU, D])
        both = sb("both", [ND, NU, D])
        stats = sb("stats", [ND, NU, 6])
        mv = sb("mv", [ND, NU, 2])
        var = sb("var", [ND, NU])
        scaled = sb("scaled", [ND, NU])
        rstd = sb("rstd", [ND, NU])
        shift = sb("shift", [ND, NU])
        pause = ctx.enter_context(nc.sbuf_tensor("pause", [ND, 1], F32))
        left = [ctx.enter_context(nc.psum_tensor(f"left{l}", [P, 512], F32)) for l in range(LANES)]
        right = [ctx.enter_context(nc.psum_tensor(f"right{l}", [P, 512], F32)) for l in range(LANES)]
        loaded, stored = sems("x_loaded"), sems("out_stored")
        pe_done, act_done, dve_done, pool_done = sems("pe_done"), sems("act_done"), sems("dve_done"), sems("pool_done")
        block = ctx.enter_context(nc.Block())

        def rows(t):
            return t[0:ND, 0:GROUP // ND * D].rearrange("p (u d) -> p u d", u=NU)

        def dv(j, name):
            return count(DV, j, name)

        def ac(j, name):
            return count(AC, j, name)

        def pn(j, name):
            return count(PE, j, name)

        @block.sync
        def _(sp):
            def load(l, j):
                if again(j):
                    sp.wait_ge(dve_done[l], dv(j - 1, "x1"))
                g = j * LANES + l
                for lo, hi in ((0, SPLIT), (SPLIT, ND)):
                    sp.dma_start(x[l][lo:hi, :, :], x_view[bass.ds(g, 1), lo:hi].rearrange("g p u d -> (g p) u d")
                                 if not isinstance(g, int) else x_view[g, lo:hi]).then_inc(loaded[l], 16)

            rounds(sp, STAGES, {"load": load}, ROUNDS)

        @block.gpsimd
        def _(pool):
            def factors(k):
                def go(l, j):
                    pool.wait_ge(dve_done[l], dv(j, "mean" + k))
                    pool.tensor_tensor(var[l][:, :], mv[l][:, :, 1], c.eps[0:ND, 0:NU], ALU.add).then_inc(pool_done[l], 1)
                    pool.wait_ge(pool_done[l], count(PO, j, "var" + k))
                    pool.tensor_tensor(rstd[l][:, :], var[l][:, :], c.power[0:ND, 0:NU], ALU.pow).then_inc(pool_done[l], 1)
                    pool.wait_ge(pool_done[l], count(PO, j, "rstd" + k))
                    pool.tensor_tensor(scaled[l][:, :], mv[l][:, :, 0], rstd[l][:, :], ALU.mult).then_inc(pool_done[l], 1)
                    pool.wait_ge(pool_done[l], count(PO, j, "m" + k))
                    pool.tensor_tensor(shift[l][:, :], scaled[l][:, :], c.minus[0:ND, 0:NU], ALU.mult).then_inc(pool_done[l], 1)
                return go

            def mix(l, j):
                pool.wait_ge(act_done[l], ac(j, "n"))
                if again(j):
                    pool.wait_ge(dve_done[l], dv(j - 1, "x2"))
                pool.tensor_tensor(apart[l][:, :, :], h4[l][:, :, :], n[l][:, :, :], ALU.subtract).then_inc(pool_done[l], 1)
                pool.tensor_tensor(both[l][:, :, :], n[l][:, :, :], x1[l][:, :, :], ALU.add).then_inc(pool_done[l], 1)

            def store(l, j):
                pool.wait_ge(dve_done[l], dv(j, "out"))
                g = j * LANES + l
                for lo, hi in ((0, SPLIT), (SPLIT, ND)):
                    pool.dma_start(out_view[bass.ds(g, 1), lo:hi].rearrange("g p u d -> (g p) u d")
                                   if not isinstance(g, int) else out_view[g, lo:hi], y[l][lo:hi, :, :]).then_inc(stored[l], 16)

            rounds(pool, STAGES, {"mix": mix, "store": store} | {"rstd" + k: factors(k) for k in "0123"}, ROUNDS)
            for l in range(LANES):
                pool.wait_ge(stored[l], 32 * ROUNDS)

        @block.tensor
        def _(pe):
            def turn(out, src, l, j, name):
                for i in range(NU):
                    last = pe.transpose(out[l][:, i * ND:(i + 1) * ND], src[l][:, i, :], c.ident[0:ND, 0:ND])
                last.then_inc(pe_done[l], 1)

            def h0T(l, j):
                pe.wait_ge(act_done[l], ac(j, "h0"))
                if again(j):
                    pe.wait_ge(act_done[l], ac(j - 1, "h6T"))
                turn(left, h, l, j, "h0T")

            def h1T(l, j):
                pe.wait_ge(dve_done[l], dv(j, "h0T"))
                if again(j):
                    pe.wait_ge(dve_done[l], dv(j - 1, "out"))
                pe.matmul(right[l][:, 0:GROUP], c.wrT[:, 0, 0:D], hT[l][:, :], start=True, stop=True).then_inc(pe_done[l], 1)

            def h2T(l, j):
                pe.wait_ge(act_done[l], ac(j, "h1T"))
                pe.matmul(left[l][:, 0:GROUP], c.wrT[:, 1, 0:D], gT[l][:, :], start=True, stop=True).then_inc(pe_done[l], 1)

            def rowwise(l, lhs, rhs, bias):
                for i in range(NU):
                    o = right[l][0:ND, i * D:(i + 1) * D]
                    pe.matmul(o, c.ones3[:, 0:ND], c.bias3[:, bias, :], start=True, stop=False)
                    last = pe.matmul(o, lhs[l][:, i * ND:(i + 1) * ND], rhs, start=False, stop=True)
                last.then_inc(pe_done[l], 1)

            def h3(l, j):
                pe.wait_ge(dve_done[l], dv(j, "h2T"))
                rowwise(l, hT, c.wrT[:, 2, 0:D], B_L2)

            def h4T(l, j):
                pe.wait_ge(act_done[l], ac(j, "h4"))
                turn(left, h4, l, j, "h4T")

            def gates(l, j):
                pe.wait_ge(dve_done[l], dv(j, "h4T"))
                for i in range(NU):
                    o = right[l][0:ND, i * D:(i + 1) * D]
                    pe.matmul(o, c.ones3[:, 0:ND], c.bias3[:, B_HN, :], start=True, stop=False)
                    pe.matmul(o, gT[l][:, i * ND:(i + 1) * ND], c.whhT[:, 0, :], start=False, stop=True)
                for i in range(NU):
                    o = left[l][0:ND, i * 2 * D:(i + 1) * 2 * D]
                    pe.matmul(o, c.ones3[:, 0:ND], c.bias3[:, B_R:B_Z + 1, :].rearrange("a b d -> a (b d)"),
                              start=True, stop=False)
                    last = pe.matmul(o, gT[l][:, i * ND:(i + 1) * ND], c.whhT[:, 1:3, :].rearrange("p g d -> p (g d)"),
                                     start=False, stop=True)
                last.then_inc(pe_done[l], 1)

            def h5T(l, j):
                pe.wait_ge(act_done[l], ac(j, "h5"))
                turn(left, h, l, j, "h5T")

            def node(l, j):
                pe.wait_ge(act_done[l], ac(j, "h5T"))
                pe.wait_ge(dve_done[l], dv(j, "r hn"))
                rowwise(l, hT, c.wnode[:, :], B_NODE)

            def h6T(l, j):
                pe.wait_ge(act_done[l], ac(j, "h6"))
                turn(left, h, l, j, "h6T")

            def own(l, j):
                pe.wait_ge(act_done[l], ac(j, "h6T"))
                rowwise(l, gT, c.wout[:, 0, :], B_OUT)

            rounds(pe, STAGES, {"h0T": h0T, "h1T": h1T, "h2T": h2T, "h3": h3, "h4T": h4T, "gates": gates, "h5T": h5T,
                                "node": node, "h6T": h6T, "self": own}, ROUNDS)

        @block.scalar
        def _(act):
            def normalized(out, src, l):
                for i in range(NU):
                    last = nc.scalar.activation(out[l][:, i, :], src[l][:, i, :], ACT.Relu, bias=shift[l][:, i:i + 1],
                                                scale=rstd[l][:, i:i + 1])
                last.then_inc(act_done[l], 1)

            def h0(l, j):
                act.wait_ge(pool_done[l], count(PO, j, "shift0"))
                if again(j):
                    act.wait_ge(pe_done[l], pn(j - 1, "h6T"))
                normalized(h, x, l)

            def h1T(l, j):
                act.wait_ge(pe_done[l], pn(j, "h1T"))
                nc.scalar.activation(gT[l][:, :], right[l][:, 0:GROUP], ACT.Relu, bias=c.bcol[:, 0:1]).then_inc(act_done[l], 1)

            def h4_(l, j):
                act.wait_ge(pool_done[l], count(PO, j, "shift1"))
                if again(j):
                    act.wait_ge(pool_done[l], count(PO, j - 1, "h4 - n"))
                normalized(h4, x1, l)

            def rz_(l, j):
                act.wait_ge(pe_done[l], pn(j, "gates"))
                nc.scalar.activation(rz[l][:, :, :], left[l][0:ND, :].rearrange("p (u c) -> p u c", u=NU), ACT.Tanh,
                                     scale=0.5).then_inc(act_done[l], 1)

            def n_(l, j):
                act.wait_ge(dve_done[l], dv(j, "n in"))
                nc.scalar.activation(n[l][:, :, :], u[l][:, :, :], ACT.Tanh).then_inc(act_done[l], 1)

            def h5(l, j):
                act.wait_ge(pool_done[l], count(PO, j, "shift2"))
                normalized(h, x2, l)

            def h5T(l, j):
                act.wait_ge(pe_done[l], pn(j, "h5T"))
                nc.scalar.activation(hT[l][:, :], left[l][:, 0:GROUP], ACT.Copy).then_inc(act_done[l], 1)

            def h6(l, j):
                act.wait_ge(pool_done[l], count(PO, j, "shift3"))
                normalized(h, x3, l)

            def h6T(l, j):
                act.wait_ge(pe_done[l], pn(j, "h6T"))
                nc.scalar.activation(gT[l][:, :], left[l][:, 0:GROUP], ACT.Copy).then_inc(act_done[l], 1)

            rounds(act, STAGES, {"h0": h0, "h1T relu": h1T, "h4": h4_, "rz": rz_, "n": n_, "h5": h5, "h5T copy": h5T,
                                 "h6": h6, "h6T copy": h6T}, ROUNDS)

        @block.vector
        def _(dve):
            def moments(l, j, src, k):
                for i in range(NU):
                    last = nc.vector.bn_stats(stats[l][:, i, :], src[l][:, i, :])
                last.then_inc(dve_done[l], 1)
                dve.wait_ge(dve_done[l], dv(j, "stats" + k))
                nc.vector.memset(pause[:, :], 0.0)
                for i in range(NU):
                    last = nc.vector.bn_aggr(mv[l][:, i, :], stats[l][:, i, :])
                last.then_inc(dve_done[l], 1)

            def ln0(l, j):
                dve.wait_ge(loaded[l], (j + 1) * 32)
                moments(l, j, x, "0")

            def h0T(l, j):
                dve.wait_ge(pe_done[l], pn(j, "h0T"))
                nc.vector.tensor_copy(hT[l][:, :], left[l][:, 0:GROUP]).then_inc(dve_done[l], 1)

            def h2T(l, j):
                dve.wait_ge(pe_done[l], pn(j, "h2T"))
                nc.vector.tensor_scalar(hT[l][:, :], left[l][:, 0:GROUP], c.bcol[:, 1:2], 0.0, ALU.add, ALU.max)\
                    .then_inc(dve_done[l], 1)

            def ln1(l, j):
                dve.wait_ge(pe_done[l], pn(j, "h3"))
                if again(j):
                    dve.wait_ge(pool_done[l], count(PO, j - 1, "n + x1"))
                nc.vector.tensor_tensor(x1[l][:, :, :], rows(right[l]), x[l][:, :, :], ALU.add).then_inc(dve_done[l], 1)
                dve.wait_ge(dve_done[l], dv(j, "x1"))
                moments(l, j, x1, "1")

            def h4T(l, j):
                dve.wait_ge(pe_done[l], pn(j, "h4T"))
                nc.vector.tensor_copy(gT[l][:, :], left[l][:, 0:GROUP]).then_inc(dve_done[l], 1)

            def n_in(l, j):
                dve.wait_ge(act_done[l], ac(j, "rz"))
                nc.vector.scalar_tensor_tensor(u[l][:, :, :], rz[l][:, :, 0:D], 1.0, rows(right[l]), ALU.add, ALU.mult)\
                    .then_inc(dve_done[l], 1)
                dve.wait_ge(dve_done[l], dv(j, "r hn"))
                nc.vector.scalar_tensor_tensor(u[l][:, :, :], u[l][:, :, :], 0.5, bc(c.bias[0:ND, B_IN, :], NU),
                                               ALU.mult, ALU.add).then_inc(dve_done[l], 1)

            def ln2(l, j):
                dve.wait_ge(pool_done[l], count(PO, j, "n + x1"))
                nc.vector.scalar_tensor_tensor(u[l][:, :, :], rz[l][:, :, D:2 * D], 1.0, apart[l][:, :, :], ALU.add, ALU.mult)\
                    .then_inc(dve_done[l], 1)
                dve.wait_ge(dve_done[l], dv(j, "z mix"))
                nc.vector.scalar_tensor_tensor(x2[l][:, :, :], u[l][:, :, :], 0.5, both[l][:, :, :], ALU.mult, ALU.add)\
                    .then_inc(dve_done[l], 1)
                dve.wait_ge(dve_done[l], dv(j, "x2"))
                moments(l, j, x2, "2")

            def ln3(l, j):
                dve.wait_ge(pe_done[l], pn(j, "node"))
                nc.vector.scalar_tensor_tensor(x3[l][:, :, :], rows(right[l]), 0.0, x2[l][:, :, :], ALU.max, ALU.add)\
                    .then_inc(dve_done[l], 1)
                dve.wait_ge(dve_done[l], dv(j, "x3"))
                moments(l, j, x3, "3")

            def out(l, j):
                dve.wait_ge(pe_done[l], pn(j, "self"))
                if again(j):
                    dve.wait_ge(stored[l], j * 32)
                nc.vector.tensor_tensor(y[l][:, :, :], rows(right[l]), x3[l][:, :, :], ALU.add).then_inc(dve_done[l], 1)

            rounds(dve, STAGES, {"ln0": ln0, "h0T copy": h0T, "h2T relu": h2T, "ln1": ln1, "h4T copy": h4T, "n in": n_in,
                                 "ln2": ln2, "ln3": ln3, "out": out}, ROUNDS)


class Work:

    def __init__(self, nc, ctx, name):
        self.nc, self.ctx, self.name = nc, ctx, name
        self.semaphore = ctx.enter_context(Semaphores(nc))

    def sb(self, name, shape, dt=F32):
        return [self.one(f"{name}{l}", shape, dt) for l in range(LANES)]

    def one(self, name, shape, dt=F32):
        return self.ctx.enter_context(self.nc.sbuf_tensor(f"{self.name}_{name}", shape, dt))

    def bank(self, name):
        return self.ctx.enter_context(self.nc.psum_tensor(f"{self.name}_{name}", [P, 512], F32))

    def banks(self, name):
        return [self.bank(f"{name}{l}") for l in range(LANES)]

    def sem(self, name):
        return self.semaphore(f"{self.name}_{name}")

    def sems(self, name):
        return [self.sem(f"{name}{l}") for l in range(LANES)]


def one_of(t, j):
    return t[:, j] if isinstance(j, int) else t[:, bass.ds(j, 1)].rearrange(
        "p a b -> p (a b)" if len(t.shape) == 3 else "p a b c -> p (a b) c")


def column(t, j):
    return t[:, j:j + 1] if isinstance(j, int) else t[:, bass.ds(j, 1)]


def tile_rows(table, j):
    return table[j * P:(j + 1) * P] if isinstance(j, int) else table[bass.ds(j * P, P)]


def row_bounds(pool):
    found = {}
    for row in (P * NHI - 1, SLOTS - 1, SLOTS, N_NODES - 1, N_EDGES - 1):
        found[row] = pool.alloc_register(f"before_bound{row}"), pool.alloc_register(f"bound{row}")
        pool.reg_mov(found[row][0], row - 1)
    return found


def gather(pool, out, table, index, bound):
    kept, bound = bound
    pool.reg_alu(bound, kept, 1, ALU.add)
    return pool.indirect_dma_start(out=out, out_offset=None, in_=table, in_offset=bass.IndirectOffsetOnAxis(ap=index, axis=0),
                                   bounds_check=bound, oob_is_err=False)


def scatter(pool, table, index, src, bound):
    kept, bound = bound
    pool.reg_alu(bound, kept, 1, ALU.add)
    return pool.indirect_dma_start(out=table, out_offset=bass.IndirectOffsetOnAxis(ap=index, axis=0), in_=src, in_offset=None,
                                   bounds_check=bound, oob_is_err=False)


(R_SRC, R_DST, R_EDGE, R_SRC_IN, R_SRC_OUT, R_DST_OUT, R_WRITE_SRC, R_WRITE_DST, R_WEIGHT, R_PLACE, R_SRC_KEY,
 R_DST_KEY) = range(12)
FIELDS = 16
NHI = -(-(PAD_NODE + 1) // P)
BY_DST, BY_SRC = 0, 1


def phase_order(nc, c, a, d):
    DV = ["lo", "hi", "before", "rank", "kept"]
    AC = ["turned bf16", "turned f32", "histogram"]
    PE = ["turned", "same", "rank"]
    STAGES = ["one-hot", "turn", "turned", "same", "before", "snapshot", "add", "look", "keep"]
    n_rounds = TILES // 2
    with ExitStack() as ctx:
        w = Work(nc, ctx, "order")
        keys = w.one("keys", [P, 2, TILES], I32)
        parts = w.one("parts", [P, 2, 2, TILES], I32)
        lof = w.one("lof", [P, 2, TILES])
        hif = w.one("hif", [P, 2, TILES])
        keyf = w.one("keyf", [P, 2, TILES])
        entry = w.one("entry", [P, 2, TILES], I32)
        weight = w.one("weight", [P, TILES])
        edge = w.one("edge", [P, TILES])
        rank = w.one("rank", [P, 2, TILES])
        ramp = w.one("ramp", [P, NHI])
        earlier = w.one("earlier", [P, P])
        onlo, onloT = w.sb("onlo", [P, P], BF16), w.sb("onloT", [P, P], BF16)
        onloTf = w.sb("onloTf", [P, P])
        onhi = w.sb("onhi", [P, NHI], BF16)
        lesser = w.sb("lesser", [P, P], BF16)
        history = w.sb("history", [P, NHI])
        product = w.sb("product", [P, NHI])
        found = w.sb("found", [P, 1])
        zero = w.one("zero", [P, NHI])
        zerob = w.one("zerob", [P, NHI], BF16)
        counts = w.one("counts", [P, 2, NHI])
        running = w.one("running", [P, 2, NHI])
        total = w.one("total", [P, 2])
        offset = w.one("offset", [P, 2])
        start = w.one("start", [P, 2, NHI])
        starts = w.one("starts", [P, NHI, 2], I32)
        work = w.banks("work")
        hist = [w.bank("hist0"), w.bank("hist1")]
        loaded, made, prepared, setup = w.sem("loaded"), w.sem("made"), w.sem("prepared"), w.sem("setup")
        pe_done, act_done, dve_done = w.sems("pe_done"), w.sems("act_done"), w.sems("dve_done")
        added = [w.sem("added0"), w.sem("added1")]
        snapped = [w.sem("snapped0"), w.sem("snapped1")]
        table_step, table_stored, sums_done = w.sem("table_step"), w.sem("table_stored"), w.sem("sums_done")

        with nc.Block() as block:
            @block.sync
            def _(sp):
                sp.wait_ge(made, 8)
                for k, name in ((BY_DST, "dst"), (BY_SRC, "src")):
                    sp.dma_start(keys[0:EDGE_ROWS, k, :], a[name].rearrange("(p t) -> p t", t=TILES)).then_inc(loaded, 16)
                sp.dma_start(weight[0:EDGE_ROWS, :], a["edge_weight"].rearrange("(p t) -> p t", t=TILES)).then_inc(loaded, 16)
                sp.wait_ge(table_step, 9)
                sp.dma_start(d["starts"].rearrange("(p h) k -> p h k", p=P), starts[:, :, :]).then_inc(table_stored, 16)
                sp.wait_ge(table_stored, 16)

            @block.gpsimd
            def _(pool):
                pool.memset(keys[:, :, :], PAD_NODE).then_inc(made, 1)
                pool.memset(weight[:, :], 0.0).then_inc(made, 1)
                pool.memset(zero[:, :], 0.0).then_inc(made, 1)
                pool.memset(zerob[:, :], 0.0).then_inc(made, 1)
                pool.memset(earlier[:, :], 1.0).then_inc(made, 1)
                pool.iota(ramp[:, :], pattern=[[1, NHI]], base=0, channel_multiplier=0,
                          allow_small_or_imprecise_dtypes=True).then_inc(made, 1)
                pool.iota(edge[:, :], pattern=[[1, TILES]], base=0, channel_multiplier=TILES,
                          allow_small_or_imprecise_dtypes=True).then_inc(made, 1)
                pool.wait_ge(made, 7)
                pool.affine_select(out=earlier[:, :], in_=earlier[:, :], compare_op=ALU.is_gt, fill=0.0,
                                   base=0, pattern=[[1, P]], channel_multiplier=-1).then_inc(made, 1)

            @block.vector
            def _(dve):
                dve.wait_ge(loaded, 48)
                flat = keys[:, :, :]
                nc.vector.tensor_scalar(parts[:, 0], flat, P - 1, None, ALU.bitwise_and).then_inc(prepared, 1)
                nc.vector.tensor_scalar(parts[:, 1], flat, 7, None, ALU.logical_shift_right).then_inc(prepared, 1)
                nc.vector.tensor_copy(keyf[:, :, :], flat).then_inc(prepared, 1)
                dve.wait_ge(prepared, 3)
                nc.vector.tensor_copy(lof[:, :, :], parts[:, 0]).then_inc(prepared, 1)
                nc.vector.tensor_copy(hif[:, :, :], parts[:, 1]).then_inc(prepared, 1)
                dve.wait_ge(prepared, 5)
                nc.vector.scalar_tensor_tensor(entry[:, :, :], lof[:, :, :], float(NHI), hif[:, :, :], ALU.mult, ALU.add)\
                    .then_inc(prepared, 1)
                dve.wait_ge(prepared, 6)

                def onehot(l, j):
                    k, t = l // 2, 2 * j + l % 2
                    if again(j):
                        dve.wait_ge(pe_done[l], count(PE, j - 1, "rank"))
                    nc.vector.tensor_scalar(onlo[l][:, :], ramp[:, 0:P], column(lof[:, k], t), None, ALU.is_equal)\
                        .then_inc(dve_done[l], 1)
                    nc.vector.tensor_scalar(onhi[l][:, :], ramp[:, :], column(hif[:, k], t), None, ALU.is_equal)\
                        .then_inc(dve_done[l], 1)

                def before(l, j):
                    dve.wait_ge(pe_done[l], count(PE, j, "same"))
                    nc.vector.tensor_tensor(lesser[l][:, :], work[l][:, 0:P], earlier[:, :], ALU.mult).then_inc(dve_done[l], 1)

                def keep(l, j):
                    k, t = l // 2, 2 * j + l % 2
                    dve.wait_ge(pe_done[l], count(PE, j, "rank"))
                    if again(j):
                        dve.wait_ge(dve_done[l], count(DV, j - 1, "kept"))
                    nc.vector.tensor_tensor_reduce(product[l][:, :], work[l][:, 0:NHI], onhi[l][:, :], 1.0, 0.0,
                                                   ALU.mult, ALU.add, found[l][:, :]).then_inc(dve_done[l], 1)
                    dve.wait_ge(dve_done[l], count(DV, j, "rank"))
                    nc.vector.tensor_copy(column(rank[:, k], t), found[l][:, :]).then_inc(dve_done[l], 1)

                rounds(dve, STAGES, {"one-hot": onehot, "before": before, "keep": keep}, n_rounds)
                dve.wait_ge(sums_done, 1)
                for k in range(2):
                    nc.vector.tensor_tensor_scan(running[:, k, :], counts[:, k, :], zero[:, :], 0.0, ALU.add, ALU.add)\
                        .then_inc(table_step, 1)
                dve.wait_ge(table_step, 2)
                nc.vector.tensor_copy(total[:, :], running[:, :, NHI - 1]).then_inc(table_step, 1)
                dve.wait_ge(sums_done, 2)
                nc.vector.tensor_copy(offset[:, :], work[0][:, 0:2]).then_inc(table_step, 1)
                dve.wait_ge(table_step, 4)
                for k in range(2):
                    nc.vector.scalar_tensor_tensor(start[:, k, :], running[:, k, :], offset[:, k:k + 1], counts[:, k, :],
                                                   ALU.add, ALU.subtract).then_inc(table_step, 1)
                dve.wait_ge(table_step, 6)
                nc.vector.tensor_scalar(counts[:, :, :], counts[:, :, :], 0.0, None, ALU.is_gt).then_inc(table_step, 1)
                dve.wait_ge(table_step, 7)
                nc.vector.scalar_tensor_tensor(running[:, :, :], start[:, :, :], -float(SLOTS), counts[:, :, :], ALU.add, ALU.mult)\
                    .then_inc(table_step, 1)
                dve.wait_ge(table_step, 8)
                nc.vector.tensor_scalar(starts[:, :, :].rearrange("p h k -> p k h"), running[:, :, :], float(SLOTS), None,
                                        ALU.add).then_inc(table_step, 1)

            @block.scalar
            def _(act):
                def turned(l, j):
                    act.wait_ge(pe_done[l], count(PE, j, "turned"))
                    nc.scalar.activation(onloT[l][:, :], work[l][:, 0:P // 2].bitcast(BF16), ACT.Copy).then_inc(act_done[l], 1)
                    nc.scalar.activation(onloTf[l][:, :], work[l][:, 0:P // 2].bitcast(BF16), ACT.Copy).then_inc(act_done[l], 1)

                def snapshot(l, j):
                    k, t = l // 2, 2 * j + l % 2
                    act.wait_ge(added[k], t + 1)
                    if again(j):
                        act.wait_ge(pe_done[l], count(PE, j - 1, "rank"))
                    nc.scalar.activation(history[l][:, :], hist[k][:, 0:NHI], ACT.Copy).then_inc(act_done[l], 1)

                rounds(act, STAGES, {"turned": turned, "snapshot": snapshot}, n_rounds)
                for k in range(2):
                    act.wait_ge(added[k], TILES + 2)
                    last = nc.scalar.activation(counts[:, k, :], hist[k][:, 0:NHI], ACT.Copy)
                last.then_inc(sums_done, 1)

            @block.tensor
            def _(pe):
                pe.wait_ge(made, 8)
                for k in range(2):
                    pe.matmul(hist[k][:, 0:NHI], zerob[:, 0:P], zerob[:, :], start=True, stop=True).then_inc(added[k], 1)

                def turn(l, j):
                    pe.wait_ge(dve_done[l], count(DV, j, "lo"))
                    if again(j):
                        pe.wait_ge(dve_done[l], count(DV, j - 1, "rank"))
                    pe.transpose(work[l][:, 0:P // 2].bitcast(BF16), onlo[l][:, :], c.identb[:, :]).then_inc(pe_done[l], 1)

                def same(l, j):
                    pe.wait_ge(act_done[l], count(AC, j, "turned f32"))
                    pe.matmul(work[l][:, 0:P], onloT[l][:, :], onloT[l][:, :], start=True, stop=True).then_inc(pe_done[l], 1)

                def add(l, j):
                    k, t = l // 2, 2 * j + l % 2
                    pe.wait_ge(dve_done[l], count(DV, j, "hi"))
                    pe.wait_ge(act_done[l], count(AC, j, "histogram"))
                    pe.matmul(hist[k][:, 0:NHI], onlo[l][:, :], onhi[l][:, :], start=False, stop=True,
                              skip_group_check=True).then_inc(added[k], 1)

                def look(l, j):
                    pe.wait_ge(dve_done[l], count(DV, j, "before"))
                    pe.matmul(work[l][:, 0:NHI], onloTf[l][:, :], history[l][:, :], start=True, stop=False)
                    pe.matmul(work[l][:, 0:NHI], lesser[l][:, :], onhi[l][:, :], start=False, stop=True).then_inc(pe_done[l], 1)

                rounds(pe, STAGES, {"turn": turn, "same": same, "add": add, "look": look}, n_rounds)
                for k in range(2):
                    pe.matmul(hist[k][:, 0:NHI], zerob[:, 0:P], zerob[:, :], start=False, stop=True,
                              skip_group_check=True).then_inc(added[k], 1)
                pe.wait_ge(table_step, 3)
                pe.matmul(work[0][:, 0:2], earlier[:, :], total[:, :], start=True, stop=True).then_inc(sums_done, 1)

        near = w.one("near", [P, TILES, 4], I32)
        ring = w.sb("ring", [P, 4], I32)
        point = w.sb("point", [P, 2], I32)
        pointed, fetched, kept = w.sems("pointed"), w.sems("fetched"), w.sems("kept")
        with nc.Block() as block:
            @block.gpsimd
            def _(pool):
                def fetch(l, j):
                    t = LANES * j + l
                    if again(j):
                        pool.wait_ge(fetched[l], 32 * j)
                    pool.tensor_copy(point[l][:, :], entry[:, :, t] if isinstance(t, int) else
                                     entry[:, :, bass.ds(t, 1)].rearrange("p a b -> p (a b)")).then_inc(pointed[l], 1)
                    pool.wait_ge(pointed[l], j + 1)
                    if again(j):
                        pool.wait_ge(kept[l], j)
                    for k in range(2):
                        gather(pool, ring[l][:, 2 * k:2 * k + 2], d["starts"], point[l][:, k:k + 1], c.bound[P * NHI - 1])\
                            .then_inc(fetched[l], 16)

                rounds(pool, ["fetch", "keep"], {"fetch": fetch}, TILES // LANES)

            @block.vector
            def _(dve):
                def keep(l, j):
                    dve.wait_ge(fetched[l], 32 * (j + 1))
                    nc.vector.tensor_copy(one_of(near, LANES * j + l), ring[l][:, :]).then_inc(kept[l], 1)

                rounds(dve, ["fetch", "keep"], {"keep": keep}, TILES // LANES)

        record = w.one("record", [P, TILES, FIELDS], I32)
        nearf = w.one("nearf", [P, 4, TILES])
        place = w.one("place", [P, 2, TILES], I32)
        placef = w.one("placef", [P, 2, TILES])
        away = w.one("away", [P, 2, TILES])
        step = w.sem("record_step")
        with nc.Block() as block:
            @block.vector
            def _(dve):
                v = nc.vector
                field = lambda f: record[:, :, f]
                far = 1 << 16
                v.memset(record[:, :, :], 0).then_inc(step, 1)
                v.tensor_copy(nearf[:, :, :], near[:, :, :].rearrange("p t f -> p f t")).then_inc(step, 1)
                dve.wait_ge(step, 2)
                v.tensor_tensor(placef[:, BY_DST, :], nearf[:, 0, :], rank[:, BY_DST, :], ALU.add).then_inc(step, 1)
                v.tensor_tensor(placef[:, BY_SRC, :], nearf[:, 3, :], rank[:, BY_SRC, :], ALU.add).then_inc(step, 1)
                v.tensor_scalar(away[:, 0, :], rank[:, BY_DST, :], 0.0, None, ALU.is_gt).then_inc(step, 1)
                v.tensor_scalar(away[:, 1, :], nearf[:, 2, :], float(SLOTS), None, ALU.is_lt).then_inc(step, 1)
                dve.wait_ge(step, 6)
                v.scalar_tensor_tensor(away[:, 1, :], rank[:, BY_SRC, :], 0.0, away[:, 1, :], ALU.is_gt, ALU.max).then_inc(step, 1)
                dve.wait_ge(step, 7)
                v.scalar_tensor_tensor(field(R_WRITE_DST), away[:, 0, :], float(far), keyf[:, BY_DST, :], ALU.mult, ALU.add).then_inc(step, 1)
                v.scalar_tensor_tensor(field(R_WRITE_SRC), away[:, 1, :], float(far), keyf[:, BY_SRC, :], ALU.mult, ALU.add).then_inc(step, 1)
                v.tensor_copy(place[:, :, :], placef[:, :, :]).then_inc(step, 1)
                v.tensor_copy(field(R_PLACE), placef[:, BY_DST, :]).then_inc(step, 1)
                v.tensor_scalar(field(R_SRC), keyf[:, BY_SRC, :], float(N_NODES - 1), None, ALU.min).then_inc(step, 1)
                v.tensor_scalar(field(R_DST), keyf[:, BY_DST, :], float(N_NODES - 1), None, ALU.min).then_inc(step, 1)
                v.tensor_scalar(field(R_EDGE), edge[:, :], float(N_EDGES - 1), None, ALU.min).then_inc(step, 1)
                v.tensor_copy(field(R_SRC_IN), near[:, :, 2]).then_inc(step, 1)
                v.tensor_copy(field(R_SRC_OUT), near[:, :, 3]).then_inc(step, 1)
                v.tensor_copy(field(R_DST_OUT), near[:, :, 1]).then_inc(step, 1)
                v.tensor_copy(record[:, :, R_WEIGHT].bitcast(F32), weight[:, :]).then_inc(step, 1)
                v.tensor_copy(record[:, :, R_SRC_KEY].bitcast(F32), keyf[:, BY_SRC, :]).then_inc(step, 1)
                v.tensor_copy(record[:, :, R_DST_KEY].bitcast(F32), keyf[:, BY_DST, :]).then_inc(step, 1)

        sent = w.sb("sent", [P, FIELDS], I32)
        spot = w.sb("spot", [P, 2], I32)
        copied, written = w.sems("copied"), w.sems("written")
        with nc.Block() as block:
            @block.gpsimd
            def _(pool):
                def send(l, j):
                    t = LANES * j + l
                    if again(j):
                        pool.wait_ge(written[l], 32 * j)
                    pool.tensor_copy(sent[l][:, :], one_of(record, t)).then_inc(copied[l], 1)
                    pool.tensor_copy(spot[l][:, :], place[:, :, t] if isinstance(t, int) else
                                     place[:, :, bass.ds(t, 1)].rearrange("p a b -> p (a b)")).then_inc(copied[l], 1)
                    pool.wait_ge(copied[l], 2 * (j + 1))
                    for k, name in ((BY_DST, "by_dst"), (BY_SRC, "by_src")):
                        scatter(pool, d[name], spot[l][:, k:k + 1], sent[l][:, :], c.bound[SLOTS - 1]).then_inc(written[l], 16)

                rounds(pool, ["send"], {"send": send}, TILES // LANES)
                for l in range(LANES):
                    pool.wait_ge(written[l], 32 * (TILES // LANES))


def allocate_edges(nc, ctx, c):
    def sb(name, shape, dt=F32):
        return ctx.enter_context(nc.sbuf_tensor(name, shape, dt))

    c.rec = [sb("rec_by_dst", [P, TILES, FIELDS], I32), sb("rec_by_src", [P, TILES, FIELDS], I32)]
    c.key = [sb("key_by_dst", [P, TILES]), sb("key_by_src", [P, TILES])]
    c.edge_of = [[sb(f"{e}_key_{k}", [TILES, 1]) for e in ("first", "last")] for k in range(2)]
    c.other = [sb("tile_after", [TILES, TILES]), sb("tile_before", [TILES, TILES])]
    c.inv = [[sb(f"inv_{n}_{k}", [P, TILES]) for n in ("count", "weight")] for k in range(2)]
    c.state = sb("state", [P, TILES, 2, D])


def phase_keys(nc, c, d):
    with ExitStack() as ctx:
        w = Work(nc, ctx, "keys")
        turned = w.sb("turned", [TILES, P])
        banks = w.banks("bank")
        zeros = w.one("zeros", [P, D])
        loaded, taken, turns, copied, stored, edges, made = (w.sem(s) for s in (
            "loaded", "taken", "turns", "copied", "stored", "edges", "made"))
        with nc.Block() as block:
            @block.sync
            def _(sp):
                for k, name in ((BY_DST, "by_dst"), (BY_SRC, "by_src")):
                    sp.dma_start(c.rec[k][:, :, :], d[name].rearrange("(t p) f -> p t f", p=P)).then_inc(loaded, 16)
                sp.wait_ge(taken, 2)
                for k in range(2):
                    for e, at in ((0, 0), (1, P - 1)):
                        sp.dma_start(c.edge_of[k][e][:, :], c.key[k][at:at + 1, :]).then_inc(edges, 16)
                sp.wait_ge(copied, 2)
                for k in range(2):
                    sp.dma_start(d["key_rows"][k].rearrange("(t p) -> t p", p=P), turned[k][:, :]).then_inc(stored, 16)
                sp.wait_ge(made, 5)
                for name in ("into", "from"):
                    sp.dma_start(d[name][SLOTS:SLOTS + P], zeros[:, :]).then_inc(stored, 16)
                sp.wait_ge(edges, 64)
                sp.wait_ge(stored, 64)

            @block.gpsimd
            def _(pool):
                pool.memset(zeros[:, :], 0.0).then_inc(made, 1)
                for m in c.other:
                    pool.memset(m[:, :], 1.0).then_inc(made, 1)
                pool.wait_ge(made, 3)
                for m, s in ((c.other[0], 1), (c.other[1], -1)):
                    pool.affine_select(out=m[:, :], in_=m[:, :], compare_op=ALU.is_gt, fill=0.0, base=0,
                                       pattern=[[-s, TILES]], channel_multiplier=s).then_inc(made, 1)

            @block.vector
            def _(dve):
                dve.wait_ge(loaded, 32)
                for k, f in ((BY_DST, R_DST_KEY), (BY_SRC, R_SRC_KEY)):
                    nc.vector.tensor_copy(c.key[k][:, :], c.rec[k][:, :, f].bitcast(F32)).then_inc(taken, 1)

            @block.tensor
            def _(pe):
                pe.wait_ge(taken, 2)
                for k in range(2):
                    pe.transpose(banks[k][0:TILES, 0:P], c.key[k][:, :], c.ident[:, :]).then_inc(turns, 1)

            @block.scalar
            def _(act):
                for k in range(2):
                    act.wait_ge(turns, k + 1)
                    nc.scalar.activation(turned[k][:, :], banks[k][0:TILES, 0:P], ACT.Copy).then_inc(copied, 1)


def phase_sum(nc, c, d, tag, order, source, width, inv, target):
    gathered = source is not None and source[1] is not None
    with ExitStack() as ctx:
        w = Work(nc, ctx, tag)
        sums = w.one("sums", [P, TILES, width])
        ends = [w.one(f"ends{e}", [TILES, width]) for e in range(2)]
        msg = w.sb("msg", [P, width])
        keys = w.sb("keys", [P, P])
        equal = w.sb("equal", [P, P])
        index = w.sb("index", [P, 1], I32)
        bank = w.banks("bank")
        ends_moved = w.sem("ends_moved")
        AT = lambda l, j: LANES * j + l
        key_row = d["key_rows"][order]

        def row_of(t, parts):
            r = key_row[t * P:(t + 1) * P] if isinstance(t, int) else key_row[bass.ds(t * P, P)]
            return r.partition_broadcast(parts)

        n_rounds = TILES // LANES
        loaded, got, pointed = w.sems("loaded"), w.sems("got"), w.sems("pointed")
        compared, multiplied, kept = w.sems("compared"), w.sems("multiplied"), w.sems("kept")
        STAGES = ["load", "compare", "multiply", "keep"]
        per = 1 if gathered or source is None else 2
        with nc.Block() as block:
            @block.sync
            def _(sp):
                def load(l, j):
                    if again(j):
                        sp.wait_ge(multiplied[l], j)
                    sp.dma_start(keys[l][:, :], row_of(AT(l, j), P)).then_inc(loaded[l], 16)
                    if per == 2:
                        sp.dma_start(msg[l][:, :], tile_rows(source[0], AT(l, j))).then_inc(loaded[l], 16)

                rounds(sp, STAGES, {"load": load}, n_rounds)

            if gathered:
                @block.gpsimd
                def _(pool):
                    def fetch(l, j):
                        if again(j):
                            pool.wait_ge(multiplied[l], j)
                        pool.tensor_copy(index[l][:, :], one_of(c.rec[order], AT(l, j))[:, source[1]:source[1] + 1])\
                            .then_inc(pointed[l], 1)
                        pool.wait_ge(pointed[l], j + 1)
                        gather(pool, msg[l][:, :], source[0], index[l][:, :], c.bound[SLOTS - 1]).then_inc(got[l], 16)

                    rounds(pool, STAGES, {"load": fetch}, n_rounds)

            @block.vector
            def _(dve):
                def compare(l, j):
                    dve.wait_ge(loaded[l], 16 * per * (j + 1))
                    if again(j):
                        dve.wait_ge(multiplied[l], j)
                    nc.vector.tensor_scalar(equal[l][:, :], keys[l][:, :], column(c.key[order], AT(l, j)), None,
                                            ALU.is_equal).then_inc(compared[l], 1)
                    if source is None:
                        nc.vector.memset(msg[l][:, 0:1], 1.0).then_inc(compared[l], 1)
                        nc.vector.tensor_copy(msg[l][:, 1:2], one_of(c.rec[order], AT(l, j))[:, R_WEIGHT:R_WEIGHT + 1].bitcast(F32))\
                            .then_inc(compared[l], 1)

                rounds(dve, STAGES, {"compare": compare}, n_rounds)

            @block.tensor
            def _(pe):
                def multiply(l, j):
                    pe.wait_ge(compared[l], (3 if source is None else 1) * (j + 1))
                    if gathered:
                        pe.wait_ge(got[l], 16 * (j + 1))
                    if again(j):
                        pe.wait_ge(kept[l], j)
                    pe.matmul(bank[l][:, 0:width], equal[l][:, :], msg[l][:, :], start=True, stop=True)\
                        .then_inc(multiplied[l], 1)

                rounds(pe, STAGES, {"multiply": multiply}, n_rounds)

            @block.scalar
            def _(act):
                def keep(l, j):
                    act.wait_ge(multiplied[l], j + 1)
                    scale = 1.0 if inv is None else column(inv, AT(l, j))
                    nc.scalar.activation(one_of(sums, AT(l, j)), bank[l][:, 0:width], ACT.Copy, scale=scale).then_inc(kept[l], 1)

                rounds(act, STAGES, {"keep": keep}, n_rounds)

        with nc.Block() as block:
            @block.sync
            def _(sp):
                for e, at in ((0, 0), (1, P - 1)):
                    sp.dma_start(ends[e][:, :], sums[at:at + 1, :, :].rearrange("a t d -> a (t d)")).then_inc(ends_moved, 16)
                sp.wait_ge(ends_moved, 32)

        loaded, compared, multiplied = w.sems("loaded2"), w.sems("compared2"), w.sems("multiplied2")
        summed, stored, pointed = w.sems("summed"), w.sems("stored"), w.sems("pointed2")
        other = [equal, w.sb("equal_last", [TILES, P])]
        result = w.sb("result", [P, width])
        STAGES = ["load", "compare", "multiply", "sum", "store"]
        final = target == "out"
        with nc.Block() as block:
            @block.sync
            def _(sp):
                def load(l, j):
                    if again(j):
                        sp.wait_ge(compared[l], 2 * j)
                    sp.dma_start(keys[l][0:TILES, :], row_of(AT(l, j), TILES)).then_inc(loaded[l], 16)

                def store(l, j):
                    if target in ("into", "from"):
                        sp.wait_ge(summed[l], j + 1)
                        sp.dma_start(tile_rows(d[target], AT(l, j)), result[l][:, :]).then_inc(stored[l], 16)

                rounds(sp, STAGES, {"load": load, "store": store}, n_rounds)
                if target in ("into", "from"):
                    for l in range(LANES):
                        sp.wait_ge(stored[l], 16 * n_rounds)

            @block.vector
            def _(dve):
                def compare(l, j):
                    dve.wait_ge(loaded[l], 16 * (j + 1))
                    if again(j):
                        dve.wait_ge(multiplied[l], j)
                    for e in range(2):
                        mask = column(c.other[e], AT(l, j)).to_broadcast([TILES, P])
                        nc.vector.scalar_tensor_tensor(other[e][l][0:TILES, :], keys[l][0:TILES, :], c.edge_of[order][e][:, :],
                                                       mask, ALU.is_equal, ALU.mult).then_inc(compared[l], 1)

                def add(l, j):
                    per_round = 2 if final else 1
                    dve.wait_ge(multiplied[l], j + 1)
                    if again(j) and isinstance(target, str):
                        dve.wait_ge(stored[l], 16 * j)
                    out = result[l][:, :] if isinstance(target, str) else one_of(target, AT(l, j))
                    nc.vector.tensor_tensor(out, bank[l][:, 0:width], one_of(sums, AT(l, j)), ALU.add).then_inc(summed[l], 1)
                    if final:
                        dve.wait_ge(summed[l], 2 * j + 1)
                        own = c.state[:, AT(l, j), 1, :] if isinstance(j, int) else \
                            c.state[:, bass.ds(AT(l, j), 1), 1, :].rearrange("p a d -> p (a d)")
                        nc.vector.tensor_tensor(result[l][:, :], result[l][:, :], own, ALU.add).then_inc(summed[l], 1)

                rounds(dve, STAGES, {"compare": compare, "sum": add}, n_rounds)

            @block.tensor
            def _(pe):
                def multiply(l, j):
                    pe.wait_ge(compared[l], 2 * (j + 1))
                    if again(j):
                        pe.wait_ge(summed[l], (2 * j - 1) if final else j)
                    for e in range(2):
                        last = pe.matmul(bank[l][:, 0:width], other[e][l][0:TILES, :], ends[e][:, :], start=(e == 0), stop=(e == 1))
                    last.then_inc(multiplied[l], 1)

                rounds(pe, STAGES, {"multiply": multiply}, n_rounds)

            if final:
                @block.gpsimd
                def _(pool):
                    def store(l, j):
                        if again(j):
                            pool.wait_ge(stored[l], 16 * j)
                        pool.tensor_copy(index[l][:, :], one_of(c.rec[order], AT(l, j))[:, R_WRITE_DST:R_WRITE_DST + 1])\
                            .then_inc(pointed[l], 1)
                        pool.wait_ge(pointed[l], j + 1)
                        pool.wait_ge(summed[l], 2 * (j + 1))
                        scatter(pool, d["out"], index[l][:, :], result[l][:, :], c.bound[N_NODES - 1]).then_inc(stored[l], 16)

                    rounds(pool, STAGES, {"store": store}, n_rounds)
                    for l in range(LANES):
                        pool.wait_ge(stored[l], 16 * n_rounds)


def phase_degrees(nc, c, d):
    with ExitStack() as outer:
        totals = [outer.enter_context(nc.sbuf_tensor(f"totals{k}", [P, TILES, 2], F32)) for k in range(2)]
        for k in range(2):
            phase_sum(nc, c, d, f"deg{k}", k, None, 2, None, totals[k])
        with ExitStack() as ctx:
            w = Work(nc, ctx, "degrees")
            present, safe, counted = (w.one(s, [P, TILES]) for s in ("present", "safe", "counted"))
            step = w.sem("step")
            with nc.Block() as block:
                @block.vector
                def _(dve):
                    v = nc.vector
                    for k in range(2):
                        base = 7 * k
                        if k:
                            dve.wait_ge(step, base)
                        v.tensor_scalar(counted[:, :], totals[k][:, :, 0], 1.0, None, ALU.max).then_inc(step, 1)
                        v.tensor_scalar(present[:, :], totals[k][:, :, 1], 0.0, None, ALU.is_gt).then_inc(step, 1)
                        dve.wait_ge(step, base + 2)
                        v.reciprocal(c.inv[k][0][:, :], counted[:, :]).then_inc(step, 1)
                        v.scalar_tensor_tensor(safe[:, :], totals[k][:, :, 1], 1.0, present[:, :], ALU.subtract, ALU.mult).then_inc(step, 1)
                        dve.wait_ge(step, base + 4)
                        v.tensor_scalar(safe[:, :], safe[:, :], 1.0, None, ALU.add).then_inc(step, 1)
                        dve.wait_ge(step, base + 5)
                        v.reciprocal(safe[:, :], safe[:, :]).then_inc(step, 1)
                        dve.wait_ge(step, base + 6)
                        v.tensor_tensor(c.inv[k][1][:, :], safe[:, :], present[:, :], ALU.mult).then_inc(step, 1)


class Norm:

    def __init__(self, w, p, u):
        self.nc, self.p, self.u = w.nc, p, u
        self.stats = w.sb("stats", [p, u, 6])
        self.mv = w.sb("mv", [p, u, 2])
        self.var = w.sb("var", [p, u])
        self.scaled = w.sb("scaled", [p, u])
        self.rstd = w.sb("rstd", [p, u])
        self.shift = w.sb("shift", [p, u])
        self.pause = w.one("pause", [p, 1])

    def moments(self, dve, l, src, done, at):
        v = self.nc.vector
        for i in range(self.u):
            last = v.bn_stats(self.stats[l][:, i, :], src[l][:, i, :])
        last.then_inc(done[l], 1)
        dve.wait_ge(done[l], at("stats"))
        v.memset(self.pause[:, :], 0.0)
        for i in range(self.u):
            last = v.bn_aggr(self.mv[l][:, i, :], self.stats[l][:, i, :])
        last.then_inc(done[l], 1)

    def factors(self, pool, c, l, done, at):
        p, u = self.p, self.u
        pool.tensor_tensor(self.var[l][:, :], self.mv[l][:, :, 1], c.eps[0:p, 0:u], ALU.add).then_inc(done[l], 1)
        pool.wait_ge(done[l], at("var"))
        pool.tensor_tensor(self.rstd[l][:, :], self.var[l][:, :], c.power[0:p, 0:u], ALU.pow).then_inc(done[l], 1)
        pool.wait_ge(done[l], at("rstd"))
        pool.tensor_tensor(self.scaled[l][:, :], self.mv[l][:, :, 0], self.rstd[l][:, :], ALU.mult).then_inc(done[l], 1)
        pool.wait_ge(done[l], at("m"))
        pool.tensor_tensor(self.shift[l][:, :], self.scaled[l][:, :], c.minus[0:p, 0:u], ALU.mult).then_inc(done[l], 1)

    def apply(self, out, src, l):
        for i in range(self.u):
            last = self.nc.scalar.activation(out[l][:, i, :], src[l][:, i, :], ACT.Relu, bias=self.shift[l][:, i:i + 1],
                                             scale=self.rstd[l][:, i:i + 1])
        return last


def pair(t, j):
    return t[:, j] if isinstance(j, int) else t[:, bass.ds(j, 1)].rearrange("p a u d -> p (a u) d")


def fields(rec, j, lo, hi):
    return rec[:, j, lo:hi] if isinstance(j, int) else rec[:, bass.ds(j, 1), lo:hi].rearrange("p a f -> p (a f)")


N2 = TILES // LANES
AT = lambda l, j: LANES * j + l
SELF = lambda bank: bank[:, 0:512].rearrange("p (u c) -> p u c", u=2)[:, :, 0:D]
SENT = slice(D, 2 * D)


def turn_pair(pe, c, out, src, l):
    for i in range(2):
        last = pe.transpose(out[:, i * P:(i + 1) * P], src[l][:, i, :], c.ident[:, :])
    return last


def layer_products(pe, bank, hT, both):
    pe.matmul(bank[:, 0:2 * D], hT[:, 0:P], both, start=True, stop=True)
    return pe.matmul(bank[:, 2 * D:3 * D], hT[:, P:2 * P], both[:, 0:D], start=True, stop=True)


def phase_enter(nc, c, d, a):
    DV = ["stats", "mean", "hT", "own"]
    PO = ["index", "var", "rstd", "m", "shift"]
    AC = ["h", "message"]
    PE = ["turn", "products"]
    STAGES = ["load", "norm", "factors", "h", "turn", "hT", "products", "own", "store"]
    with ExitStack() as ctx:
        w = Work(nc, ctx, "enter")
        index, x, h, hT, message = w.sb("index", [P, 2], I32), w.sb("x", [P, 2, D]), w.sb("h", [P, 2, D]), w.sb("hT", [P, 2 * P]), w.sb("message", [P, D])
        norm = Norm(w, P, 2)
        left, right = w.banks("left"), w.banks("right")
        loaded, stored, kept = w.sems("loaded"), w.sems("stored"), w.sems("kept")
        pe_done, act_done, dve_done, pool_done = w.sems("pe_done"), w.sems("act_done"), w.sems("dve_done"), w.sems("pool_done")
        with nc.Block() as block:
            @block.gpsimd
            def _(pool):
                def load(l, j):
                    if again(j):
                        pool.wait_ge(loaded[l], 32 * j)
                        pool.wait_ge(act_done[l], count(AC, j - 1, "h"))
                        pool.wait_ge(kept[l], 16 * j)
                    pool.tensor_copy(index[l][:, :], fields(c.rec[BY_DST], AT(l, j), R_SRC, R_DST + 1)).then_inc(pool_done[l], 1)
                    pool.wait_ge(pool_done[l], count(PO, j, "index"))
                    for i in range(2):
                        gather(pool, x[l][:, i, :], a["x"], index[l][:, i:i + 1], c.bound[N_NODES - 1]).then_inc(loaded[l], 16)

                def factors(l, j):
                    pool.wait_ge(dve_done[l], count(DV, j, "mean"))
                    norm.factors(pool, c, l, pool_done, lambda s: count(PO, j, s))

                rounds(pool, STAGES, {"load": load, "factors": factors}, N2)

            @block.sync
            def _(sp):
                def keep(l, j):
                    sp.wait_ge(loaded[l], 32 * (j + 1))
                    sp.dma_start(tile_rows(d["kept"], AT(l, j)), x[l][:, :, :]).then_inc(kept[l], 16)

                def store(l, j):
                    sp.wait_ge(act_done[l], count(AC, j, "message"))
                    sp.dma_start(tile_rows(d["message"], AT(l, j)), message[l][:, :]).then_inc(stored[l], 16)

                rounds(sp, STAGES, {"norm": keep, "store": store}, N2)
                for l in range(LANES):
                    sp.wait_ge(stored[l], 16 * N2)
                    sp.wait_ge(kept[l], 16 * N2)

            @block.vector
            def _(dve):
                def moments(l, j):
                    dve.wait_ge(loaded[l], 32 * (j + 1))
                    norm.moments(dve, l, x, dve_done, lambda s: count(DV, j, s))

                def copy(l, j):
                    dve.wait_ge(pe_done[l], count(PE, j, "turn"))
                    nc.vector.tensor_copy(hT[l][:, :], left[l][:, 0:2 * P]).then_inc(dve_done[l], 1)

                def own(l, j):
                    dve.wait_ge(pe_done[l], count(PE, j, "products"))
                    dve.wait_ge(act_done[l], count(AC, j, "message"))
                    nc.vector.tensor_tensor(pair(c.state, AT(l, j)), SELF(right[l]), bc(c.bias[:, B_L0, :], 2), ALU.add)\
                        .then_inc(dve_done[l], 1)

                rounds(dve, STAGES, {"norm": moments, "hT": copy, "own": own}, N2)

            @block.scalar
            def _(act):
                def apply(l, j):
                    act.wait_ge(pool_done[l], count(PO, j, "shift"))
                    if again(j):
                        act.wait_ge(pe_done[l], count(PE, j - 1, "turn"))
                    norm.apply(h, x, l).then_inc(act_done[l], 1)

                def send(l, j):
                    act.wait_ge(pe_done[l], count(PE, j, "products"))
                    if again(j):
                        act.wait_ge(stored[l], 16 * j)
                    nc.scalar.activation(message[l][:, :], right[l][:, SENT], ACT.Copy).then_inc(act_done[l], 1)

                rounds(act, STAGES, {"h": apply, "own": send}, N2)

            @block.tensor
            def _(pe):
                def turn(l, j):
                    pe.wait_ge(act_done[l], count(AC, j, "h"))
                    if again(j):
                        pe.wait_ge(dve_done[l], count(DV, j - 1, "hT"))
                    turn_pair(pe, c, left[l], h, l).then_inc(pe_done[l], 1)

                def products(l, j):
                    pe.wait_ge(dve_done[l], count(DV, j, "hT"))
                    if again(j):
                        pe.wait_ge(dve_done[l], count(DV, j - 1, "own"))
                    layer_products(pe, right[l], hT[l], c.wrT[:, 0, :]).then_inc(pe_done[l], 1)

                rounds(pe, STAGES, {"turn": turn, "products": products}, N2)


def phase_layer(nc, c, d, layer):
    DV = ["sum", "own"]
    AC = ["hT", "message"]
    PE = ["turn", "products"]
    STAGES = ["load", "sum", "turn", "hT", "products", "own", "store"]
    with ExitStack() as ctx:
        w = Work(nc, ctx, f"layer{layer}")
        index, near, s, hT, message = w.sb("index", [P, 1], I32), w.sb("near", [P, 2, D]), w.sb("s", [P, 2, D]), w.sb("hT", [P, 2 * P]), w.sb("message", [P, D])
        left, right = w.banks("left"), w.banks("right")
        loaded, gathered, stored, pointed = w.sems("loaded"), w.sems("gathered"), w.sems("stored"), w.sems("pointed")
        pe_done, act_done, dve_done = w.sems("pe_done"), w.sems("act_done"), w.sems("dve_done")
        with nc.Block() as block:
            @block.gpsimd
            def _(pool):
                def load(l, j):
                    if again(j):
                        pool.wait_ge(gathered[l], 16 * j)
                        pool.wait_ge(dve_done[l], count(DV, j - 1, "sum"))
                    pool.tensor_copy(index[l][:, :], fields(c.rec[BY_DST], AT(l, j), R_SRC_IN, R_SRC_IN + 1)).then_inc(pointed[l], 1)
                    pool.wait_ge(pointed[l], j + 1)
                    gather(pool, near[l][:, 0, :], d["into"], index[l][:, :], c.bound[SLOTS]).then_inc(gathered[l], 16)

                rounds(pool, STAGES, {"load": load}, N2)

            @block.sync
            def _(sp):
                def load(l, j):
                    if again(j):
                        sp.wait_ge(dve_done[l], count(DV, j - 1, "sum"))
                    sp.dma_start(near[l][:, 1, :], tile_rows(d["into"], AT(l, j))).then_inc(loaded[l], 16)

                def store(l, j):
                    sp.wait_ge(act_done[l], count(AC, j, "message"))
                    sp.dma_start(tile_rows(d["message"], AT(l, j)), message[l][:, :]).then_inc(stored[l], 16)

                rounds(sp, STAGES, {"load": load, "store": store}, N2)
                for l in range(LANES):
                    sp.wait_ge(stored[l], 16 * N2)

            @block.vector
            def _(dve):
                def add(l, j):
                    dve.wait_ge(loaded[l], 16 * (j + 1))
                    dve.wait_ge(gathered[l], 16 * (j + 1))
                    if again(j):
                        dve.wait_ge(pe_done[l], count(PE, j - 1, "turn"))
                    nc.vector.tensor_tensor(s[l][:, :, :], near[l][:, :, :], pair(c.state, AT(l, j)), ALU.add).then_inc(dve_done[l], 1)

                def own(l, j):
                    dve.wait_ge(pe_done[l], count(PE, j, "products"))
                    dve.wait_ge(act_done[l], count(AC, j, "message"))
                    nc.vector.tensor_tensor(pair(c.state, AT(l, j)), SELF(right[l]), bc(c.bias[:, B_L0 + layer, :], 2), ALU.add)\
                        .then_inc(dve_done[l], 1)

                rounds(dve, STAGES, {"sum": add, "own": own}, N2)

            @block.scalar
            def _(act):
                def relu(l, j):
                    act.wait_ge(pe_done[l], count(PE, j, "turn"))
                    if again(j):
                        act.wait_ge(pe_done[l], count(PE, j - 1, "products"))
                    nc.scalar.activation(hT[l][:, :], left[l][:, 0:2 * P], ACT.Relu).then_inc(act_done[l], 1)

                def send(l, j):
                    act.wait_ge(pe_done[l], count(PE, j, "products"))
                    if again(j):
                        act.wait_ge(stored[l], 16 * j)
                    nc.scalar.activation(message[l][:, :], right[l][:, SENT], ACT.Copy).then_inc(act_done[l], 1)

                rounds(act, STAGES, {"hT": relu, "own": send}, N2)

            @block.tensor
            def _(pe):
                def turn(l, j):
                    pe.wait_ge(dve_done[l], count(DV, j, "sum"))
                    if again(j):
                        pe.wait_ge(act_done[l], count(AC, j - 1, "hT"))
                    turn_pair(pe, c, left[l], s, l).then_inc(pe_done[l], 1)

                def products(l, j):
                    pe.wait_ge(act_done[l], count(AC, j, "hT"))
                    if again(j):
                        pe.wait_ge(dve_done[l], count(DV, j - 1, "own"))
                    layer_products(pe, right[l], hT[l], c.wrT[:, layer, :]).then_inc(pe_done[l], 1)

                rounds(pe, STAGES, {"turn": turn, "products": products}, N2)


def phase_join(nc, c, d):
    DV = ["sum", "x", "stats", "mean"]
    PO = ["index", "var", "rstd", "m", "shift", "kept"]
    AC = ["h", "message"]
    STAGES = ["load", "sum", "factors", "h", "message", "store"]
    with ExitStack() as ctx:
        w = Work(nc, ctx, "join")
        index, near, s, x0, x = w.sb("index", [P, 1], I32), w.sb("near", [P, 2, D]), w.sb("s", [P, 2, D]), w.sb("x0", [P, 2, D]), w.sb("x", [P, 2, D])
        h, message = w.sb("h", [P, 2, D]), w.sb("message", [P, 2, D])
        norm = Norm(w, P, 2)
        loaded, gathered, stored = w.sems("loaded"), w.sems("gathered"), w.sems("stored")
        act_done, dve_done, pool_done = w.sems("act_done"), w.sems("dve_done"), w.sems("pool_done")
        with nc.Block() as block:
            @block.gpsimd
            def _(pool):
                def load(l, j):
                    if again(j):
                        pool.wait_ge(gathered[l], 16 * j)
                        pool.wait_ge(dve_done[l], count(DV, j - 1, "sum"))
                    pool.tensor_copy(index[l][:, :], fields(c.rec[BY_DST], AT(l, j), R_SRC_IN, R_SRC_IN + 1)).then_inc(pool_done[l], 1)
                    pool.wait_ge(pool_done[l], count(PO, j, "index"))
                    gather(pool, near[l][:, 0, :], d["into"], index[l][:, :], c.bound[SLOTS]).then_inc(gathered[l], 16)

                def factors(l, j):
                    pool.wait_ge(dve_done[l], count(DV, j, "mean"))
                    norm.factors(pool, c, l, pool_done, lambda s: count(PO, j, s))
                    pool.tensor_copy(pair(c.state, AT(l, j)), x[l][:, :, :]).then_inc(pool_done[l], 1)

                rounds(pool, STAGES, {"load": load, "factors": factors}, N2)

            @block.sync
            def _(sp):
                def load(l, j):
                    if again(j):
                        sp.wait_ge(dve_done[l], count(DV, j - 1, "x"))
                    sp.dma_start(near[l][:, 1, :], tile_rows(d["into"], AT(l, j))).then_inc(loaded[l], 16)
                    sp.dma_start(x0[l][:, :, :], tile_rows(d["kept"], AT(l, j))).then_inc(loaded[l], 16)

                def store(l, j):
                    sp.wait_ge(act_done[l], count(AC, j, "message"))
                    sp.dma_start(tile_rows(d["message"], AT(l, j)), message[l][:, 0, :]).then_inc(stored[l], 16)
                    sp.dma_start(tile_rows(d["reverse"], AT(l, j)), message[l][:, 1, :]).then_inc(stored[l], 16)

                rounds(sp, STAGES, {"load": load, "store": store}, N2)
                for l in range(LANES):
                    sp.wait_ge(stored[l], 32 * N2)

            @block.vector
            def _(dve):
                def add(l, j):
                    dve.wait_ge(loaded[l], 32 * (j + 1))
                    dve.wait_ge(gathered[l], 16 * (j + 1))
                    nc.vector.tensor_tensor(s[l][:, :, :], near[l][:, :, :], pair(c.state, AT(l, j)), ALU.add).then_inc(dve_done[l], 1)
                    dve.wait_ge(dve_done[l], count(DV, j, "sum"))
                    if again(j):
                        dve.wait_ge(act_done[l], count(AC, j - 1, "h"))
                        dve.wait_ge(pool_done[l], count(PO, j - 1, "kept"))
                    nc.vector.tensor_tensor(x[l][:, :, :], s[l][:, :, :], x0[l][:, :, :], ALU.add).then_inc(dve_done[l], 1)
                    dve.wait_ge(dve_done[l], count(DV, j, "x"))
                    norm.moments(dve, l, x, dve_done, lambda s: count(DV, j, s))

                rounds(dve, STAGES, {"sum": add}, N2)

            @block.scalar
            def _(act):
                def apply(l, j):
                    act.wait_ge(pool_done[l], count(PO, j, "shift"))
                    norm.apply(h, x, l).then_inc(act_done[l], 1)

                def send(l, j):
                    act.wait_ge(act_done[l], count(AC, j, "h"))
                    if again(j):
                        act.wait_ge(stored[l], 32 * j)
                    nc.scalar.activation(message[l][:, :, :], h[l][:, :, :], ACT.Copy,
                                         scale=fields(c.rec[BY_DST], AT(l, j), R_WEIGHT, R_WEIGHT + 1).bitcast(F32)).then_inc(act_done[l], 1)

                rounds(act, STAGES, {"h": apply, "message": send}, N2)


def phase_edges(nc, c, d, a):
    DV = ["filter", "product"]
    AC = ["eT", "tanh"]
    PE = ["turn", "products"]
    STAGES = ["load", "turn", "eT", "products", "tanh", "filter", "store"]
    with ExitStack() as ctx:
        w = Work(nc, ctx, "edges")
        index, e, eT, g, f = w.sb("index", [P, 1], I32), w.sb("e", [P, D]), w.sb("eT", [P, P]), w.sb("g", [P, D]), w.sb("f", [P, D])
        left, right = w.banks("left"), w.banks("right")
        gathered, stored, pointed = w.sems("gathered"), w.sems("stored"), w.sems("pointed")
        pe_done, act_done, dve_done = w.sems("pe_done"), w.sems("act_done"), w.sems("dve_done")
        with nc.Block() as block:
            @block.gpsimd
            def _(pool):
                def load(l, j):
                    if again(j):
                        pool.wait_ge(gathered[l], 16 * j)
                        pool.wait_ge(pe_done[l], count(PE, j - 1, "turn"))
                    pool.tensor_copy(index[l][:, :], fields(c.rec[BY_DST], AT(l, j), R_EDGE, R_EDGE + 1)).then_inc(pointed[l], 1)
                    pool.wait_ge(pointed[l], j + 1)
                    gather(pool, e[l][:, :], a["edge_attr_128"], index[l][:, :], c.bound[N_EDGES - 1]).then_inc(gathered[l], 16)

                rounds(pool, STAGES, {"load": load}, N2)

            @block.sync
            def _(sp):
                def store(l, j):
                    sp.wait_ge(dve_done[l], count(DV, j, "product"))
                    sp.dma_start(tile_rows(d["filter"], AT(l, j)), f[l][:, :]).then_inc(stored[l], 16)

                rounds(sp, STAGES, {"store": store}, N2)
                for l in range(LANES):
                    sp.wait_ge(stored[l], 16 * N2)

            @block.vector
            def _(dve):
                def go(l, j):
                    dve.wait_ge(act_done[l], count(AC, j, "tanh"))
                    if again(j):
                        dve.wait_ge(stored[l], 16 * j)
                    nc.vector.scalar_tensor_tensor(f[l][:, :], g[l][:, :], 1.0, right[l][:, D:2 * D], ALU.add, ALU.mult)\
                        .then_inc(dve_done[l], 1)
                    dve.wait_ge(dve_done[l], count(DV, j, "filter"))
                    nc.vector.tensor_scalar(f[l][:, :], f[l][:, :], 0.5, None, ALU.mult).then_inc(dve_done[l], 1)

                rounds(dve, STAGES, {"filter": go}, N2)

            @block.scalar
            def _(act):
                def copy(l, j):
                    act.wait_ge(pe_done[l], count(PE, j, "turn"))
                    nc.scalar.activation(eT[l][:, :], left[l][:, 0:P], ACT.Copy).then_inc(act_done[l], 1)

                def tanh(l, j):
                    act.wait_ge(pe_done[l], count(PE, j, "products"))
                    if again(j):
                        act.wait_ge(dve_done[l], count(DV, j - 1, "filter"))
                    nc.scalar.activation(g[l][:, :], right[l][:, 0:D], ACT.Tanh, scale=0.5).then_inc(act_done[l], 1)

                rounds(act, STAGES, {"eT": copy, "tanh": tanh}, N2)

            @block.tensor
            def _(pe):
                def turn(l, j):
                    pe.wait_ge(gathered[l], 16 * (j + 1))
                    if again(j):
                        pe.wait_ge(act_done[l], count(AC, j - 1, "eT"))
                    pe.transpose(left[l][:, 0:P], e[l][:, :], c.ident[:, :]).then_inc(pe_done[l], 1)

                def products(l, j):
                    pe.wait_ge(act_done[l], count(AC, j, "eT"))
                    if again(j):
                        pe.wait_ge(dve_done[l], count(DV, j - 1, "filter"))
                    o = right[l][:, 0:2 * D]
                    pe.matmul(o, c.ones3[:, :], c.bias3[:, B_GATE:B_FILT + 1, :].rearrange("a b d -> a (b d)"), start=True, stop=False)
                    pe.matmul(o, eT[l][:, :], c.wgf[:, :, :].rearrange("p g d -> p (g d)"), start=False, stop=True)\
                        .then_inc(pe_done[l], 1)

                rounds(pe, STAGES, {"turn": turn, "products": products}, N2)


def phase_gru(nc, c, d):
    DV = ["stats1", "mean1", "outT", "r hn src", "r hn dst", "n in src", "n in dst", "z mix", "x", "stats2", "mean2", "own", "message"]
    PO = ["index", "x1", "var1", "rstd1", "m1", "shift1", "h - n", "n + x1", "var2", "rstd2", "m2", "shift2", "kept"]
    AC = ["h", "hT", "rz src", "rz dst", "n", "h5", "h5T"]
    PE = ["turn h", "turn out", "gates", "turn h5", "node"]
    STAGES = ["load", "norm1", "factors1", "h", "turn h", "hT", "gates", "rz", "n in", "n", "mix", "norm2", "factors2", "h5",
              "turn h5", "h5T", "node", "own", "store"]
    with ExitStack() as ctx:
        w = Work(nc, ctx, "gru")
        index = w.sb("index", [P, 3], I32)
        x1, h, x2, h5 = (w.sb(n, [P, 2, D]) for n in ("x1", "h", "x2", "h5"))
        into, out = w.sb("into", [P, 2, D]), w.sb("out", [P, 2, D])
        hT, outT = w.sb("hT", [P, 4 * P]), w.sb("outT", [P, 2 * P])
        rz = w.sb("rz", [P, 2, 2 * D])
        u, n, apart, both, own = (w.sb(s, [P, 2, D]) for s in ("u", "n", "apart", "both", "own"))
        filt, message = w.sb("filt", [P, 1, D]), w.sb("message", [P, 1, D])
        norm = Norm(w, P, 2)
        left, right = w.banks("left"), w.banks("right")
        loaded, gathered, stored = w.sems("loaded"), w.sems("gathered"), w.sems("stored")
        pe_done, act_done, dve_done, pool_done = w.sems("pe_done"), w.sems("act_done"), w.sems("dve_done"), w.sems("pool_done")
        with nc.Block() as block:
            @block.gpsimd
            def _(pool):
                def load(l, j):
                    if again(j):
                        pool.wait_ge(gathered[l], 48 * j)
                        pool.wait_ge(pe_done[l], count(PE, j - 1, "turn out"))
                        pool.wait_ge(pool_done[l], count(PO, j - 1, "n + x1"))
                    pool.tensor_copy(index[l][:, :], fields(c.rec[BY_DST], AT(l, j), R_SRC_IN, R_DST_OUT + 1)).then_inc(pool_done[l], 1)
                    pool.tensor_copy(x1[l][:, :, :], pair(c.state, AT(l, j))).then_inc(pool_done[l], 1)
                    pool.wait_ge(pool_done[l], count(PO, j, "index"))
                    gather(pool, into[l][:, 0, :], d["into"], index[l][:, 0:1], c.bound[SLOTS]).then_inc(gathered[l], 16)
                    gather(pool, out[l][:, 0, :], d["from"], index[l][:, 1:2], c.bound[SLOTS]).then_inc(gathered[l], 16)
                    gather(pool, out[l][:, 1, :], d["from"], index[l][:, 2:3], c.bound[SLOTS]).then_inc(gathered[l], 16)

                def factors(k):
                    def go(l, j):
                        pool.wait_ge(dve_done[l], count(DV, j, "mean" + k))
                        norm.factors(pool, c, l, pool_done, lambda s: count(PO, j, s + k))
                        if k == "2":
                            pool.tensor_copy(pair(c.state, AT(l, j)), x2[l][:, :, :]).then_inc(pool_done[l], 1)
                    return go

                def mix(l, j):
                    pool.wait_ge(act_done[l], count(AC, j, "n"))
                    if again(j):
                        pool.wait_ge(dve_done[l], count(DV, j - 1, "x"))
                    pool.tensor_tensor(apart[l][:, :, :], h[l][:, :, :], n[l][:, :, :], ALU.subtract).then_inc(pool_done[l], 1)
                    pool.tensor_tensor(both[l][:, :, :], n[l][:, :, :], x1[l][:, :, :], ALU.add).then_inc(pool_done[l], 1)

                rounds(pool, STAGES, {"load": load, "factors1": factors("1"), "factors2": factors("2"), "mix": mix}, N2)

            @block.sync
            def _(sp):
                def load(l, j):
                    if again(j):
                        sp.wait_ge(pe_done[l], count(PE, j - 1, "turn h"))
                        sp.wait_ge(dve_done[l], count(DV, j - 1, "message"))
                    sp.dma_start(into[l][:, 1, :], tile_rows(d["into"], AT(l, j))).then_inc(loaded[l], 16)
                    sp.dma_start(filt[l][:, 0, :], tile_rows(d["filter"], AT(l, j))).then_inc(loaded[l], 16)

                def store(l, j):
                    sp.wait_ge(dve_done[l], count(DV, j, "message"))
                    sp.dma_start(tile_rows(d["kept"], AT(l, j)), own[l][:, :, :]).then_inc(stored[l], 16)
                    sp.dma_start(tile_rows(d["reverse"], AT(l, j)), message[l][:, 0, :]).then_inc(stored[l], 16)

                rounds(sp, STAGES, {"load": load, "store": store}, N2)
                for l in range(LANES):
                    sp.wait_ge(stored[l], 32 * N2)

            @block.vector
            def _(dve):
                def norm1(l, j):
                    dve.wait_ge(pool_done[l], count(PO, j, "x1"))
                    norm.moments(dve, l, x1, dve_done, lambda s: count(DV, j, s + "1"))

                def copy(l, j):
                    dve.wait_ge(pe_done[l], count(PE, j, "turn out"))
                    nc.vector.tensor_copy(outT[l][:, :], right[l][:, 0:2 * P]).then_inc(dve_done[l], 1)

                def n_in(l, j):
                    dve.wait_ge(act_done[l], count(AC, j, "rz dst"))
                    for i, bank in enumerate((left, right)):
                        nc.vector.scalar_tensor_tensor(u[l][:, i, :], rz[l][:, i, 0:D], 1.0, bank[l][:, 0:D], ALU.add, ALU.mult)\
                            .then_inc(dve_done[l], 1)
                    dve.wait_ge(dve_done[l], count(DV, j, "r hn dst"))
                    for i, bank in enumerate((left, right)):
                        nc.vector.scalar_tensor_tensor(u[l][:, i, :], u[l][:, i, :], 0.5, bank[l][:, 3 * D:4 * D], ALU.mult, ALU.add)\
                            .then_inc(dve_done[l], 1)

                def norm2(l, j):
                    dve.wait_ge(pool_done[l], count(PO, j, "n + x1"))
                    nc.vector.scalar_tensor_tensor(u[l][:, :, :], rz[l][:, :, D:2 * D], 1.0, apart[l][:, :, :], ALU.add, ALU.mult)\
                        .then_inc(dve_done[l], 1)
                    dve.wait_ge(dve_done[l], count(DV, j, "z mix"))
                    if again(j):
                        dve.wait_ge(pool_done[l], count(PO, j - 1, "kept"))
                    nc.vector.scalar_tensor_tensor(x2[l][:, :, :], u[l][:, :, :], 0.5, both[l][:, :, :], ALU.mult, ALU.add)\
                        .then_inc(dve_done[l], 1)
                    dve.wait_ge(dve_done[l], count(DV, j, "x"))
                    norm.moments(dve, l, x2, dve_done, lambda s: count(DV, j, s + "2"))

                def node(l, j):
                    dve.wait_ge(pe_done[l], count(PE, j, "node"))
                    dve.wait_ge(loaded[l], 32 * (j + 1))
                    if again(j):
                        dve.wait_ge(stored[l], 32 * j)
                    nc.vector.tensor_tensor(own[l][:, :, :], right[l][:, 0:2 * D].rearrange("p (u d) -> p u d", u=2),
                                            bc(c.bias[:, B_SHIFT, :], 2), ALU.add).then_inc(dve_done[l], 1)
                    nc.vector.tensor_tensor(message[l][:, 0, :], right[l][:, D:2 * D], filt[l][:, 0, :], ALU.mult).then_inc(dve_done[l], 1)

                rounds(dve, STAGES, {"norm1": norm1, "hT": copy, "n in": n_in, "norm2": norm2, "own": node}, N2)

            @block.scalar
            def _(act):
                def apply1(l, j):
                    act.wait_ge(pool_done[l], count(PO, j, "shift1"))
                    norm.apply(h, x1, l).then_inc(act_done[l], 1)

                def copy(l, j):
                    act.wait_ge(pe_done[l], count(PE, j, "turn h"))
                    nc.scalar.activation(hT[l][:, :], left[l][:, :], ACT.Copy).then_inc(act_done[l], 1)

                def rz_(l, j):
                    act.wait_ge(pe_done[l], count(PE, j, "gates"))
                    for i, bank in enumerate((left, right)):
                        nc.scalar.activation(rz[l][:, i, :], bank[l][:, D:3 * D], ACT.Tanh, scale=0.5).then_inc(act_done[l], 1)

                def n_(l, j):
                    act.wait_ge(dve_done[l], count(DV, j, "n in dst"))
                    nc.scalar.activation(n[l][:, :, :], u[l][:, :, :], ACT.Tanh).then_inc(act_done[l], 1)

                def apply2(l, j):
                    act.wait_ge(pool_done[l], count(PO, j, "shift2"))
                    norm.apply(h5, x2, l).then_inc(act_done[l], 1)

                def copy5(l, j):
                    act.wait_ge(pe_done[l], count(PE, j, "turn h5"))
                    nc.scalar.activation(hT[l][:, 0:2 * P], left[l][:, 0:2 * P], ACT.Copy).then_inc(act_done[l], 1)

                rounds(act, STAGES, {"h": apply1, "hT": copy, "rz": rz_, "n": n_, "h5": apply2, "h5T": copy5}, N2)

            @block.tensor
            def _(pe):
                def turn(l, j):
                    pe.wait_ge(act_done[l], count(AC, j, "h"))
                    pe.wait_ge(loaded[l], 32 * (j + 1))
                    pe.wait_ge(gathered[l], 48 * (j + 1))
                    if again(j):
                        pe.wait_ge(act_done[l], count(AC, j - 1, "h5T"))
                        pe.wait_ge(dve_done[l], count(DV, j - 1, "message"))
                    turn_pair(pe, c, left[l], h, l)
                    turn_pair(pe, c, left[l][:, 2 * P:4 * P], into, l).then_inc(pe_done[l], 1)
                    turn_pair(pe, c, right[l], out, l).then_inc(pe_done[l], 1)

                def gates(l, j):
                    pe.wait_ge(act_done[l], count(AC, j, "hT"))
                    pe.wait_ge(dve_done[l], count(DV, j, "outT"))
                    for i, bank in enumerate((left, right)):
                        o, cols = bank[l], slice(i * P, (i + 1) * P)
                        pe.matmul(o[:, :], c.ones3[:, :], c.bias3[:, B_HN:B_IN + 1, :].rearrange("a b d -> a (b d)"), start=True, stop=False)
                        pe.matmul(o[:, 0:3 * D], hT[l][:, cols], c.whhT[:, :, :].rearrange("p g d -> p (g d)"), start=False, stop=False)
                        pe.matmul(o[:, D:4 * D], hT[l][:, 2 * P + i * P:2 * P + (i + 1) * P], c.wfwd[:, :, :].rearrange("p g d -> p (g d)"),
                                  start=False, stop=False)
                        last = pe.matmul(o[:, D:4 * D], outT[l][:, cols], c.wrev[:, :, :].rearrange("p g d -> p (g d)"), start=False, stop=True)
                    last.then_inc(pe_done[l], 1)

                def turn5(l, j):
                    pe.wait_ge(act_done[l], count(AC, j, "h5"))
                    turn_pair(pe, c, left[l], h5, l).then_inc(pe_done[l], 1)

                def node(l, j):
                    pe.wait_ge(act_done[l], count(AC, j, "h5T"))
                    for i in range(2):
                        o = right[l][:, i * D:(i + 1) * D]
                        pe.matmul(o, c.ones3[:, :], c.bias3[:, B_NODE_MSG, :], start=True, stop=False)
                        last = pe.matmul(o, hT[l][:, i * P:(i + 1) * P], c.wnode[:, :], start=False, stop=True)
                    last.then_inc(pe_done[l], 1)

                rounds(pe, STAGES, {"turn h": turn, "gates": gates, "turn h5": turn5, "node": node}, N2)


def phase_filter(nc, c, d):
    DV = ["sum", "x", "stats", "mean", "hT", "out", "own"]
    PO = ["index", "x2", "var", "rstd", "m", "shift"]
    AC = ["h", "message"]
    PE = ["turn", "products"]
    STAGES = ["load", "sum", "factors", "h", "turn", "hT", "products", "own", "store"]
    with ExitStack() as ctx:
        w = Work(nc, ctx, "filter")
        index = w.sb("index", [P, 3], I32)
        near, s, x2, own, x, h, y = (w.sb(n, [P, 2, D]) for n in ("near", "s", "x2", "own", "x", "h", "y"))
        hT, message = w.sb("hT", [P, 2 * P]), w.sb("message", [P, D])
        norm = Norm(w, P, 2)
        left, right = w.banks("left"), w.banks("right")
        loaded, gathered, stored, written = w.sems("loaded"), w.sems("gathered"), w.sems("stored"), w.sems("written")
        pe_done, act_done, dve_done, pool_done = w.sems("pe_done"), w.sems("act_done"), w.sems("dve_done"), w.sems("pool_done")
        with nc.Block() as block:
            @block.gpsimd
            def _(pool):
                def load(l, j):
                    if again(j):
                        pool.wait_ge(written[l], 16 * j)
                        pool.wait_ge(dve_done[l], count(DV, j - 1, "x"))
                    pool.tensor_copy(index[l][:, 0:2], fields(c.rec[BY_DST], AT(l, j), R_SRC_OUT, R_DST_OUT + 1))
                    pool.tensor_copy(index[l][:, 2:3], fields(c.rec[BY_DST], AT(l, j), R_WRITE_SRC, R_WRITE_SRC + 1)).then_inc(pool_done[l], 1)
                    pool.tensor_copy(x2[l][:, :, :], pair(c.state, AT(l, j))).then_inc(pool_done[l], 1)
                    pool.wait_ge(pool_done[l], count(PO, j, "index"))
                    for i in range(2):
                        gather(pool, near[l][:, i, :], d["from"], index[l][:, i:i + 1], c.bound[SLOTS]).then_inc(gathered[l], 16)

                def factors(l, j):
                    pool.wait_ge(dve_done[l], count(DV, j, "mean"))
                    norm.factors(pool, c, l, pool_done, lambda s: count(PO, j, s))

                def write(l, j):
                    pool.wait_ge(dve_done[l], count(DV, j, "out"))
                    scatter(pool, d["out"], index[l][:, 2:3], y[l][:, 0, :], c.bound[N_NODES - 1]).then_inc(written[l], 16)

                rounds(pool, STAGES, {"load": load, "factors": factors, "store": write}, N2)
                for l in range(LANES):
                    pool.wait_ge(written[l], 16 * N2)

            @block.sync
            def _(sp):
                def load(l, j):
                    if again(j):
                        sp.wait_ge(dve_done[l], count(DV, j - 1, "sum"))
                    sp.dma_start(own[l][:, :, :], tile_rows(d["kept"], AT(l, j))).then_inc(loaded[l], 16)

                def store(l, j):
                    sp.wait_ge(act_done[l], count(AC, j, "message"))
                    sp.dma_start(tile_rows(d["message"], AT(l, j)), message[l][:, :]).then_inc(stored[l], 16)

                rounds(sp, STAGES, {"load": load, "store": store}, N2)
                for l in range(LANES):
                    sp.wait_ge(stored[l], 16 * N2)

            @block.vector
            def _(dve):
                def add(l, j):
                    dve.wait_ge(loaded[l], 16 * (j + 1))
                    dve.wait_ge(gathered[l], 32 * (j + 1))
                    nc.vector.tensor_tensor(s[l][:, :, :], near[l][:, :, :], own[l][:, :, :], ALU.add).then_inc(dve_done[l], 1)
                    dve.wait_ge(dve_done[l], count(DV, j, "sum"))
                    dve.wait_ge(pool_done[l], count(PO, j, "x2"))
                    nc.vector.scalar_tensor_tensor(x[l][:, :, :], s[l][:, :, :], 0.0, x2[l][:, :, :], ALU.max, ALU.add).then_inc(dve_done[l], 1)
                    dve.wait_ge(dve_done[l], count(DV, j, "x"))
                    norm.moments(dve, l, x, dve_done, lambda s: count(DV, j, s))

                def copy(l, j):
                    dve.wait_ge(pe_done[l], count(PE, j, "turn"))
                    nc.vector.tensor_copy(hT[l][:, :], left[l][:, 0:2 * P]).then_inc(dve_done[l], 1)

                def out(l, j):
                    dve.wait_ge(pe_done[l], count(PE, j, "products"))
                    dve.wait_ge(act_done[l], count(AC, j, "message"))
                    if again(j):
                        dve.wait_ge(written[l], 16 * j)
                    nc.vector.tensor_tensor(y[l][:, 0, :], right[l][:, 0:D], x[l][:, 0, :], ALU.add).then_inc(dve_done[l], 1)
                    t = AT(l, j)
                    mine = c.state[:, t, 1, :] if isinstance(t, int) else c.state[:, bass.ds(t, 1), 1, :].rearrange("p a d -> p (a d)")
                    nc.vector.tensor_tensor(mine, right[l][:, 2 * D:3 * D], x[l][:, 1, :], ALU.add).then_inc(dve_done[l], 1)

                rounds(dve, STAGES, {"sum": add, "hT": copy, "own": out}, N2)

            @block.scalar
            def _(act):
                def apply(l, j):
                    act.wait_ge(pool_done[l], count(PO, j, "shift"))
                    norm.apply(h, x, l).then_inc(act_done[l], 1)

                def send(l, j):
                    act.wait_ge(pe_done[l], count(PE, j, "products"))
                    if again(j):
                        act.wait_ge(stored[l], 16 * j)
                    nc.scalar.activation(message[l][:, :], right[l][:, SENT], ACT.Copy).then_inc(act_done[l], 1)

                rounds(act, STAGES, {"h": apply, "own": send}, N2)

            @block.tensor
            def _(pe):
                def turn(l, j):
                    pe.wait_ge(act_done[l], count(AC, j, "h"))
                    if again(j):
                        pe.wait_ge(dve_done[l], count(DV, j - 1, "hT"))
                    turn_pair(pe, c, left[l], h, l).then_inc(pe_done[l], 1)

                def products(l, j):
                    pe.wait_ge(dve_done[l], count(DV, j, "hT"))
                    if again(j):
                        pe.wait_ge(dve_done[l], count(DV, j - 1, "own"))
                    both = c.wout[:, :, :].rearrange("p g d -> p (g d)")
                    pe.matmul(right[l][:, 0:2 * D], c.ones3[:, :], c.bias3[:, B_OUT:B_OUT + 2, :].rearrange("a b d -> a (b d)"),
                              start=True, stop=False)
                    pe.matmul(right[l][:, 0:2 * D], hT[l][:, 0:P], both, start=False, stop=True)
                    o = right[l][:, 2 * D:3 * D]
                    pe.matmul(o, c.ones3[:, :], c.bias3[:, B_OUT, :], start=True, stop=False)
                    pe.matmul(o, hT[l][:, P:2 * P], both[:, 0:D], start=False, stop=True).then_inc(pe_done[l], 1)

                rounds(pe, STAGES, {"turn": turn, "products": products}, N2)


def build(nc, a, out):
    def table(name, rows, cols, dt=F32):
        return nc.dram_tensor(name, [rows, cols], dt, kind="Internal").ap()

    d = {"out": out}
    d["starts"] = table("starts", P * NHI, 2, I32)
    d["by_dst"] = table("by_dst", SLOTS, FIELDS, I32)
    d["by_src"] = table("by_src", SLOTS, FIELDS, I32)
    d["key_rows"] = table("key_rows", 2, SLOTS)
    d["into"] = table("into", SLOTS + P, D)
    d["from"] = table("from", SLOTS + P, D)
    d["message"] = table("message", SLOTS, D)
    d["reverse"] = table("reverse", SLOTS, D)
    d["filter"] = table("filter", SLOTS, D)
    d["kept"] = nc.dram_tensor("kept", [SLOTS, 2, D], F32, kind="Internal").ap()
    with ExitStack() as ctx:
        c = allocate(nc, ctx)
        c.bound = row_bounds(nc.gpsimd)
        phase_setup(nc, c, a)
        phase_dense(nc, c, a["x"], out)
        phase_order(nc, c, a, d)
        allocate_edges(nc, ctx, c)
        phase_keys(nc, c, d)
        phase_degrees(nc, c, d)
        phase_enter(nc, c, d, a)
        for layer in (0, 1):
            phase_sum(nc, c, d, f"sum{layer}", BY_DST, (d["message"], None), D, c.inv[BY_DST][0], "into")
            phase_layer(nc, c, d, layer + 1)
        phase_sum(nc, c, d, "sum2", BY_DST, (d["message"], None), D, c.inv[BY_DST][0], "into")
        phase_join(nc, c, d)
        phase_sum(nc, c, d, "fwd", BY_DST, (d["message"], None), D, c.inv[BY_DST][1], "into")
        phase_sum(nc, c, d, "rev", BY_SRC, (d["reverse"], R_PLACE), D, c.inv[BY_SRC][1], "from")
        phase_edges(nc, c, d, a)
        phase_gru(nc, c, d)
        phase_sum(nc, c, d, "nodes", BY_SRC, (d["reverse"], R_PLACE), D, c.inv[BY_SRC][0], "from")
        phase_filter(nc, c, d)
        phase_sum(nc, c, d, "last", BY_DST, (d["message"], None), D, None, "out")


_INS = ['x', 'src', 'dst', 'edge_attr_128', 'edge_weight', 'L0_gnn_W_l', 'L0_gnn_b_l', 'L0_gnn_W_r', 'L1_gnn_W1',
        'L1_gnn_W2', 'L1_gnn_w_ih', 'L1_gnn_w_hh', 'L1_gnn_b_ih', 'L1_gnn_b_hh', 'L2_gnn_W_node', 'L2_gnn_b_node',
        'L2_gnn_W_gate', 'L2_gnn_b_gate', 'L2_gnn_W_filt', 'L2_gnn_b_filt', 'L2_gnn_bn_gamma', 'L2_gnn_bn_beta',
        'L2_gnn_bn_mean', 'L2_gnn_bn_var', 'L3_gnn_W_neigh', 'L3_gnn_b_neigh', 'L3_gnn_W_self', 'L3_gnn_b_self']


def kernel(**inputs):
    import numpy as np
    import concourse.bacc as bacc
    from concourse.bass_utils import run_bass_kernel_spmd

    nc = bacc.Bacc("TRN2", target_bir_lowering=False, num_devices=1)
    arrays, args = {}, {}
    for name in _INS:
        arrays[name] = np.ascontiguousarray(inputs[name])
        args[name] = nc.dram_tensor(name, arrays[name].shape, mybir.dt.from_np(arrays[name].dtype), kind="ExternalInput").ap()
    out = nc.dram_tensor("out", (N_NODES, D), F32, kind="ExternalOutput").ap()
    build(nc, args, out)
    r = run_bass_kernel_spmd(nc, [arrays], core_ids=[0])
    return r.results[0]["out"]
```

```python
from contextlib import ExitStack

import concourse.bass as bass
from concourse import mybir

F32 = mybir.dt.float32
BF16 = mybir.dt.bfloat16
I32 = mybir.dt.int32
ALU = mybir.AluOpType
ACT = mybir.ActivationFunctionType

P = 128
D = 128
N_NODES = 50000
N_EDGES = 12500
TILES = 100
SLOTS = TILES * P
PAD_NODE = N_NODES
EDGE_ROWS = N_EDGES // TILES
LANES = 4
LN_EPS = 1e-5
BN_EPS = 1e-3

ND, NU = 125, 4
GROUP = ND * NU
DENSE_LANES = 5
ROUNDS = N_NODES // (GROUP * DENSE_LANES)
assert ROUNDS * DENSE_LANES == TILES
DENSE_AT = lambda l, j: DENSE_LANES * j + l
AT = lambda l, j: LANES * j + l
SPLIT = 112

(B_HN, B_R, B_Z, B_IN, B_L0, B_L1, B_L2, B_NODE_MSG, B_NODE, B_OUT, B_ZERO, B_GATE, B_FILT, B_SHIFT) = range(14)
NBIAS = 14


class Semaphores:

    def __init__(self, nc):
        self.nc, self.all = nc, []

    def __call__(self, name):
        self.all.append(self.nc.alloc_semaphore(name))
        return self.all[-1]

    def __enter__(self):
        return self

    def __exit__(self, *error):
        if error[0] is None:
            self.nc.clear_and_free_semaphores(self.all)
            self.nc.all_engine_barrier()


def rounds(eng, stages, mine, n, lanes=LANES):
    k = len(stages)
    late = [l * k // lanes for l in range(lanes)]

    def one(j, first=False, last=False):
        for slot in range(k):
            for l in range(lanes):
                s = slot - late[l]
                if s >= 0 and not last and stages[s] in mine:
                    mine[stages[s]](l, j)
                elif s < 0 and not first and stages[s + k] in mine:
                    mine[stages[s + k]](l, j - 1)

    one(0, first=True)
    one(1)
    with eng.Fori(2, n) as j:
        one(j)
    one(n, last=True)


def timetable(slots, starts):
    stages = [""] * slots
    for name, slot in starts.items():
        assert stages[slot] == ""
        stages[slot] = name
    return stages


def count(names, j, name):
    return j * len(names) + names.index(name) + 1


def again(j):
    return not (isinstance(j, int) and j == 0)


def bc(ap, n):
    return ap.unsqueeze(1).to_broadcast([ap.shape[0], n, ap.shape[1]])


def col(ap, n):
    return ap.unsqueeze(2).to_broadcast([ap.shape[0], ap.shape[1], n])


class Chip:
    pass


def allocate(nc, ctx):
    c = Chip()

    def sb(name, shape, dt):
        return ctx.enter_context(nc.sbuf_tensor(name, shape, dt))

    c.ident = sb("ident", [P, P], F32)
    c.identb = sb("identb", [P, P], BF16)
    c.wrT = sb("wrT", [P, 3, 2 * D], F32)
    c.whhT = sb("whhT", [P, 3, D], F32)
    c.wfwd = sb("wfwd", [P, 3, D], F32)
    c.wrev = sb("wrev", [P, 3, D], F32)
    c.wnode = sb("wnode", [P, D], F32)
    c.wgf = sb("wgf", [P, 2, D], F32)
    c.wout = sb("wout", [P, 2, D], F32)
    c.bcol = sb("bcol", [P, 2], F32)
    c.bias = sb("bias", [P, NBIAS, D], F32)
    c.bias3 = sb("bias3", [3, NBIAS, D], BF16)
    c.ones3 = sb("ones3", [3, P], BF16)
    c.eps = sb("eps", [P, 4], F32)
    c.minus = sb("minus", [P, 4], F32)
    c.power = sb("power", [P, P], F32)
    return c


def phase_setup(nc, c, a):
    with ExitStack() as ctx:
        def sb(name, shape, dt):
            return ctx.enter_context(nc.sbuf_tensor(name, shape, dt))

        sem = ctx.enter_context(Semaphores(nc))
        raw = sb("raw", [P, 17, D], F32)
        rows = sb("rows", [P, 18, D], F32)
        w12 = sb("w12", [P, 2, D], F32)
        wihT = sb("wihT", [P, 2, 3, D], F32)
        scale = sb("scale", [P, D], F32)
        rstd = sb("bn_rstd", [P, D], F32)
        shifted = sb("shifted", [P, D], F32)
        part = [sb(f"part{i}", [1, NBIAS * D], BF16) for i in range(3)]
        rest = [sb(f"rest{i}", [1, NBIAS * D], F32) for i in range(2)]
        turned = ctx.enter_context(nc.psum_tensor("turned", [P, 17, P], F32))
        folded = ctx.enter_context(nc.psum_tensor("folded", [P, 2, 512], F32))
        loaded = sem("loaded")
        zeroed = sem("zeroed")
        ones_set = sem("ones_set")
        ident_made = sem("ident_made")
        turns_done = sem("turns_done")
        turned_copied = sem("turned_copied")
        folds_done = sem("folds_done")
        folds_copied = sem("folds_copied")
        vec = sem("vec")
        rstd_made = sem("rstd_made")
        parts_placed = sem("parts_placed")
        block = ctx.enter_context(nc.Block())
        IH, HH, NODE, GATE, FILT, GAMMA, BETA, MEAN, VAR, NEIGH, SELF = 3, 6, 9, 10, 11, 12, 13, 14, 15, 16, 17
        loads = []
        for i in range(3):
            loads.append((raw[:, i, :], a["L0_gnn_W_l"][i]))
            loads.append((raw[:, 3 + i, :], a["L0_gnn_W_r"][i]))
            loads.append((raw[:, 6 + i, :], a["L1_gnn_w_hh"][i * D:(i + 1) * D, :]))
            for h in range(2):
                loads.append((raw[:, 9 + 3 * h + i, :], a["L1_gnn_w_ih"][i * D:(i + 1) * D, h * D:(h + 1) * D]))
        loads.append((raw[:, 15, :], a["L3_gnn_W_self"]))
        loads.append((raw[:, 16, :], a["L3_gnn_W_neigh"]))
        loads.append((w12[:, 0, :], a["L1_gnn_W1"]))
        loads.append((w12[:, 1, :], a["L1_gnn_W2"]))
        loads.append((c.wnode[:, :], a["L2_gnn_W_node"]))
        loads.append((c.wgf[:, 0, :], a["L2_gnn_W_gate"]))
        loads.append((c.wgf[:, 1, :], a["L2_gnn_W_filt"]))
        vectors = [a["L0_gnn_b_l"][i] for i in range(3)]
        for v in ("L1_gnn_b_ih", "L1_gnn_b_hh"):
            vectors += [a[v][i * D:(i + 1) * D] for i in range(3)]
        vectors += [a["L2_gnn_" + v] for v in ("b_node", "b_gate", "b_filt", "bn_gamma", "bn_beta", "bn_mean", "bn_var")]
        vectors += [a["L3_gnn_b_neigh"], a["L3_gnn_b_self"]]
        for i, v in enumerate(vectors):
            loads.append((rows[:, i, :], v.partition_broadcast(P)))
        for i in range(2):
            loads.append((c.bcol[:, i:i + 1], a["L0_gnn_b_l"][i].rearrange("(p x) -> p x", x=1)))

        @block.sync
        def _(sp):
            for out, src in loads:
                sp.dma_start(out, src).then_inc(loaded, 16)
            sp.wait_ge(vec, 22)
            for i in range(3):
                sp.dma_start(c.bias3[i:i + 1, :, :].rearrange("a b d -> a (b d)"), part[i][:, :]).then_inc(parts_placed, 16)
            sp.wait_ge(parts_placed, 48)

        @block.gpsimd
        def _(pool):
            pool.memset(c.ident[:, :], 0.0).then_inc(zeroed, 1)
            pool.memset(c.ones3[:, :], 1.0).then_inc(ones_set, 1)
            pool.wait_ge(zeroed, 1)
            pool.affine_select(out=c.ident[:, :], in_=c.ident[:, :], compare_op=ALU.not_equal, fill=1.0,
                               base=0, pattern=[[-1, P]], channel_multiplier=1).then_inc(ident_made, 1)
            pool.memset(c.power[:, :], -0.5).then_inc(zeroed, 1)
            pool.memset(c.eps[:, :], LN_EPS)
            pool.memset(c.minus[:, :], -1.0)
            pool.wait_ge(loaded, 16 * len(loads))
            pool.tensor_scalar(scale[:, :], rows[:, VAR, :], BN_EPS, None, ALU.add).then_inc(zeroed, 1)
            pool.wait_ge(zeroed, 3)
            pool.tensor_tensor(rstd[:, :], scale[:, :], c.power[:, :], ALU.pow).then_inc(rstd_made, 1)

        @block.tensor
        def _(pe):
            pe.wait_ge(ident_made, 1)
            pe.wait_ge(loaded, 16 * len(loads))
            for i in range(17):
                pe.transpose(turned[:, i, :], raw[:, i, :], c.ident[:, :]).then_inc(turns_done, 1)
            pe.wait_ge(turned_copied, 17)
            for h in range(2):
                pe.matmul(folded[:, h, 0:3 * D], w12[:, h, :], wihT[:, h, :, :].rearrange("p g d -> p (g d)"),
                          start=True, stop=True).then_inc(folds_done, 1)

        @block.scalar
        def _(act):
            place = [c.wrT[:, i, D:2 * D] for i in range(3)] + [c.wrT[:, i, 0:D] for i in range(3)]
            place += [c.whhT[:, i, :] for i in (1, 2, 0)]
            place += [wihT[:, h, i, :] for h in range(2) for i in range(3)]
            place += [c.wout[:, 0, :], c.wout[:, 1, :]]
            for i, out in enumerate(place):
                act.wait_ge(turns_done, 17)
                nc.scalar.activation(out, turned[:, i, :], ACT.Copy).then_inc(turned_copied, 1)
            for h, out in enumerate((c.wfwd, c.wrev)):
                act.wait_ge(folds_done, 2)
                nc.scalar.activation(out[:, :, :], folded[:, h, 0:3 * D].rearrange("p (g d) -> p g d", g=3),
                                     ACT.Copy).then_inc(folds_copied, 1)

        @block.vector
        def _(dve):
            dve.wait_ge(ident_made, 1)
            nc.vector.tensor_copy(c.identb[:, :], c.ident[:, :]).then_inc(vec, 1)
            dve.wait_ge(loaded, 16 * len(loads))
            b = c.bias
            for out, row in ((B_HN, HH + 2), (B_IN, IH + 2), (B_L0, 0), (B_L1, 1), (B_L2, 2), (B_GATE, GATE), (B_FILT, FILT)):
                nc.vector.tensor_copy(b[:, out, :], rows[:, row, :]).then_inc(vec, 1)
            nc.vector.memset(b[:, B_ZERO, :], 0.0)
            for out, x, y in ((B_R, IH, HH), (B_Z, IH + 1, HH + 1), (B_OUT, NEIGH, SELF)):
                nc.vector.tensor_tensor(b[:, out, :], rows[:, x, :], rows[:, y, :], ALU.add).then_inc(vec, 1)
            dve.wait_ge(rstd_made, 1)
            nc.vector.tensor_tensor(scale[:, :], rstd[:, :], rows[:, GAMMA, :], ALU.mult).then_inc(vec, 1)
            dve.wait_ge(vec, 12)
            nc.vector.tensor_tensor(c.wnode[:, :], c.wnode[:, :], scale[:, :], ALU.mult).then_inc(vec, 1)
            nc.vector.tensor_tensor(b[:, B_NODE_MSG, :], rows[:, NODE, :], scale[:, :], ALU.mult).then_inc(vec, 1)
            nc.vector.tensor_tensor(shifted[:, :], rows[:, MEAN, :], scale[:, :], ALU.mult).then_inc(vec, 1)
            dve.wait_ge(vec, 15)
            nc.vector.tensor_tensor(b[:, B_SHIFT, :], rows[:, BETA, :], shifted[:, :], ALU.subtract).then_inc(vec, 1)
            dve.wait_ge(vec, 16)
            nc.vector.tensor_tensor(b[:, B_NODE, :], b[:, B_NODE_MSG, :], b[:, B_SHIFT, :], ALU.add).then_inc(vec, 1)
            dve.wait_ge(vec, 17)
            whole = b[0:1, :, :].rearrange("a b d -> a (b d)")
            nc.vector.tensor_copy(part[0][:, :], whole).then_inc(vec, 1)
            dve.wait_ge(vec, 18)
            nc.vector.tensor_tensor(rest[0][:, :], whole, part[0][:, :], ALU.subtract).then_inc(vec, 1)
            dve.wait_ge(vec, 19)
            nc.vector.tensor_copy(part[1][:, :], rest[0][:, :]).then_inc(vec, 1)
            dve.wait_ge(vec, 20)
            nc.vector.tensor_tensor(rest[1][:, :], rest[0][:, :], part[1][:, :], ALU.subtract).then_inc(vec, 1)
            dve.wait_ge(vec, 21)
            nc.vector.tensor_copy(part[2][:, :], rest[1][:, :]).then_inc(vec, 1)


def phase_dense(nc, c, x_dram, out_dram, d, e):
    x_view = x_dram.rearrange("(g p u) d -> g p u d", p=ND, u=NU)
    out_view = out_dram.rearrange("(g p u) d -> g p u d", p=ND, u=NU)
    PE = ["h0T", "h1T", "h2T", "h3", "h4T", "rz low", "rz high", "hn", "h5T", "node", "h6T", "self"]
    AC = ["h0", "h0T", "h1T", "h4", "h4T", "rz low", "rz high", "n", "h5T", "h6T"]
    DV = ["stats0", "mean0", "var0", "shift0", "h2T", "x1", "stats1", "mean1", "var1", "shift1", "r hn", "n in", "z mix",
          "x2", "stats2", "mean2", "var2", "h5", "x3", "stats3", "mean3", "var3", "h6", "out"]
    PO = ["rstd0", "rstd1", "h4 - n", "n + x1", "rstd2", "rstd3"]
    STAGES = timetable(316, {"load": 1, "ln0": 13, "rstd0": 21, "shift0": 29, "h0": 31, "h0T": 39, "h0T copy": 43, "h1T": 47,
                             "h1T relu": 55, "look up": 56, "h2T": 59, "h2T relu": 65, "h3": 69, "ln1": 82, "rstd1": 93,
                             "shift1": 99, "h4": 109, "record": 110, "h4T": 117, "h4T copy": 121, "gates low": 126,
                             "rz low": 132, "send": 133, "gates high": 137, "rz high": 144, "hn": 148, "n in": 156, "n": 164,
                             "mix": 168, "ln2": 180, "rstd2": 193, "h5": 199, "h5T": 205, "h5T copy": 209, "node": 216,
                             "ln3": 226, "rstd3": 241, "h6": 257, "h6T": 270, "h6T copy": 274, "self": 284, "out": 297,
                             "store": 302})
    with ExitStack() as ctx:
        w = Work(nc, ctx, "dense", DENSE_LANES)
        x, x1, x2, x3, y, h, h4, u, n, apart, both = (w.sb(s, [ND, NU, D]) for s in (
            "x", "x1", "x2", "x3", "y", "h", "h4", "u", "n", "apart", "both"))
        hT, gT = w.sb("hT", [P, GROUP]), w.sb("gT", [P, GROUP])
        rz = w.sb("rz", [ND, NU, 2 * D])
        norm = Norm(w, ND, NU)
        bank = w.banks("bank")
        loaded, stored = w.sems("x_loaded"), w.sems("out_stored")
        pe_done, act_done, dve_done, pool_done = w.sems("pe_done"), w.sems("act_done"), w.sems("dve_done"), w.sems("pool_done")
        records = Records(nc, w, c, d, e)
        block = ctx.enter_context(nc.Block())

        def rows(t):
            return t[0:ND, 0:NU * D].rearrange("p (u d) -> p u d", u=NU)

        def dv(j, name):
            return count(DV, j, name)

        def ac(j, name):
            return count(AC, j, name)

        def pn(j, name):
            return count(PE, j, name)

        def po(j, name):
            return count(PO, j, name)

        def part(view, g, lo, hi):
            return view[g, lo:hi] if isinstance(g, int) else view[bass.ds(g, 1), lo:hi].rearrange("g p u d -> (g p) u d")

        @block.sync
        def _(sp):
            def load(l, j):
                if again(j):
                    sp.wait_ge(dve_done[l], dv(j - 1, "x1"))
                for lo, hi in ((0, SPLIT), (SPLIT, ND)):
                    sp.dma_start(x[l][lo:hi, :, :], part(x_view, DENSE_AT(l, j), lo, hi)).then_inc(loaded[l], 16)

            def store(l, j):
                sp.wait_ge(dve_done[l], dv(j, "out"))
                for lo, hi in ((0, SPLIT), (SPLIT, ND)):
                    sp.dma_start(part(out_view, DENSE_AT(l, j), lo, hi), y[l][lo:hi, :, :]).then_inc(stored[l], 16)

            rounds(sp, STAGES, {"load": load, "store": store}, ROUNDS, DENSE_LANES)
            for l in range(DENSE_LANES):
                sp.wait_ge(stored[l], 32 * ROUNDS)

        @block.gpsimd
        def _(pool):
            def factors(k):
                def go(l, j):
                    pool.wait_ge(dve_done[l], dv(j, "var" + k))
                    norm.power(pool, c, l).then_inc(pool_done[l], 1)
                return go

            def mix(l, j):
                pool.wait_ge(act_done[l], ac(j, "n"))
                if again(j):
                    pool.wait_ge(dve_done[l], dv(j - 1, "x2"))
                pool.tensor_tensor(apart[l][:, :, :], h4[l][:, :, :], n[l][:, :, :], ALU.subtract).then_inc(pool_done[l], 1)
                pool.tensor_tensor(both[l][:, :, :], n[l][:, :, :], x1[l][:, :, :], ALU.add).then_inc(pool_done[l], 1)

            rounds(pool, STAGES, {"mix": mix, "look up": records.look_up(pool), "send": records.send(pool)}
                   | {"rstd" + k: factors(k) for k in "0123"}, ROUNDS, DENSE_LANES)
            records.finish(pool)

        @block.tensor
        def _(pe):
            def turn(src, l):
                for i in range(NU):
                    last = pe.transpose(bank[l][:, i * ND:(i + 1) * ND], src[l][:, i, :], c.ident[0:ND, 0:ND])
                last.then_inc(pe_done[l], 1)

            def h0T(l, j):
                pe.wait_ge(act_done[l], ac(j, "h0"))
                if again(j):
                    pe.wait_ge(dve_done[l], dv(j - 1, "out"))
                turn(h, l)

            def h1T(l, j):
                pe.wait_ge(act_done[l], ac(j, "h0T"))
                pe.matmul(bank[l][:, 0:GROUP], c.wrT[:, 0, 0:D], hT[l][:, :], start=True, stop=True).then_inc(pe_done[l], 1)

            def h2T(l, j):
                pe.wait_ge(act_done[l], ac(j, "h1T"))
                pe.matmul(bank[l][:, 0:GROUP], c.wrT[:, 1, 0:D], gT[l][:, :], start=True, stop=True).then_inc(pe_done[l], 1)

            def rowwise(l, lhs, rhs, bias):
                for i in range(NU):
                    o = bank[l][0:ND, i * D:(i + 1) * D]
                    pe.matmul(o, c.ones3[:, 0:ND], c.bias3[:, bias, :], start=True, stop=False)
                    last = pe.matmul(o, lhs[l][:, i * ND:(i + 1) * ND], rhs, start=False, stop=True)
                last.then_inc(pe_done[l], 1)

            def h3(l, j):
                pe.wait_ge(dve_done[l], dv(j, "h2T"))
                rowwise(l, hT, c.wrT[:, 2, 0:D], B_L2)

            def h4T(l, j):
                pe.wait_ge(act_done[l], ac(j, "h4"))
                turn(h4, l)

            def gates(k, waited):
                def go(l, j):
                    pe.wait_ge(act_done[l], ac(j, waited))
                    for i in range(2):
                        o = bank[l][0:ND, i * 2 * D:(i + 1) * 2 * D]
                        at = 2 * k + i
                        pe.matmul(o, c.ones3[:, 0:ND], c.bias3[:, B_R:B_Z + 1, :].rearrange("a b d -> a (b d)"),
                                  start=True, stop=False)
                        last = pe.matmul(o, gT[l][:, at * ND:(at + 1) * ND], c.whhT[:, 1:3, :].rearrange("p g d -> p (g d)"),
                                         start=False, stop=True)
                    last.then_inc(pe_done[l], 1)
                return go

            def hn(l, j):
                pe.wait_ge(act_done[l], ac(j, "rz high"))
                rowwise(l, gT, c.whhT[:, 0, :], B_HN)

            def h5T(l, j):
                pe.wait_ge(dve_done[l], dv(j, "h5"))
                turn(h, l)

            def node(l, j):
                pe.wait_ge(act_done[l], ac(j, "h5T"))
                rowwise(l, hT, c.wnode[:, :], B_NODE)

            def h6T(l, j):
                pe.wait_ge(dve_done[l], dv(j, "h6"))
                turn(h, l)

            def own(l, j):
                pe.wait_ge(act_done[l], ac(j, "h6T"))
                rowwise(l, gT, c.wout[:, 0, :], B_OUT)

            rounds(pe, STAGES, {"h0T": h0T, "h1T": h1T, "h2T": h2T, "h3": h3, "h4T": h4T, "gates low": gates(0, "h4T"), "gates high": gates(1, "rz low"), "hn": hn, "h5T": h5T,
                                "node": node, "h6T": h6T, "self": own}, ROUNDS, DENSE_LANES)

        @block.scalar
        def _(act):
            def relu_of(out, name):
                def go(l, j):
                    act.wait_ge(pe_done[l], pn(j, name))
                    nc.scalar.activation(out[l][:, :], bank[l][:, 0:GROUP], ACT.Relu).then_inc(act_done[l], 1)
                return go

            def h0(l, j):
                act.wait_ge(dve_done[l], dv(j, "shift0"))
                if again(j):
                    act.wait_ge(pe_done[l], pn(j - 1, "h6T"))
                norm.apply(h, x, l).then_inc(act_done[l], 1)

            def h1T(l, j):
                act.wait_ge(pe_done[l], pn(j, "h1T"))
                nc.scalar.activation(gT[l][:, :], bank[l][:, 0:GROUP], ACT.Relu, bias=c.bcol[:, 0:1]).then_inc(act_done[l], 1)

            def h4_(l, j):
                act.wait_ge(dve_done[l], dv(j, "shift1"))
                if again(j):
                    act.wait_ge(pool_done[l], po(j - 1, "h4 - n"))
                norm.apply(h4, x1, l).then_inc(act_done[l], 1)

            def rz_(k, name):
                def go(l, j):
                    act.wait_ge(pe_done[l], pn(j, name))
                    nc.scalar.activation(rz[l][:, 2 * k:2 * k + 2, :], bank[l][0:ND, :].rearrange("p (u c) -> p u c", u=2),
                                         ACT.Tanh, scale=0.5).then_inc(act_done[l], 1)
                return go

            def n_(l, j):
                act.wait_ge(dve_done[l], dv(j, "n in"))
                nc.scalar.activation(n[l][:, :, :], u[l][:, :, :], ACT.Tanh).then_inc(act_done[l], 1)

            rounds(act, STAGES, {"h0": h0, "h0T copy": relu_of(hT, "h0T"), "h1T relu": h1T, "h4": h4_,
                                 "h4T copy": relu_of(gT, "h4T"), "rz low": rz_(0, "rz low"), "rz high": rz_(1, "rz high"), "n": n_, "h5T copy": relu_of(hT, "h5T"),
                                 "h6T copy": relu_of(gT, "h6T")}, ROUNDS, DENSE_LANES)

        @block.vector
        def _(dve):
            def moments(l, j, src, k):
                norm.factor_base(dve, l, src[l], dve_done, lambda s: dv(j, s + k))

            def shift(k):
                def go(l, j):
                    dve.wait_ge(pool_done[l], po(j, "rstd" + k))
                    norm.move(l).then_inc(dve_done[l], 1)
                return go

            def apply(src, k):
                def go(l, j):
                    dve.wait_ge(pool_done[l], po(j, "rstd" + k))
                    norm.apply_here(h, src[l], l).then_inc(dve_done[l], 1)
                return go

            def ln0(l, j):
                dve.wait_ge(loaded[l], (j + 1) * 32)
                moments(l, j, x, "0")

            def h2T(l, j):
                dve.wait_ge(pe_done[l], pn(j, "h2T"))
                nc.vector.tensor_scalar(hT[l][:, :], bank[l][:, 0:GROUP], c.bcol[:, 1:2], 0.0, ALU.add, ALU.max)\
                    .then_inc(dve_done[l], 1)

            def ln1(l, j):
                dve.wait_ge(pe_done[l], pn(j, "h3"))
                if again(j):
                    dve.wait_ge(pool_done[l], po(j - 1, "n + x1"))
                nc.vector.tensor_tensor(x1[l][:, :, :], rows(bank[l]), x[l][:, :, :], ALU.add).then_inc(dve_done[l], 1)
                dve.wait_ge(dve_done[l], dv(j, "x1"))
                moments(l, j, x1, "1")

            def n_in(l, j):
                dve.wait_ge(pe_done[l], pn(j, "hn"))
                nc.vector.scalar_tensor_tensor(u[l][:, :, :], rz[l][:, :, 0:D], 1.0, rows(bank[l]), ALU.add, ALU.mult)\
                    .then_inc(dve_done[l], 1)
                dve.wait_ge(dve_done[l], dv(j, "r hn"))
                nc.vector.scalar_tensor_tensor(u[l][:, :, :], u[l][:, :, :], 0.5, bc(c.bias[0:ND, B_IN, :], NU),
                                               ALU.mult, ALU.add).then_inc(dve_done[l], 1)

            def ln2(l, j):
                dve.wait_ge(pool_done[l], po(j, "n + x1"))
                nc.vector.scalar_tensor_tensor(u[l][:, :, :], rz[l][:, :, D:2 * D], 1.0, apart[l][:, :, :], ALU.add, ALU.mult)\
                    .then_inc(dve_done[l], 1)
                dve.wait_ge(dve_done[l], dv(j, "z mix"))
                nc.vector.scalar_tensor_tensor(x2[l][:, :, :], u[l][:, :, :], 0.5, both[l][:, :, :], ALU.mult, ALU.add)\
                    .then_inc(dve_done[l], 1)
                dve.wait_ge(dve_done[l], dv(j, "x2"))
                moments(l, j, x2, "2")

            def ln3(l, j):
                dve.wait_ge(pe_done[l], pn(j, "node"))
                nc.vector.scalar_tensor_tensor(x3[l][:, :, :], rows(bank[l]), 0.0, x2[l][:, :, :], ALU.max, ALU.add)\
                    .then_inc(dve_done[l], 1)
                dve.wait_ge(dve_done[l], dv(j, "x3"))
                moments(l, j, x3, "3")

            def out(l, j):
                dve.wait_ge(pe_done[l], pn(j, "self"))
                if again(j):
                    dve.wait_ge(stored[l], j * 32)
                nc.vector.tensor_tensor(y[l][:, :, :], rows(bank[l]), x3[l][:, :, :], ALU.add).then_inc(dve_done[l], 1)

            rounds(dve, STAGES, {"ln0": ln0, "shift0": shift("0"), "h2T relu": h2T, "ln1": ln1, "shift1": shift("1"), "n in": n_in,
                                 "ln2": ln2, "h5": apply(x2, "2"), "ln3": ln3, "h6": apply(x3, "3"), "out": out, "record": records.make(dve)}, ROUNDS, DENSE_LANES)


class Work:

    def __init__(self, nc, ctx, name, lanes=LANES):
        self.nc, self.ctx, self.name, self.lanes = nc, ctx, name, lanes
        self.semaphore = ctx.enter_context(Semaphores(nc))

    def sb(self, name, shape, dt=F32):
        return [self.one(f"{name}{l}", shape, dt) for l in range(self.lanes)]

    def one(self, name, shape, dt=F32):
        return self.ctx.enter_context(self.nc.sbuf_tensor(f"{self.name}_{name}", shape, dt))

    def bank(self, name):
        return self.ctx.enter_context(self.nc.psum_tensor(f"{self.name}_{name}", [P, 512], F32))

    def banks(self, name):
        return [self.bank(f"{name}{l}") for l in range(self.lanes)]

    def sem(self, name):
        return self.semaphore(f"{self.name}_{name}")

    def sems(self, name):
        return [self.sem(f"{name}{l}") for l in range(self.lanes)]


def one_of(t, j):
    return t[:, j] if isinstance(j, int) else t[:, bass.ds(j, 1)].rearrange(
        "p a b -> p (a b)" if len(t.shape) == 3 else "p a b c -> p (a b) c")


def tile_of_two(t, j):
    return t[:, :, j] if isinstance(j, int) else t[:, :, bass.ds(j, 1)].rearrange("p a b -> p (a b)")


def column(t, j):
    return t[:, j:j + 1] if isinstance(j, int) else t[:, bass.ds(j, 1)]


def tile_rows(table, j):
    return table[j * P:(j + 1) * P] if isinstance(j, int) else table[bass.ds(j * P, P)]


def row_bounds(pool):
    found = {}
    for row in (P * NHI - 1, SLOTS - 1, SLOTS, N_NODES - 1, N_EDGES - 1):
        found[row] = pool.alloc_register(f"before_bound{row}"), pool.alloc_register(f"bound{row}")
        pool.reg_mov(found[row][0], row - 1)
    return found


def gather(pool, out, table, index, bound):
    kept, bound = bound
    pool.reg_alu(bound, kept, 1, ALU.add)
    return pool.indirect_dma_start(out=out, out_offset=None, in_=table, in_offset=bass.IndirectOffsetOnAxis(ap=index, axis=0),
                                   bounds_check=bound, oob_is_err=False)


def scatter(pool, table, index, src, bound):
    kept, bound = bound
    pool.reg_alu(bound, kept, 1, ALU.add)
    return pool.indirect_dma_start(out=table, out_offset=bass.IndirectOffsetOnAxis(ap=index, axis=0), in_=src, in_offset=None,
                                   bounds_check=bound, oob_is_err=False)


(R_SRC, R_DST, R_EDGE, R_WRITE_DST, R_WEIGHT, R_SRC_KEY, R_DST_KEY, R_DST_OUT, R_SRC_IN, R_SRC_OUT, R_WRITE_SRC,
 R_PLACE) = range(12)
OWN_FIELDS = R_DST_OUT
FIELDS = 12
NHI = -(-(PAD_NODE + 1) // P)
FAR = float(1 << 16)
BY_DST, BY_SRC = 0, 1


def phase_order(nc, c, a, d, e):
    DV = ["lo", "hi", "before", "rank", "kept"]
    AC = ["turned bf16", "turned f32", "histogram"]
    PE = ["turned", "same", "rank"]
    STAGES = ["one-hot", "turn", "turned", "same", "before", "snapshot", "add", "look", "keep"]
    n_rounds = TILES // 2
    with ExitStack() as ctx:
        w = Work(nc, ctx, "order")
        keys = w.one("keys", [P, 2, TILES], I32)
        parts = w.one("parts", [P, 2, 2, TILES], I32)
        lof = w.one("lof", [P, 2, TILES])
        hif = w.one("hif", [P, 2, TILES])
        keyf = w.one("keyf", [P, 2, TILES])
        weight = w.one("weight", [P, TILES])
        edge = w.one("edge", [P, TILES])
        entry, rank = e.entry, e.rank
        ramp = w.one("ramp", [P, NHI])
        earlier = w.one("earlier", [P, P])
        onlo, onloT = w.sb("onlo", [P, P], BF16), w.sb("onloT", [P, P], BF16)
        onloTf = w.sb("onloTf", [P, P])
        onhi = w.sb("onhi", [P, NHI], BF16)
        lesser = w.sb("lesser", [P, P], BF16)
        history = w.sb("history", [P, NHI])
        product = w.sb("product", [P, NHI])
        found = w.sb("found", [P, 1])
        zero = w.one("zero", [P, NHI])
        zerob = w.one("zerob", [P, NHI], BF16)
        counts = w.one("counts", [P, 2, NHI])
        running = w.one("running", [P, 2, NHI])
        total = w.one("total", [P, 2])
        offset = w.one("offset", [P, 2])
        start = w.one("start", [P, 2, NHI])
        starts = w.one("starts", [P, NHI, 2], I32)
        work = w.banks("work")
        hist = [w.bank("hist0"), w.bank("hist1")]
        loaded, made, prepared, setup = w.sem("loaded"), w.sem("made"), w.sem("prepared"), w.sem("setup")
        pe_done, act_done, dve_done = w.sems("pe_done"), w.sems("act_done"), w.sems("dve_done")
        added = [w.sem("added0"), w.sem("added1")]
        snapped = [w.sem("snapped0"), w.sem("snapped1")]
        table_step, table_stored, sums_done = w.sem("table_step"), w.sem("table_stored"), w.sem("sums_done")

        with nc.Block() as block:
            @block.sync
            def _(sp):
                sp.wait_ge(made, 8)
                for k, name in ((BY_DST, "dst"), (BY_SRC, "src")):
                    sp.dma_start(keys[0:EDGE_ROWS, k, :], a[name].rearrange("(p t) -> p t", t=TILES)).then_inc(loaded, 16)
                sp.dma_start(weight[0:EDGE_ROWS, :], a["edge_weight"].rearrange("(p t) -> p t", t=TILES)).then_inc(loaded, 16)
                sp.wait_ge(table_step, 9)
                sp.dma_start(d["starts"].rearrange("(p h) k -> p h k", p=P), starts[:, :, :]).then_inc(table_stored, 16)
                sp.wait_ge(table_stored, 16)

            @block.gpsimd
            def _(pool):
                pool.memset(keys[:, :, :], PAD_NODE).then_inc(made, 1)
                pool.memset(weight[:, :], 0.0).then_inc(made, 1)
                pool.memset(zero[:, :], 0.0).then_inc(made, 1)
                pool.memset(zerob[:, :], 0.0).then_inc(made, 1)
                pool.memset(earlier[:, :], 1.0).then_inc(made, 1)
                pool.iota(ramp[:, :], pattern=[[1, NHI]], base=0, channel_multiplier=0,
                          allow_small_or_imprecise_dtypes=True).then_inc(made, 1)
                pool.iota(edge[:, :], pattern=[[1, TILES]], base=0, channel_multiplier=TILES,
                          allow_small_or_imprecise_dtypes=True).then_inc(made, 1)
                pool.wait_ge(made, 7)
                pool.affine_select(out=earlier[:, :], in_=earlier[:, :], compare_op=ALU.is_gt, fill=0.0,
                                   base=0, pattern=[[1, P]], channel_multiplier=-1).then_inc(made, 1)

            @block.vector
            def _(dve):
                dve.wait_ge(loaded, 48)
                flat = keys[:, :, :]
                nc.vector.tensor_scalar(parts[:, 0], flat, P - 1, None, ALU.bitwise_and).then_inc(prepared, 1)
                nc.vector.tensor_scalar(parts[:, 1], flat, 7, None, ALU.logical_shift_right).then_inc(prepared, 1)
                nc.vector.tensor_copy(keyf[:, :, :], flat).then_inc(prepared, 1)
                dve.wait_ge(prepared, 3)
                nc.vector.tensor_copy(lof[:, :, :], parts[:, 0]).then_inc(prepared, 1)
                nc.vector.tensor_copy(hif[:, :, :], parts[:, 1]).then_inc(prepared, 1)
                dve.wait_ge(prepared, 5)
                nc.vector.scalar_tensor_tensor(entry[:, :, :], lof[:, :, :], float(NHI), hif[:, :, :], ALU.mult, ALU.add)\
                    .then_inc(prepared, 1)
                dve.wait_ge(prepared, 6)

                def onehot(l, j):
                    k, t = l // 2, 2 * j + l % 2
                    if again(j):
                        dve.wait_ge(pe_done[l], count(PE, j - 1, "rank"))
                    nc.vector.tensor_scalar(onlo[l][:, :], ramp[:, 0:P], column(lof[:, k], t), None, ALU.is_equal)\
                        .then_inc(dve_done[l], 1)
                    nc.vector.tensor_scalar(onhi[l][:, :], ramp[:, :], column(hif[:, k], t), None, ALU.is_equal)\
                        .then_inc(dve_done[l], 1)

                def before(l, j):
                    dve.wait_ge(pe_done[l], count(PE, j, "same"))
                    nc.vector.tensor_tensor(lesser[l][:, :], work[l][:, 0:P], earlier[:, :], ALU.mult).then_inc(dve_done[l], 1)

                def keep(l, j):
                    k, t = l // 2, 2 * j + l % 2
                    dve.wait_ge(pe_done[l], count(PE, j, "rank"))
                    if again(j):
                        dve.wait_ge(dve_done[l], count(DV, j - 1, "kept"))
                    nc.vector.tensor_tensor_reduce(product[l][:, :], work[l][:, 0:NHI], onhi[l][:, :], 1.0, 0.0,
                                                   ALU.mult, ALU.add, found[l][:, :]).then_inc(dve_done[l], 1)
                    dve.wait_ge(dve_done[l], count(DV, j, "rank"))
                    nc.vector.tensor_copy(column(rank[:, k], t), found[l][:, :]).then_inc(dve_done[l], 1)

                rounds(dve, STAGES, {"one-hot": onehot, "before": before, "keep": keep}, n_rounds)
                dve.wait_ge(sums_done, 1)
                for k in range(2):
                    nc.vector.tensor_tensor_scan(running[:, k, :], counts[:, k, :], zero[:, :], 0.0, ALU.add, ALU.add)\
                        .then_inc(table_step, 1)
                dve.wait_ge(table_step, 2)
                nc.vector.tensor_copy(total[:, :], running[:, :, NHI - 1]).then_inc(table_step, 1)
                dve.wait_ge(sums_done, 2)
                nc.vector.tensor_copy(offset[:, :], work[0][:, 0:2]).then_inc(table_step, 1)
                dve.wait_ge(table_step, 4)
                for k in range(2):
                    nc.vector.scalar_tensor_tensor(start[:, k, :], running[:, k, :], offset[:, k:k + 1], counts[:, k, :],
                                                   ALU.add, ALU.subtract).then_inc(table_step, 1)
                dve.wait_ge(table_step, 6)
                nc.vector.tensor_scalar(counts[:, :, :], counts[:, :, :], 0.0, None, ALU.is_gt).then_inc(table_step, 1)
                dve.wait_ge(table_step, 7)
                nc.vector.scalar_tensor_tensor(running[:, :, :], start[:, :, :], -float(SLOTS), counts[:, :, :], ALU.add, ALU.mult)\
                    .then_inc(table_step, 1)
                dve.wait_ge(table_step, 8)
                nc.vector.tensor_scalar(starts[:, :, :].rearrange("p h k -> p k h"), running[:, :, :], float(SLOTS), None,
                                        ALU.add).then_inc(table_step, 1)

            @block.scalar
            def _(act):
                def turned(l, j):
                    act.wait_ge(pe_done[l], count(PE, j, "turned"))
                    nc.scalar.activation(onloT[l][:, :], work[l][:, 0:P // 2].bitcast(BF16), ACT.Copy).then_inc(act_done[l], 1)
                    nc.scalar.activation(onloTf[l][:, :], work[l][:, 0:P // 2].bitcast(BF16), ACT.Copy).then_inc(act_done[l], 1)

                def snapshot(l, j):
                    k, t = l // 2, 2 * j + l % 2
                    act.wait_ge(added[k], t + 1)
                    if again(j):
                        act.wait_ge(pe_done[l], count(PE, j - 1, "rank"))
                    nc.scalar.activation(history[l][:, :], hist[k][:, 0:NHI], ACT.Copy).then_inc(act_done[l], 1)

                rounds(act, STAGES, {"turned": turned, "snapshot": snapshot}, n_rounds)
                for k in range(2):
                    act.wait_ge(added[k], TILES + 2)
                    last = nc.scalar.activation(counts[:, k, :], hist[k][:, 0:NHI], ACT.Copy)
                last.then_inc(sums_done, 1)

            @block.tensor
            def _(pe):
                pe.wait_ge(made, 8)
                for k in range(2):
                    pe.matmul(hist[k][:, 0:NHI], zerob[:, 0:P], zerob[:, :], start=True, stop=True).then_inc(added[k], 1)

                def turn(l, j):
                    pe.wait_ge(dve_done[l], count(DV, j, "lo"))
                    if again(j):
                        pe.wait_ge(dve_done[l], count(DV, j - 1, "rank"))
                    pe.transpose(work[l][:, 0:P // 2].bitcast(BF16), onlo[l][:, :], c.identb[:, :]).then_inc(pe_done[l], 1)

                def same(l, j):
                    pe.wait_ge(act_done[l], count(AC, j, "turned f32"))
                    pe.matmul(work[l][:, 0:P], onloT[l][:, :], onloT[l][:, :], start=True, stop=True).then_inc(pe_done[l], 1)

                def add(l, j):
                    k, t = l // 2, 2 * j + l % 2
                    pe.wait_ge(dve_done[l], count(DV, j, "hi"))
                    pe.wait_ge(act_done[l], count(AC, j, "histogram"))
                    pe.matmul(hist[k][:, 0:NHI], onlo[l][:, :], onhi[l][:, :], start=False, stop=True,
                              skip_group_check=True).then_inc(added[k], 1)

                def look(l, j):
                    pe.wait_ge(dve_done[l], count(DV, j, "before"))
                    pe.matmul(work[l][:, 0:NHI], onloTf[l][:, :], history[l][:, :], start=True, stop=False)
                    pe.matmul(work[l][:, 0:NHI], lesser[l][:, :], onhi[l][:, :], start=False, stop=True).then_inc(pe_done[l], 1)

                rounds(pe, STAGES, {"turn": turn, "same": same, "add": add, "look": look}, n_rounds)
                for k in range(2):
                    pe.matmul(hist[k][:, 0:NHI], zerob[:, 0:P], zerob[:, :], start=False, stop=True,
                              skip_group_check=True).then_inc(added[k], 1)
                pe.wait_ge(table_step, 3)
                pe.matmul(work[0][:, 0:2], earlier[:, :], total[:, :], start=True, stop=True).then_inc(sums_done, 1)

        away = w.one("away", [P, 2, TILES])
        step = w.sem("record_step")
        with nc.Block() as block:
            @block.vector
            def _(dve):
                v = nc.vector
                field = lambda f: e.own[:, :, f]
                v.tensor_scalar(away[:, :, :], rank[:, :, :], 0.0, None, ALU.is_gt).then_inc(step, 1)
                dve.wait_ge(step, 1)
                v.scalar_tensor_tensor(field(R_WRITE_DST), away[:, BY_DST, :], FAR, keyf[:, BY_DST, :], ALU.mult, ALU.add).then_inc(step, 1)
                v.scalar_tensor_tensor(e.write_src[:, :], away[:, BY_SRC, :], FAR, keyf[:, BY_SRC, :], ALU.mult, ALU.add).then_inc(step, 1)
                v.tensor_scalar(field(R_SRC), keyf[:, BY_SRC, :], float(N_NODES - 1), None, ALU.min).then_inc(step, 1)
                v.tensor_scalar(field(R_DST), keyf[:, BY_DST, :], float(N_NODES - 1), None, ALU.min).then_inc(step, 1)
                v.tensor_scalar(field(R_EDGE), edge[:, :], float(N_EDGES - 1), None, ALU.min).then_inc(step, 1)
                for f, values in ((R_WEIGHT, weight[:, :]), (R_SRC_KEY, keyf[:, BY_SRC, :]), (R_DST_KEY, keyf[:, BY_DST, :])):
                    v.tensor_copy(e.own[:, :, f].bitcast(F32), values).then_inc(step, 1)


class Records:
    MADE = ["own", "starts", "places", "away", "place", "write"]

    def __init__(self, nc, w, c, d, e):
        self.nc, self.c, self.d, self.e = nc, c, d, e
        self.near = w.sb("near", [P, 4], I32)
        self.point, self.spot = w.sb("point", [P, 2], I32), w.sb("spot", [P, 2], I32)
        self.sent = w.sb("sent", [P, FIELDS], I32)
        self.away = w.sb("away", [P, 1])
        self.pointed, self.fetched, self.made, self.written = (w.sems(s) for s in ("pointed", "fetched", "made", "written"))

    def look_up(self, pool):
        def go(l, j):
            if again(j):
                pool.wait_ge(self.fetched[l], 32 * j)
            pool.tensor_copy(self.point[l][:, :], tile_of_two(self.e.entry, DENSE_AT(l, j))).then_inc(self.pointed[l], 1)
            pool.wait_ge(self.pointed[l], j + 1)
            if again(j):
                pool.wait_ge(self.made[l], count(self.MADE, j - 1, "write"))
            for k in range(2):
                gather(pool, self.near[l][:, 2 * k:2 * k + 2], self.d["starts"], self.point[l][:, k:k + 1], self.c.bound[P * NHI - 1])\
                    .then_inc(self.fetched[l], 16)
        return go

    def make(self, dve):
        v = self.nc.vector

        def go(l, j):
            near, sent, spot, made = self.near[l], self.sent[l], self.spot[l], self.made[l]
            dve.wait_ge(self.fetched[l], 32 * (j + 1))
            if again(j):
                dve.wait_ge(self.written[l], 32 * j)
            v.tensor_copy(sent[:, 0:OWN_FIELDS], one_of(self.e.own, DENSE_AT(l, j))).then_inc(made, 1)
            v.tensor_copy(sent[:, R_DST_OUT:R_SRC_OUT + 1], near[:, 1:4]).then_inc(made, 1)
            v.tensor_tensor(spot[:, :], near[:, 0:4:3], tile_of_two(self.e.rank, DENSE_AT(l, j)), ALU.add).then_inc(made, 1)
            v.tensor_scalar(self.away[l][:, :], near[:, 2:3], float(SLOTS), FAR, ALU.is_lt, ALU.mult).then_inc(made, 1)
            dve.wait_ge(made, count(self.MADE, j, "places"))
            v.tensor_copy(sent[:, R_PLACE:R_PLACE + 1], spot[:, 0:1]).then_inc(made, 1)
            dve.wait_ge(made, count(self.MADE, j, "away"))
            v.tensor_tensor(sent[:, R_WRITE_SRC:R_WRITE_SRC + 1], self.away[l][:, :], column(self.e.write_src, DENSE_AT(l, j)), ALU.max)\
                .then_inc(made, 1)
        return go

    def send(self, pool):
        def go(l, j):
            pool.wait_ge(self.made[l], count(self.MADE, j, "write"))
            for k, name in ((BY_DST, "by_dst"), (BY_SRC, "by_src")):
                scatter(pool, self.d[name], self.spot[l][:, k:k + 1], self.sent[l][:, :], self.c.bound[SLOTS - 1]).then_inc(self.written[l], 16)
        return go

    def finish(self, pool):
        for l in range(DENSE_LANES):
            pool.wait_ge(self.written[l], 32 * ROUNDS)


def allocate_order(nc, ctx):
    e = Chip()
    e.entry = ctx.enter_context(nc.sbuf_tensor("entry", [P, 2, TILES], I32))
    e.rank = ctx.enter_context(nc.sbuf_tensor("rank", [P, 2, TILES], F32))
    e.own = ctx.enter_context(nc.sbuf_tensor("own_fields", [P, TILES, OWN_FIELDS], I32))
    e.write_src = ctx.enter_context(nc.sbuf_tensor("write_src", [P, TILES], F32))
    return e


def allocate_edges(nc, ctx, c):
    def sb(name, shape, dt=F32):
        return ctx.enter_context(nc.sbuf_tensor(name, shape, dt))

    c.rec = [sb("rec_by_dst", [P, TILES, FIELDS], I32), sb("rec_by_src", [P, TILES, FIELDS], I32)]
    c.key = [sb("key_by_dst", [P, TILES]), sb("key_by_src", [P, TILES])]
    c.meets = [[sb(f"meets_{e}_{k}", [TILES, TILES]) for e in ("before", "after")] for k in range(2)]
    c.inv = [[sb(f"inv_{n}_{k}", [P, TILES]) for n in ("count", "weight")] for k in range(2)]
    c.state = sb("state", [P, TILES, 2, D])


def phase_keys(nc, c, d):
    with ExitStack() as ctx:
        w = Work(nc, ctx, "keys")
        turned = w.sb("turned", [TILES, P])
        inside = [w.one(f"inside{k}", [TILES, 2, P]) for k in range(2)]
        diagonal = [[w.one(f"diagonal{k}{e}", [TILES, TILES]) for e in range(2)] for k in range(2)]
        ones = w.one("ones", [TILES, TILES])
        near = [w.one("near_before", [TILES, TILES]), w.one("near_after", [TILES, TILES])]
        banks = w.banks("bank")
        zeros = w.one("zeros", [P, D])
        loaded, taken, turns, copied, stored, made, marked, spread, met = (w.sem(s) for s in (
            "loaded", "taken", "turns", "copied", "stored", "made", "marked", "spread", "met"))
        with nc.Block() as block:
            @block.sync
            def _(sp):
                for k, name in ((BY_DST, "by_dst"), (BY_SRC, "by_src")):
                    sp.dma_start(c.rec[k][:, :, :], d[name].rearrange("(t p) f -> p t f", p=P)).then_inc(loaded, 16)
                sp.wait_ge(made, 4)
                for name in ("into", "from"):
                    sp.dma_start(d[name][SLOTS:SLOTS + P], zeros[:, :]).then_inc(stored, 16)
                sp.wait_ge(copied, 2)
                for k in range(2):
                    sp.dma_start(d["key_rows"][k].rearrange("(t p) -> t p", p=P), turned[k][:, :]).then_inc(stored, 16)
                sp.wait_ge(marked, 8)
                for k in range(2):
                    sp.dma_start(d["inside"][k].rearrange("e (t p) -> t e p", p=P), inside[k][:, :, :]).then_inc(stored, 16)
                sp.wait_ge(stored, 96)

            @block.gpsimd
            def _(pool):
                pool.memset(zeros[:, :], 0.0).then_inc(made, 1)
                pool.memset(ones[:, :], 1.0).then_inc(made, 1)
                for m in near:
                    pool.memset(m[:, :], 1.0).then_inc(made, 1)
                pool.wait_ge(made, 4)
                for m, s in zip(near, (-1, 1)):
                    pool.affine_select(out=m[:, :], in_=m[:, :], compare_op=ALU.is_gt, fill=0.0, base=0,
                                       pattern=[[-s, TILES]], channel_multiplier=s).then_inc(made, 1)

            @block.vector
            def _(dve):
                dve.wait_ge(loaded, 32)
                for k, f in ((BY_DST, R_DST_KEY), (BY_SRC, R_SRC_KEY)):
                    nc.vector.tensor_copy(c.key[k][:, :], c.rec[k][:, :, f].bitcast(F32)).then_inc(taken, 1)
                dve.wait_ge(copied, 2)
                for k in range(2):
                    for e, at in ((0, 0), (1, P - 1)):
                        edge = turned[k][:, at:at + 1]
                        nc.vector.tensor_scalar(inside[k][:, e, :], turned[k][:, :], edge, None, ALU.is_equal).then_inc(marked, 1)
                        nc.vector.tensor_scalar(diagonal[k][e][:, :], c.ident[0:TILES, 0:TILES], edge, None, ALU.mult).then_inc(marked, 1)
                dve.wait_ge(made, 6)
                for k in range(2):
                    dve.wait_ge(spread, 2 * (k + 1))
                    for e, at in ((0, P - 1), (1, 0)):
                        nc.vector.scalar_tensor_tensor(c.meets[k][e][:, :], banks[2 * k + e][0:TILES, 0:TILES], turned[k][:, at:at + 1],
                                                       near[e][:, :], ALU.is_equal, ALU.mult).then_inc(met, 1)

            @block.tensor
            def _(pe):
                pe.wait_ge(taken, 2)
                for k in range(2):
                    pe.transpose(banks[k][0:TILES, 0:P], c.key[k][:, :], c.ident[:, :]).then_inc(turns, 1)
                pe.wait_ge(made, 6)
                pe.wait_ge(marked, 8)
                for k in range(2):
                    for e in range(2):
                        pe.matmul(banks[2 * k + e][0:TILES, 0:TILES], ones[:, :], diagonal[k][e][:, :], start=True, stop=True)\
                            .then_inc(spread, 1)

            @block.scalar
            def _(act):
                for k in range(2):
                    act.wait_ge(turns, k + 1)
                    nc.scalar.activation(turned[k][:, :], banks[k][0:TILES, 0:P], ACT.Copy).then_inc(copied, 1)


SET = 4
SUM_LANES = 5
SUM_ROUNDS = TILES // (SET * SUM_LANES)


def set_rows(table, g):
    rows = table[g * SET * P:(g + 1) * SET * P] if isinstance(g, int) else table[bass.ds(g * (SET * P), SET * P)]
    return rows.rearrange("(u p) d -> p u d", p=P)


def set_of(t, g):
    return t[:, g * SET:(g + 1) * SET] if isinstance(g, int) else t[:, bass.ds(g * SET, SET)]


def phase_sum(nc, c, d, tag, order, source, width, inv, target):
    gathered = source is not None and source[1] is not None
    with ExitStack() as ctx:
        w = Work(nc, ctx, tag, SUM_LANES)
        sums = w.one("sums", [P, TILES, width])
        ends = [w.one(f"ends{e}", [TILES, width]) for e in range(2)]
        msg = w.sb("msg", [P, SET, width])
        keys = w.sb("keys", [P, SET, P])
        index = w.sb("index", [P, SET], I32)
        bank = w.banks("bank")
        ends_moved, joined_made, joined_copied = w.sem("ends_moved"), w.sem("joined_made"), w.sem("joined_copied")
        AT = lambda l, j: SUM_LANES * j + l
        key_row = d["key_rows"][order]

        def row_of(g):
            r = key_row[g * SET * P:(g + 1) * SET * P] if isinstance(g, int) else key_row[bass.ds(g * (SET * P), SET * P)]
            return r.partition_broadcast(P)

        loaded, got, pointed = w.sems("loaded"), w.sems("got"), w.sems("pointed")
        compared, multiplied, kept = w.sems("compared"), w.sems("multiplied"), w.sems("kept")
        STAGES = ["load", "", "compare", "multiply", "keep"]
        per = 1 if gathered or source is None else 2
        with nc.Block() as block:
            @block.sync
            def _(sp):
                def load(l, j):
                    if again(j):
                        sp.wait_ge(multiplied[l], j)
                    sp.dma_start(keys[l][:, :, :].rearrange("p u e -> p (u e)"), row_of(AT(l, j))).then_inc(loaded[l], 16)
                    if per == 2:
                        sp.dma_start(msg[l][:, :, :], set_rows(source[0], AT(l, j))).then_inc(loaded[l], 16)

                rounds(sp, STAGES, {"load": load}, SUM_ROUNDS, SUM_LANES)

            if gathered:
                @block.gpsimd
                def _(pool):
                    def fetch(l, j):
                        if again(j):
                            pool.wait_ge(multiplied[l], j)
                        pool.tensor_copy(index[l][:, :], set_of(c.rec[order], AT(l, j))[:, :, source[1]]).then_inc(pointed[l], 1)
                        pool.wait_ge(pointed[l], j + 1)
                        for u in range(SET):
                            gather(pool, msg[l][:, u, :], source[0], index[l][:, u:u + 1], c.bound[SLOTS - 1]).then_inc(got[l], 16)

                    rounds(pool, STAGES, {"load": fetch}, SUM_ROUNDS, SUM_LANES)

            @block.vector
            def _(dve):
                def compare(l, j):
                    dve.wait_ge(loaded[l], 16 * per * (j + 1))
                    mine = set_of(c.key[order], AT(l, j))
                    for u in range(SET):
                        last = nc.vector.tensor_scalar(keys[l][:, u, :], keys[l][:, u, :], mine[:, u:u + 1], None,
                                                       ALU.is_equal)
                    if source is None:
                        nc.vector.memset(msg[l][:, :, 0], 1.0)
                        last = nc.vector.tensor_copy(msg[l][:, :, 1], set_of(c.rec[order], AT(l, j))[:, :, R_WEIGHT].bitcast(F32))
                    last.then_inc(compared[l], 1)

                rounds(dve, STAGES, {"compare": compare}, SUM_ROUNDS, SUM_LANES)

            @block.tensor
            def _(pe):
                def multiply(l, j):
                    pe.wait_ge(compared[l], j + 1)
                    if gathered:
                        pe.wait_ge(got[l], 16 * SET * (j + 1))
                    if again(j):
                        pe.wait_ge(kept[l], j)
                    for u in range(SET):
                        last = pe.matmul(bank[l][:, u * width:(u + 1) * width], keys[l][:, u, :], msg[l][:, u, :], start=True, stop=True)
                    last.then_inc(multiplied[l], 1)

                rounds(pe, STAGES, {"multiply": multiply}, SUM_ROUNDS, SUM_LANES)

            @block.scalar
            def _(act):
                def keep(l, j):
                    act.wait_ge(multiplied[l], j + 1)
                    into = set_of(sums, AT(l, j))
                    if inv is None:
                        last = nc.scalar.activation(into, bank[l][:, 0:SET * width].rearrange("p (u d) -> p u d", u=SET), ACT.Copy)
                    else:
                        scale = set_of(inv, AT(l, j))
                        for u in range(SET):
                            last = nc.scalar.activation(into[:, u, :], bank[l][:, u * width:(u + 1) * width], ACT.Copy,
                                                        scale=scale[:, u:u + 1])
                    last.then_inc(kept[l], 1)

                rounds(act, STAGES, {"keep": keep}, SUM_ROUNDS, SUM_LANES)

        carried = msg[0][0:TILES, 0:2, :]
        carry_dram = d["carried2" if width == 2 else "carried"]
        with nc.Block() as block:
            @block.sync
            def _(sp):
                for e, at in ((0, 0), (1, P - 1)):
                    sp.dma_start(ends[e][:, :], sums[at:at + 1, :, :].rearrange("a t d -> a (t d)")).then_inc(ends_moved, 16)
                sp.wait_ge(joined_copied, 1)
                sp.dma_start(carry_dram.rearrange("e (t d) -> t e d", t=TILES), carried).then_inc(ends_moved, 16)
                sp.wait_ge(ends_moved, 48)

            @block.tensor
            def _(pe):
                pe.wait_ge(ends_moved, 32)
                for e in range(2):
                    last = pe.matmul(bank[0][0:TILES, e * width:(e + 1) * width], c.meets[order][e][:, :], ends[1 - e][:, :],
                                     start=True, stop=True)
                last.then_inc(joined_made, 1)

            @block.scalar
            def _(act):
                act.wait_ge(joined_made, 1)
                nc.scalar.activation(carried, bank[0][0:TILES, 0:2 * width].rearrange("p (e d) -> p e d", e=2), ACT.Copy)\
                    .then_inc(joined_copied, 1)

        loaded, multiplied = w.sems("loaded2"), w.sems("multiplied2")
        summed, owned, stored, pointed = w.sems("summed"), w.sems("owned"), w.sems("stored"), w.sems("pointed2")
        carry = [m[0:2, :, :] for m in msg]
        inside = [k[0:2, :, :] for k in keys]
        result = keys
        STAGES = ["load", "", "multiply", "sum", "store"]
        final = target == "out"
        with nc.Block() as block:
            @block.sync
            def _(sp):
                def columns(t, g, size):
                    return t[:, g * size:(g + 1) * size] if isinstance(g, int) else t[:, bass.ds(g * size, size)]

                def load(l, j):
                    if again(j) and final:
                        sp.wait_ge(stored[l], 16 * SET * j)
                    elif again(j):
                        sp.wait_ge(multiplied[l], j)
                    sp.dma_start(inside[l][:, :, :].rearrange("e u p -> e (u p)"), columns(d["inside"][order], AT(l, j), SET * P))\
                        .then_inc(loaded[l], 16)
                    sp.dma_start(carry[l][:, :, :].rearrange("e u d -> e (u d)"), columns(carry_dram, AT(l, j), SET * width))\
                        .then_inc(loaded[l], 16)

                def store(l, j):
                    if target in ("into", "from"):
                        sp.wait_ge(summed[l], j + 1)
                        sp.dma_start(set_rows(d[target], AT(l, j)), set_of(sums, AT(l, j))).then_inc(stored[l], 16)

                rounds(sp, STAGES, {"load": load, "store": store}, SUM_ROUNDS, SUM_LANES)
                if target in ("into", "from"):
                    for l in range(SUM_LANES):
                        sp.wait_ge(stored[l], 16 * SUM_ROUNDS)

            @block.vector
            def _(dve):
                def add(l, j):
                    dve.wait_ge(multiplied[l], j + 1)
                    out = result[l][:, :, :] if final else set_of(sums if isinstance(target, str) else target, AT(l, j))
                    nc.vector.tensor_tensor(out, bank[l][:, 0:SET * width].rearrange("p (u d) -> p u d", u=SET), set_of(sums, AT(l, j)),
                                            ALU.add).then_inc(summed[l], 1)
                    if final:
                        dve.wait_ge(summed[l], j + 1)
                        own = c.state[:, AT(l, j) * SET:(AT(l, j) + 1) * SET, 1, :] if isinstance(j, int) else \
                            c.state[:, bass.ds(AT(l, j) * SET, SET), 1, :]
                        nc.vector.tensor_tensor(result[l][:, :, :], result[l][:, :, :], own, ALU.add).then_inc(owned[l], 1)

                rounds(dve, STAGES, {"sum": add}, SUM_ROUNDS, SUM_LANES)

            @block.tensor
            def _(pe):
                def multiply(l, j):
                    pe.wait_ge(loaded[l], 32 * (j + 1))
                    if again(j):
                        pe.wait_ge(summed[l], j)
                    for u in range(SET):
                        last = pe.matmul(bank[l][:, u * width:(u + 1) * width], inside[l][:, u, :], carry[l][:, u, :], start=True, stop=True)
                    last.then_inc(multiplied[l], 1)

                rounds(pe, STAGES, {"multiply": multiply}, SUM_ROUNDS, SUM_LANES)

            if final:
                @block.gpsimd
                def _(pool):
                    def store(l, j):
                        if again(j):
                            pool.wait_ge(stored[l], 16 * SET * j)
                        pool.tensor_copy(index[l][:, :], set_of(c.rec[order], AT(l, j))[:, :, R_WRITE_DST]).then_inc(pointed[l], 1)
                        pool.wait_ge(pointed[l], j + 1)
                        pool.wait_ge(owned[l], j + 1)
                        for u in range(SET):
                            scatter(pool, d["out"], index[l][:, u:u + 1], result[l][:, u, :], c.bound[N_NODES - 1])\
                                .then_inc(stored[l], 16)

                    rounds(pool, STAGES, {"store": store}, SUM_ROUNDS, SUM_LANES)
                    for l in range(SUM_LANES):
                        pool.wait_ge(stored[l], 16 * SET * SUM_ROUNDS)


def phase_degrees(nc, c, d):
    with ExitStack() as outer:
        totals = [outer.enter_context(nc.sbuf_tensor(f"totals{k}", [P, TILES, 2], F32)) for k in range(2)]
        for k in range(2):
            phase_sum(nc, c, d, f"deg{k}", k, None, 2, None, totals[k])
        with ExitStack() as ctx:
            w = Work(nc, ctx, "degrees")
            present, safe, counted = (w.one(s, [P, TILES]) for s in ("present", "safe", "counted"))
            step = w.sem("step")
            with nc.Block() as block:
                @block.vector
                def _(dve):
                    v = nc.vector
                    for k in range(2):
                        base = 7 * k
                        if k:
                            dve.wait_ge(step, base)
                        v.tensor_scalar(counted[:, :], totals[k][:, :, 0], 1.0, None, ALU.max).then_inc(step, 1)
                        v.tensor_scalar(present[:, :], totals[k][:, :, 1], 0.0, None, ALU.is_gt).then_inc(step, 1)
                        dve.wait_ge(step, base + 2)
                        v.reciprocal(c.inv[k][0][:, :], counted[:, :]).then_inc(step, 1)
                        v.scalar_tensor_tensor(safe[:, :], totals[k][:, :, 1], 1.0, present[:, :], ALU.subtract, ALU.mult).then_inc(step, 1)
                        dve.wait_ge(step, base + 4)
                        v.tensor_scalar(safe[:, :], safe[:, :], 1.0, None, ALU.add).then_inc(step, 1)
                        dve.wait_ge(step, base + 5)
                        v.reciprocal(safe[:, :], safe[:, :]).then_inc(step, 1)
                        dve.wait_ge(step, base + 6)
                        v.tensor_tensor(c.inv[k][1][:, :], safe[:, :], present[:, :], ALU.mult).then_inc(step, 1)


class Norm:

    def __init__(self, w, p, u):
        self.nc, self.p, self.u = w.nc, p, u
        self.stats = w.sb("stats", [p, u, 6])
        self.mv = w.sb("mv", [p, u, 2])
        self.var = w.sb("var", [p, u])
        self.rstd = w.sb("rstd", [p, u])
        self.shift = w.sb("shift", [p, u])
        self.pause = w.one("pause", [p, 1])

    def moments(self, dve, l, src, done, at):
        v = self.nc.vector
        for i in range(self.u):
            last = v.bn_stats(self.stats[l][:, i, :], src[:, i, :])
        last.then_inc(done[l], 1)
        dve.wait_ge(done[l], at("stats"))
        v.memset(self.pause[:, :], 0.0)
        for i in range(self.u):
            last = v.bn_aggr(self.mv[l][:, i, :], self.stats[l][:, i, :])
        last.then_inc(done[l], 1)

    def factor_base(self, dve, l, src, done, at):
        self.moments(dve, l, src, done, at)
        dve.wait_ge(done[l], at("mean"))
        self.variance(l).then_inc(done[l], 1)

    def variance(self, l):
        return self.nc.vector.tensor_scalar(self.var[l][:, :], self.mv[l][:, :, 1], LN_EPS, None, ALU.add)

    def power(self, pool, c, l):
        return pool.tensor_tensor(self.rstd[l][:, :], self.var[l][:, :], c.power[0:self.p, 0:self.u], ALU.pow)

    def move(self, l):
        return self.nc.vector.scalar_tensor_tensor(self.shift[l][:, :], self.mv[l][:, :, 0], -1.0, self.rstd[l][:, :],
                                                   ALU.mult, ALU.mult)

    def apply_here(self, out, src, l):
        for i in range(self.u):
            last = self.nc.vector.tensor_scalar(out[l][:, i, :], src[:, i, :], self.mv[l][:, i, 0:1],
                                                self.rstd[l][:, i:i + 1], ALU.subtract, ALU.mult)
        return last

    def apply(self, out, src, l):
        for i in range(self.u):
            last = self.nc.scalar.activation(out[l][:, i, :], src[l][:, i, :], ACT.Relu, bias=self.shift[l][:, i:i + 1],
                                             scale=self.rstd[l][:, i:i + 1])
        return last


def pair(t, j):
    return t[:, j] if isinstance(j, int) else t[:, bass.ds(j, 1)].rearrange("p a u d -> p (a u) d")


def fields(rec, j, lo, hi):
    return rec[:, j, lo:hi] if isinstance(j, int) else rec[:, bass.ds(j, 1), lo:hi].rearrange("p a f -> p (a f)")


N2 = TILES // LANES
SELF = lambda bank: bank[:, 0:512].rearrange("p (u c) -> p u c", u=2)[:, :, 0:D]
SENT = slice(D, 2 * D)


def turn_pair(pe, c, out, src, l):
    for i in range(2):
        last = pe.transpose(out[:, i * P:(i + 1) * P], src[l][:, i, :], c.ident[:, :])
    return last


def layer_products(pe, bank, hT, both):
    pe.matmul(bank[:, 0:2 * D], hT[:, 0:P], both, start=True, stop=True)
    return pe.matmul(bank[:, 2 * D:3 * D], hT[:, P:2 * P], both[:, 0:D], start=True, stop=True)


def phase_enter(nc, c, d, a):
    DV = ["stats", "mean", "var", "h", "own"]
    PO = ["index", "rstd"]
    AC = ["hT", "message"]
    PE = ["turn", "products"]
    STAGES = ["load", "", "", "norm", "", "rstd", "h", "turn", "hT", "products", "", "own", "store"]
    with ExitStack() as ctx:
        w = Work(nc, ctx, "enter")
        index, x, h, hT, message = w.sb("index", [P, 2], I32), w.sb("x", [P, 2, D]), w.sb("h", [P, 2, D]), w.sb("hT", [P, 2 * P]), w.sb("message", [P, D])
        norm = Norm(w, P, 2)
        left, right = w.banks("left"), w.banks("right")
        loaded, stored, kept = w.sems("loaded"), w.sems("stored"), w.sems("kept")
        pe_done, act_done, dve_done, pool_done = w.sems("pe_done"), w.sems("act_done"), w.sems("dve_done"), w.sems("pool_done")
        with nc.Block() as block:
            @block.gpsimd
            def _(pool):
                def load(l, j):
                    if again(j):
                        pool.wait_ge(loaded[l], 32 * j)
                        pool.wait_ge(dve_done[l], count(DV, j - 1, "h"))
                        pool.wait_ge(kept[l], 16 * j)
                    pool.tensor_copy(index[l][:, :], fields(c.rec[BY_DST], AT(l, j), R_SRC, R_DST + 1)).then_inc(pool_done[l], 1)
                    pool.wait_ge(pool_done[l], count(PO, j, "index"))
                    for i in range(2):
                        gather(pool, x[l][:, i, :], a["x"], index[l][:, i:i + 1], c.bound[N_NODES - 1]).then_inc(loaded[l], 16)

                def factors(l, j):
                    pool.wait_ge(dve_done[l], count(DV, j, "var"))
                    norm.power(pool, c, l).then_inc(pool_done[l], 1)

                rounds(pool, STAGES, {"load": load, "rstd": factors}, N2)

            @block.sync
            def _(sp):
                def keep(l, j):
                    sp.wait_ge(loaded[l], 32 * (j + 1))
                    sp.dma_start(tile_rows(d["kept"], AT(l, j)), x[l][:, :, :]).then_inc(kept[l], 16)

                def store(l, j):
                    sp.wait_ge(act_done[l], count(AC, j, "message"))
                    sp.dma_start(tile_rows(d["message"], AT(l, j)), message[l][:, :]).then_inc(stored[l], 16)

                rounds(sp, STAGES, {"norm": keep, "store": store}, N2)
                for l in range(LANES):
                    sp.wait_ge(stored[l], 16 * N2)
                    sp.wait_ge(kept[l], 16 * N2)

            @block.vector
            def _(dve):
                def moments(l, j):
                    dve.wait_ge(loaded[l], 32 * (j + 1))
                    norm.factor_base(dve, l, x[l], dve_done, lambda s: count(DV, j, s))

                def apply(l, j):
                    dve.wait_ge(pool_done[l], count(PO, j, "rstd"))
                    if again(j):
                        dve.wait_ge(pe_done[l], count(PE, j - 1, "turn"))
                    norm.apply_here(h, x[l], l).then_inc(dve_done[l], 1)

                def own(l, j):
                    dve.wait_ge(pe_done[l], count(PE, j, "products"))
                    dve.wait_ge(act_done[l], count(AC, j, "message"))
                    nc.vector.tensor_tensor(pair(c.state, AT(l, j)), SELF(right[l]), bc(c.bias[:, B_L0, :], 2), ALU.add)\
                        .then_inc(dve_done[l], 1)

                rounds(dve, STAGES, {"norm": moments, "h": apply, "own": own}, N2)

            @block.scalar
            def _(act):
                def relu(l, j):
                    act.wait_ge(pe_done[l], count(PE, j, "turn"))
                    nc.scalar.activation(hT[l][:, :], left[l][:, 0:2 * P], ACT.Relu).then_inc(act_done[l], 1)

                def send(l, j):
                    act.wait_ge(pe_done[l], count(PE, j, "products"))
                    if again(j):
                        act.wait_ge(stored[l], 16 * j)
                    nc.scalar.activation(message[l][:, :], right[l][:, SENT], ACT.Copy).then_inc(act_done[l], 1)

                rounds(act, STAGES, {"hT": relu, "own": send}, N2)

            @block.tensor
            def _(pe):
                def turn(l, j):
                    pe.wait_ge(dve_done[l], count(DV, j, "h"))
                    if again(j):
                        pe.wait_ge(act_done[l], count(AC, j - 1, "hT"))
                    turn_pair(pe, c, left[l], h, l).then_inc(pe_done[l], 1)

                def products(l, j):
                    pe.wait_ge(act_done[l], count(AC, j, "hT"))
                    if again(j):
                        pe.wait_ge(dve_done[l], count(DV, j - 1, "own"))
                    layer_products(pe, right[l], hT[l], c.wrT[:, 0, :]).then_inc(pe_done[l], 1)

                rounds(pe, STAGES, {"turn": turn, "products": products}, N2)


def phase_layer(nc, c, d, layer):
    DV = ["sum", "own"]
    AC = ["hT", "message"]
    PE = ["turn", "products"]
    STAGES = ["load", "sum", "", "turn", "hT", "products", "own", "", "", "store"]
    with ExitStack() as ctx:
        w = Work(nc, ctx, f"layer{layer}")
        index, near, s, hT, message = w.sb("index", [P, 1], I32), w.sb("near", [P, 2, D]), w.sb("s", [P, 2, D]), w.sb("hT", [P, 2 * P]), w.sb("message", [P, D])
        left, right = w.banks("left"), w.banks("right")
        loaded, gathered, stored, pointed = w.sems("loaded"), w.sems("gathered"), w.sems("stored"), w.sems("pointed")
        pe_done, act_done, dve_done = w.sems("pe_done"), w.sems("act_done"), w.sems("dve_done")
        with nc.Block() as block:
            @block.gpsimd
            def _(pool):
                def load(l, j):
                    if again(j):
                        pool.wait_ge(gathered[l], 16 * j)
                        pool.wait_ge(dve_done[l], count(DV, j - 1, "sum"))
                    pool.tensor_copy(index[l][:, :], fields(c.rec[BY_DST], AT(l, j), R_SRC_IN, R_SRC_IN + 1)).then_inc(pointed[l], 1)
                    pool.wait_ge(pointed[l], j + 1)
                    gather(pool, near[l][:, 0, :], d["into"], index[l][:, :], c.bound[SLOTS]).then_inc(gathered[l], 16)

                rounds(pool, STAGES, {"load": load}, N2)

            @block.sync
            def _(sp):
                def load(l, j):
                    if again(j):
                        sp.wait_ge(dve_done[l], count(DV, j - 1, "sum"))
                    sp.dma_start(near[l][:, 1, :], tile_rows(d["into"], AT(l, j))).then_inc(loaded[l], 16)

                def store(l, j):
                    sp.wait_ge(act_done[l], count(AC, j, "message"))
                    sp.dma_start(tile_rows(d["message"], AT(l, j)), message[l][:, :]).then_inc(stored[l], 16)

                rounds(sp, STAGES, {"load": load, "store": store}, N2)
                for l in range(LANES):
                    sp.wait_ge(stored[l], 16 * N2)

            @block.vector
            def _(dve):
                def add(l, j):
                    dve.wait_ge(loaded[l], 16 * (j + 1))
                    dve.wait_ge(gathered[l], 16 * (j + 1))
                    if again(j):
                        dve.wait_ge(pe_done[l], count(PE, j - 1, "turn"))
                    nc.vector.tensor_tensor(s[l][:, :, :], near[l][:, :, :], pair(c.state, AT(l, j)), ALU.add).then_inc(dve_done[l], 1)

                def own(l, j):
                    dve.wait_ge(pe_done[l], count(PE, j, "products"))
                    dve.wait_ge(act_done[l], count(AC, j, "message"))
                    nc.vector.tensor_tensor(pair(c.state, AT(l, j)), SELF(right[l]), bc(c.bias[:, B_L0 + layer, :], 2), ALU.add)\
                        .then_inc(dve_done[l], 1)

                rounds(dve, STAGES, {"sum": add, "own": own}, N2)

            @block.scalar
            def _(act):
                def relu(l, j):
                    act.wait_ge(pe_done[l], count(PE, j, "turn"))
                    if again(j):
                        act.wait_ge(pe_done[l], count(PE, j - 1, "products"))
                    nc.scalar.activation(hT[l][:, :], left[l][:, 0:2 * P], ACT.Relu).then_inc(act_done[l], 1)

                def send(l, j):
                    act.wait_ge(pe_done[l], count(PE, j, "products"))
                    if again(j):
                        act.wait_ge(stored[l], 16 * j)
                    nc.scalar.activation(message[l][:, :], right[l][:, SENT], ACT.Copy).then_inc(act_done[l], 1)

                rounds(act, STAGES, {"hT": relu, "own": send}, N2)

            @block.tensor
            def _(pe):
                def turn(l, j):
                    pe.wait_ge(dve_done[l], count(DV, j, "sum"))
                    if again(j):
                        pe.wait_ge(act_done[l], count(AC, j - 1, "hT"))
                    turn_pair(pe, c, left[l], s, l).then_inc(pe_done[l], 1)

                def products(l, j):
                    pe.wait_ge(act_done[l], count(AC, j, "hT"))
                    if again(j):
                        pe.wait_ge(dve_done[l], count(DV, j - 1, "own"))
                    layer_products(pe, right[l], hT[l], c.wrT[:, layer, :]).then_inc(pe_done[l], 1)

                rounds(pe, STAGES, {"turn": turn, "products": products}, N2)


def phase_join(nc, c, d):
    DV = ["x", "stats", "mean", "var", "kept", "shift"]
    PO = ["index", "sum", "rstd"]
    AC = ["h", "message"]
    STAGES = timetable(120, {"load": 0, "sum": 45, "x": 63, "rstd": 82, "shift": 92, "h": 96, "message": 107, "store": 115})
    with ExitStack() as ctx:
        w = Work(nc, ctx, "join")
        index, near, s, x0, x = w.sb("index", [P, 1], I32), w.sb("near", [P, 2, D]), w.sb("s", [P, 2, D]), w.sb("x0", [P, 2, D]), w.sb("x", [P, 2, D])
        h, message = w.sb("h", [P, 2, D]), w.sb("message", [P, 2, D])
        norm = Norm(w, P, 2)
        loaded, gathered, stored = w.sems("loaded"), w.sems("gathered"), w.sems("stored")
        act_done, dve_done, pool_done = w.sems("act_done"), w.sems("dve_done"), w.sems("pool_done")
        with nc.Block() as block:
            @block.gpsimd
            def _(pool):
                def load(l, j):
                    if again(j):
                        pool.wait_ge(gathered[l], 16 * j)
                        pool.wait_ge(dve_done[l], count(DV, j - 1, "x"))
                    pool.tensor_copy(index[l][:, :], fields(c.rec[BY_DST], AT(l, j), R_SRC_IN, R_SRC_IN + 1)).then_inc(pool_done[l], 1)
                    pool.wait_ge(pool_done[l], count(PO, j, "index"))
                    gather(pool, near[l][:, 0, :], d["into"], index[l][:, :], c.bound[SLOTS]).then_inc(gathered[l], 16)

                def add(l, j):
                    pool.wait_ge(loaded[l], 32 * (j + 1))
                    pool.tensor_tensor(s[l][:, :, :], x0[l][:, :, :], pair(c.state, AT(l, j)), ALU.add).then_inc(pool_done[l], 1)

                def factors(l, j):
                    pool.wait_ge(dve_done[l], count(DV, j, "var"))
                    norm.power(pool, c, l).then_inc(pool_done[l], 1)

                rounds(pool, STAGES, {"load": load, "sum": add, "rstd": factors}, N2)

            @block.sync
            def _(sp):
                def load(l, j):
                    if again(j):
                        sp.wait_ge(dve_done[l], count(DV, j - 1, "x"))
                    sp.dma_start(near[l][:, 1, :], tile_rows(d["into"], AT(l, j))).then_inc(loaded[l], 16)
                    sp.dma_start(x0[l][:, :, :], tile_rows(d["kept"], AT(l, j))).then_inc(loaded[l], 16)

                def store(l, j):
                    sp.wait_ge(act_done[l], count(AC, j, "message"))
                    sp.dma_start(tile_rows(d["message"], AT(l, j)), message[l][:, 0, :]).then_inc(stored[l], 16)
                    sp.dma_start(tile_rows(d["reverse"], AT(l, j)), message[l][:, 1, :]).then_inc(stored[l], 16)

                rounds(sp, STAGES, {"load": load, "store": store}, N2)
                for l in range(LANES):
                    sp.wait_ge(stored[l], 32 * N2)

            @block.vector
            def _(dve):
                def add(l, j):
                    dve.wait_ge(loaded[l], 32 * (j + 1))
                    dve.wait_ge(gathered[l], 16 * (j + 1))
                    dve.wait_ge(pool_done[l], count(PO, j, "sum"))
                    if again(j):
                        dve.wait_ge(act_done[l], count(AC, j - 1, "h"))
                    nc.vector.tensor_tensor(x[l][:, :, :], near[l][:, :, :], s[l][:, :, :], ALU.add).then_inc(dve_done[l], 1)
                    dve.wait_ge(dve_done[l], count(DV, j, "x"))
                    norm.factor_base(dve, l, x[l], dve_done, lambda s: count(DV, j, s))
                    nc.vector.tensor_copy(pair(c.state, AT(l, j)), x[l][:, :, :]).then_inc(dve_done[l], 1)

                def shift(l, j):
                    dve.wait_ge(pool_done[l], count(PO, j, "rstd"))
                    norm.move(l).then_inc(dve_done[l], 1)

                rounds(dve, STAGES, {"x": add, "shift": shift}, N2)

            @block.scalar
            def _(act):
                def apply(l, j):
                    act.wait_ge(dve_done[l], count(DV, j, "shift"))
                    norm.apply(h, x, l).then_inc(act_done[l], 1)

                def send(l, j):
                    act.wait_ge(act_done[l], count(AC, j, "h"))
                    if again(j):
                        act.wait_ge(stored[l], 32 * j)
                    nc.scalar.activation(message[l][:, :, :], h[l][:, :, :], ACT.Copy,
                                         scale=fields(c.rec[BY_DST], AT(l, j), R_WEIGHT, R_WEIGHT + 1).bitcast(F32)).then_inc(act_done[l], 1)

                rounds(act, STAGES, {"h": apply, "message": send}, N2)


def phase_edges(nc, c, d, a):
    DV = ["filter", "product"]
    AC = ["eT", "tanh"]
    PE = ["turn", "products"]
    STAGES = ["load", "", "turn", "eT", "", "products", "tanh", "filter", "store"]
    with ExitStack() as ctx:
        w = Work(nc, ctx, "edges")
        index, e, eT, g, f = w.sb("index", [P, 1], I32), w.sb("e", [P, D]), w.sb("eT", [P, P]), w.sb("g", [P, D]), w.sb("f", [P, D])
        left, right = w.banks("left"), w.banks("right")
        gathered, stored, pointed = w.sems("gathered"), w.sems("stored"), w.sems("pointed")
        pe_done, act_done, dve_done = w.sems("pe_done"), w.sems("act_done"), w.sems("dve_done")
        with nc.Block() as block:
            @block.gpsimd
            def _(pool):
                def load(l, j):
                    if again(j):
                        pool.wait_ge(gathered[l], 16 * j)
                        pool.wait_ge(pe_done[l], count(PE, j - 1, "turn"))
                    pool.tensor_copy(index[l][:, :], fields(c.rec[BY_DST], AT(l, j), R_EDGE, R_EDGE + 1)).then_inc(pointed[l], 1)
                    pool.wait_ge(pointed[l], j + 1)
                    gather(pool, e[l][:, :], a["edge_attr_128"], index[l][:, :], c.bound[N_EDGES - 1]).then_inc(gathered[l], 16)

                rounds(pool, STAGES, {"load": load}, N2)

            @block.sync
            def _(sp):
                def store(l, j):
                    sp.wait_ge(dve_done[l], count(DV, j, "product"))
                    sp.dma_start(tile_rows(d["filter"], AT(l, j)), f[l][:, :]).then_inc(stored[l], 16)

                rounds(sp, STAGES, {"store": store}, N2)
                for l in range(LANES):
                    sp.wait_ge(stored[l], 16 * N2)

            @block.vector
            def _(dve):
                def go(l, j):
                    dve.wait_ge(act_done[l], count(AC, j, "tanh"))
                    if again(j):
                        dve.wait_ge(stored[l], 16 * j)
                    nc.vector.scalar_tensor_tensor(f[l][:, :], g[l][:, :], 1.0, right[l][:, D:2 * D], ALU.add, ALU.mult)\
                        .then_inc(dve_done[l], 1)
                    dve.wait_ge(dve_done[l], count(DV, j, "filter"))
                    nc.vector.tensor_scalar(f[l][:, :], f[l][:, :], 0.5, None, ALU.mult).then_inc(dve_done[l], 1)

                rounds(dve, STAGES, {"filter": go}, N2)

            @block.scalar
            def _(act):
                def copy(l, j):
                    act.wait_ge(pe_done[l], count(PE, j, "turn"))
                    nc.scalar.activation(eT[l][:, :], left[l][:, 0:P], ACT.Copy).then_inc(act_done[l], 1)

                def tanh(l, j):
                    act.wait_ge(pe_done[l], count(PE, j, "products"))
                    if again(j):
                        act.wait_ge(dve_done[l], count(DV, j - 1, "filter"))
                    nc.scalar.activation(g[l][:, :], right[l][:, 0:D], ACT.Tanh, scale=0.5).then_inc(act_done[l], 1)

                rounds(act, STAGES, {"eT": copy, "tanh": tanh}, N2)

            @block.tensor
            def _(pe):
                def turn(l, j):
                    pe.wait_ge(gathered[l], 16 * (j + 1))
                    if again(j):
                        pe.wait_ge(act_done[l], count(AC, j - 1, "eT"))
                    pe.transpose(left[l][:, 0:P], e[l][:, :], c.ident[:, :]).then_inc(pe_done[l], 1)

                def products(l, j):
                    pe.wait_ge(act_done[l], count(AC, j, "eT"))
                    if again(j):
                        pe.wait_ge(dve_done[l], count(DV, j - 1, "filter"))
                    o = right[l][:, 0:2 * D]
                    pe.matmul(o, c.ones3[:, :], c.bias3[:, B_GATE:B_FILT + 1, :].rearrange("a b d -> a (b d)"), start=True, stop=False)
                    pe.matmul(o, eT[l][:, :], c.wgf[:, :, :].rearrange("p g d -> p (g d)"), start=False, stop=True)\
                        .then_inc(pe_done[l], 1)

                rounds(pe, STAGES, {"turn": turn, "products": products}, N2)


def phase_gru(nc, c, d):
    DV = ["stats1", "mean1", "var1", "h", "r hn src", "r hn dst", "n in src", "n in dst", "h - n", "z mix", "x", "stats2", "mean2",
          "var2", "h5", "own", "message"]
    PO = ["index", "rstd1", "n + x1", "rstd2"]
    AC = ["hT", "intoT", "outT", "rz src", "rz dst", "n", "h5T"]
    PE = ["turn h", "turn out", "gates src", "gates dst", "turn h5", "node"]
    STAGES = ["load", "", "norm1", "rstd1", "h", "turn h", "hT", "gates src", "", "gates dst", "", "rz", "n in", "n", "",
              "mix", "norm2", "rstd2", "h5", "turn h5", "h5T", "node", "", "own", "store"]
    with ExitStack() as ctx:
        w = Work(nc, ctx, "gru")
        index = w.sb("index", [P, 3], I32)
        h, h5 = w.sb("h", [P, 2, D]), w.sb("h5", [P, 2, D])
        into, out = w.sb("into", [P, 2, D]), w.sb("out", [P, 2, D])
        hT, outT = w.sb("hT", [P, 4 * P]), w.sb("outT", [P, 2 * P])
        rz = w.sb("rz", [P, 2, 2 * D])
        u, n, apart, both, own = (w.sb(s, [P, 2, D]) for s in ("u", "n", "apart", "both", "own"))
        filt, message = w.sb("filt", [P, 1, D]), w.sb("message", [P, 1, D])
        norm = Norm(w, P, 2)
        left, right = w.banks("left"), w.banks("right")
        loaded, gathered, stored = w.sems("loaded"), w.sems("gathered"), w.sems("stored")
        pe_done, act_done, dve_done, pool_done = w.sems("pe_done"), w.sems("act_done"), w.sems("dve_done"), w.sems("pool_done")
        with nc.Block() as block:
            @block.gpsimd
            def _(pool):
                def load(l, j):
                    if again(j):
                        pool.wait_ge(gathered[l], 48 * j)
                        pool.wait_ge(pe_done[l], count(PE, j - 1, "turn out"))
                    pool.tensor_copy(index[l][:, :], fields(c.rec[BY_DST], AT(l, j), R_DST_OUT, R_SRC_OUT + 1)).then_inc(pool_done[l], 1)
                    pool.wait_ge(pool_done[l], count(PO, j, "index"))
                    gather(pool, into[l][:, 0, :], d["into"], index[l][:, 1:2], c.bound[SLOTS]).then_inc(gathered[l], 16)
                    gather(pool, out[l][:, 0, :], d["from"], index[l][:, 2:3], c.bound[SLOTS]).then_inc(gathered[l], 16)
                    gather(pool, out[l][:, 1, :], d["from"], index[l][:, 0:1], c.bound[SLOTS]).then_inc(gathered[l], 16)

                def factors(k):
                    def go(l, j):
                        pool.wait_ge(dve_done[l], count(DV, j, "var" + k))
                        norm.power(pool, c, l).then_inc(pool_done[l], 1)
                    return go

                def mix(l, j):
                    pool.wait_ge(act_done[l], count(AC, j, "n"))
                    if again(j):
                        pool.wait_ge(dve_done[l], count(DV, j - 1, "x"))
                    pool.tensor_tensor(both[l][:, :, :], n[l][:, :, :], pair(c.state, AT(l, j)), ALU.add).then_inc(pool_done[l], 1)

                rounds(pool, STAGES, {"load": load, "rstd1": factors("1"), "rstd2": factors("2"), "mix": mix}, N2)

            @block.sync
            def _(sp):
                def load(l, j):
                    if again(j):
                        sp.wait_ge(pe_done[l], count(PE, j - 1, "turn h"))
                        sp.wait_ge(dve_done[l], count(DV, j - 1, "message"))
                    sp.dma_start(into[l][:, 1, :], tile_rows(d["into"], AT(l, j))).then_inc(loaded[l], 16)
                    sp.dma_start(filt[l][:, 0, :], tile_rows(d["filter"], AT(l, j))).then_inc(loaded[l], 16)

                def store(l, j):
                    sp.wait_ge(dve_done[l], count(DV, j, "message"))
                    sp.dma_start(tile_rows(d["kept"], AT(l, j)), own[l][:, :, :]).then_inc(stored[l], 16)
                    sp.dma_start(tile_rows(d["reverse"], AT(l, j)), message[l][:, 0, :]).then_inc(stored[l], 16)

                rounds(sp, STAGES, {"load": load, "store": store}, N2)
                for l in range(LANES):
                    sp.wait_ge(stored[l], 32 * N2)

            @block.vector
            def _(dve):
                def norm1(l, j):
                    norm.factor_base(dve, l, pair(c.state, AT(l, j)), dve_done, lambda s: count(DV, j, s + "1"))

                def apply1(l, j):
                    dve.wait_ge(pool_done[l], count(PO, j, "rstd1"))
                    if again(j):
                        dve.wait_ge(pe_done[l], count(PE, j - 1, "turn h"))
                    norm.apply_here(h, pair(c.state, AT(l, j)), l).then_inc(dve_done[l], 1)

                def n_in(l, j):
                    dve.wait_ge(act_done[l], count(AC, j, "rz dst"))
                    for i, bank in enumerate((left, right)):
                        nc.vector.scalar_tensor_tensor(u[l][:, i, :], rz[l][:, i, 0:D], 1.0, bank[l][:, 0:D], ALU.add, ALU.mult)\
                            .then_inc(dve_done[l], 1)
                    dve.wait_ge(dve_done[l], count(DV, j, "r hn dst"))
                    for i, bank in enumerate((left, right)):
                        nc.vector.scalar_tensor_tensor(u[l][:, i, :], u[l][:, i, :], 0.5, bank[l][:, 3 * D:4 * D], ALU.mult, ALU.add)\
                            .then_inc(dve_done[l], 1)

                def norm2(l, j):
                    dve.wait_ge(act_done[l], count(AC, j, "n"))
                    nc.vector.scalar_tensor_tensor(apart[l][:, :, :], h[l][:, :, :], 0.0, n[l][:, :, :], ALU.max, ALU.subtract)\
                        .then_inc(dve_done[l], 1)
                    dve.wait_ge(dve_done[l], count(DV, j, "h - n"))
                    nc.vector.scalar_tensor_tensor(u[l][:, :, :], rz[l][:, :, D:2 * D], 1.0, apart[l][:, :, :], ALU.add, ALU.mult)\
                        .then_inc(dve_done[l], 1)
                    dve.wait_ge(dve_done[l], count(DV, j, "z mix"))
                    dve.wait_ge(pool_done[l], count(PO, j, "n + x1"))
                    nc.vector.scalar_tensor_tensor(pair(c.state, AT(l, j)), u[l][:, :, :], 0.5, both[l][:, :, :], ALU.mult, ALU.add)\
                        .then_inc(dve_done[l], 1)
                    dve.wait_ge(dve_done[l], count(DV, j, "x"))
                    nc.vector.memset(norm.pause[:, :], 0.0)
                    norm.factor_base(dve, l, pair(c.state, AT(l, j)), dve_done, lambda s: count(DV, j, s + "2"))

                def apply2(l, j):
                    dve.wait_ge(pool_done[l], count(PO, j, "rstd2"))
                    norm.apply_here(h5, pair(c.state, AT(l, j)), l).then_inc(dve_done[l], 1)

                def node(l, j):
                    dve.wait_ge(pe_done[l], count(PE, j, "node"))
                    dve.wait_ge(loaded[l], 32 * (j + 1))
                    if again(j):
                        dve.wait_ge(stored[l], 32 * j)
                    nc.vector.tensor_tensor(own[l][:, :, :], right[l][:, 0:2 * D].rearrange("p (u d) -> p u d", u=2),
                                            bc(c.bias[:, B_SHIFT, :], 2), ALU.add).then_inc(dve_done[l], 1)
                    nc.vector.tensor_tensor(message[l][:, 0, :], right[l][:, D:2 * D], filt[l][:, 0, :], ALU.mult).then_inc(dve_done[l], 1)

                rounds(dve, STAGES, {"norm1": norm1, "h": apply1, "n in": n_in, "norm2": norm2, "h5": apply2, "own": node}, N2)

            @block.scalar
            def _(act):
                def copy(l, j):
                    act.wait_ge(pe_done[l], count(PE, j, "turn h"))
                    nc.scalar.activation(hT[l][:, 0:2 * P], left[l][:, 0:2 * P], ACT.Relu).then_inc(act_done[l], 1)
                    nc.scalar.activation(hT[l][:, 2 * P:4 * P], left[l][:, 2 * P:4 * P], ACT.Copy).then_inc(act_done[l], 1)
                    act.wait_ge(pe_done[l], count(PE, j, "turn out"))
                    nc.scalar.activation(outT[l][:, :], right[l][:, 0:2 * P], ACT.Copy).then_inc(act_done[l], 1)

                def rz_(l, j):
                    for i, (bank, side) in enumerate(((left, "gates src"), (right, "gates dst"))):
                        act.wait_ge(pe_done[l], count(PE, j, side))
                        nc.scalar.activation(rz[l][:, i, :], bank[l][:, D:3 * D], ACT.Tanh, scale=0.5).then_inc(act_done[l], 1)

                def n_(l, j):
                    act.wait_ge(dve_done[l], count(DV, j, "n in dst"))
                    nc.scalar.activation(n[l][:, :, :], u[l][:, :, :], ACT.Tanh).then_inc(act_done[l], 1)

                def copy5(l, j):
                    act.wait_ge(pe_done[l], count(PE, j, "turn h5"))
                    nc.scalar.activation(hT[l][:, 0:2 * P], left[l][:, 0:2 * P], ACT.Relu).then_inc(act_done[l], 1)

                rounds(act, STAGES, {"hT": copy, "rz": rz_, "n": n_, "h5T": copy5}, N2)

            @block.tensor
            def _(pe):
                def turn(l, j):
                    pe.wait_ge(dve_done[l], count(DV, j, "h"))
                    pe.wait_ge(loaded[l], 32 * (j + 1))
                    pe.wait_ge(gathered[l], 48 * (j + 1))
                    if again(j):
                        pe.wait_ge(act_done[l], count(AC, j - 1, "h5T"))
                        pe.wait_ge(dve_done[l], count(DV, j - 1, "message"))
                    turn_pair(pe, c, left[l], h, l)
                    turn_pair(pe, c, left[l][:, 2 * P:4 * P], into, l).then_inc(pe_done[l], 1)
                    turn_pair(pe, c, right[l], out, l).then_inc(pe_done[l], 1)

                def gates(i, bank):
                    def go(l, j):
                        pe.wait_ge(act_done[l], count(AC, j, "outT"))
                        o, cols = bank[l], slice(i * P, (i + 1) * P)
                        pe.matmul(o[:, :], c.ones3[:, :], c.bias3[:, B_HN:B_IN + 1, :].rearrange("a b d -> a (b d)"), start=True, stop=False)
                        pe.matmul(o[:, 0:3 * D], hT[l][:, cols], c.whhT[:, :, :].rearrange("p g d -> p (g d)"), start=False, stop=False)
                        pe.matmul(o[:, D:4 * D], hT[l][:, 2 * P + i * P:2 * P + (i + 1) * P], c.wfwd[:, :, :].rearrange("p g d -> p (g d)"),
                                  start=False, stop=False)
                        last = pe.matmul(o[:, D:4 * D], outT[l][:, cols], c.wrev[:, :, :].rearrange("p g d -> p (g d)"), start=False, stop=True)
                        last.then_inc(pe_done[l], 1)
                    return go

                def turn5(l, j):
                    pe.wait_ge(dve_done[l], count(DV, j, "h5"))
                    turn_pair(pe, c, left[l], h5, l).then_inc(pe_done[l], 1)

                def node(l, j):
                    pe.wait_ge(act_done[l], count(AC, j, "h5T"))
                    for i in range(2):
                        o = right[l][:, i * D:(i + 1) * D]
                        pe.matmul(o, c.ones3[:, :], c.bias3[:, B_NODE_MSG, :], start=True, stop=False)
                        last = pe.matmul(o, hT[l][:, i * P:(i + 1) * P], c.wnode[:, :], start=False, stop=True)
                    last.then_inc(pe_done[l], 1)

                rounds(pe, STAGES, {"turn h": turn, "gates src": gates(0, left), "gates dst": gates(1, right), "turn h5": turn5, "node": node}, N2)


def phase_filter(nc, c, d):
    DV = ["sum", "x", "stats", "mean", "var", "h", "out", "own"]
    PO = ["index", "rstd"]
    AC = ["hT", "message"]
    PE = ["turn", "products"]
    STAGES = ["load", "", "", "", "", "sum", "rstd", "h", "turn", "hT", "products", "own", "store", "", "", "", "", "", ""]
    with ExitStack() as ctx:
        w = Work(nc, ctx, "filter")
        index = w.sb("index", [P, 4], I32)
        near, s, own, x, h, y = (w.sb(n, [P, 2, D]) for n in ("near", "s", "own", "x", "h", "y"))
        hT, message = w.sb("hT", [P, 2 * P]), w.sb("message", [P, D])
        norm = Norm(w, P, 2)
        left, right = w.banks("left"), w.banks("right")
        loaded, gathered, stored, written = w.sems("loaded"), w.sems("gathered"), w.sems("stored"), w.sems("written")
        pe_done, act_done, dve_done, pool_done = w.sems("pe_done"), w.sems("act_done"), w.sems("dve_done"), w.sems("pool_done")
        with nc.Block() as block:
            @block.gpsimd
            def _(pool):
                def load(l, j):
                    if again(j):
                        pool.wait_ge(written[l], 16 * j)
                        pool.wait_ge(dve_done[l], count(DV, j - 1, "sum"))
                    pool.tensor_copy(index[l][:, :], fields(c.rec[BY_DST], AT(l, j), R_DST_OUT, R_WRITE_SRC + 1)).then_inc(pool_done[l], 1)
                    pool.wait_ge(pool_done[l], count(PO, j, "index"))
                    for i, at in ((0, 2), (1, 0)):
                        gather(pool, near[l][:, i, :], d["from"], index[l][:, at:at + 1], c.bound[SLOTS]).then_inc(gathered[l], 16)

                def factors(l, j):
                    pool.wait_ge(dve_done[l], count(DV, j, "var"))
                    norm.power(pool, c, l).then_inc(pool_done[l], 1)

                def write(l, j):
                    pool.wait_ge(dve_done[l], count(DV, j, "out"))
                    scatter(pool, d["out"], index[l][:, 3:4], y[l][:, 0, :], c.bound[N_NODES - 1]).then_inc(written[l], 16)

                rounds(pool, STAGES, {"load": load, "rstd": factors, "store": write}, N2)
                for l in range(LANES):
                    pool.wait_ge(written[l], 16 * N2)

            @block.sync
            def _(sp):
                def load(l, j):
                    if again(j):
                        sp.wait_ge(dve_done[l], count(DV, j - 1, "sum"))
                    sp.dma_start(own[l][:, :, :], tile_rows(d["kept"], AT(l, j))).then_inc(loaded[l], 16)

                def store(l, j):
                    sp.wait_ge(act_done[l], count(AC, j, "message"))
                    sp.dma_start(tile_rows(d["message"], AT(l, j)), message[l][:, :]).then_inc(stored[l], 16)

                rounds(sp, STAGES, {"load": load, "store": store}, N2)
                for l in range(LANES):
                    sp.wait_ge(stored[l], 16 * N2)

            @block.vector
            def _(dve):
                def add(l, j):
                    dve.wait_ge(loaded[l], 16 * (j + 1))
                    dve.wait_ge(gathered[l], 32 * (j + 1))
                    nc.vector.tensor_tensor(s[l][:, :, :], near[l][:, :, :], own[l][:, :, :], ALU.add).then_inc(dve_done[l], 1)
                    dve.wait_ge(dve_done[l], count(DV, j, "sum"))
                    nc.vector.scalar_tensor_tensor(x[l][:, :, :], s[l][:, :, :], 0.0, pair(c.state, AT(l, j)), ALU.max, ALU.add).then_inc(dve_done[l], 1)
                    dve.wait_ge(dve_done[l], count(DV, j, "x"))
                    norm.factor_base(dve, l, x[l], dve_done, lambda s: count(DV, j, s))

                def apply(l, j):
                    dve.wait_ge(pool_done[l], count(PO, j, "rstd"))
                    norm.apply_here(h, x[l], l).then_inc(dve_done[l], 1)

                def out(l, j):
                    dve.wait_ge(pe_done[l], count(PE, j, "products"))
                    dve.wait_ge(act_done[l], count(AC, j, "message"))
                    if again(j):
                        dve.wait_ge(written[l], 16 * j)
                    nc.vector.tensor_tensor(y[l][:, 0, :], right[l][:, 0:D], x[l][:, 0, :], ALU.add).then_inc(dve_done[l], 1)
                    t = AT(l, j)
                    mine = c.state[:, t, 1, :] if isinstance(t, int) else c.state[:, bass.ds(t, 1), 1, :].rearrange("p a d -> p (a d)")
                    nc.vector.tensor_tensor(mine, right[l][:, 2 * D:3 * D], x[l][:, 1, :], ALU.add).then_inc(dve_done[l], 1)

                rounds(dve, STAGES, {"sum": add, "h": apply, "own": out}, N2)

            @block.scalar
            def _(act):
                def relu(l, j):
                    act.wait_ge(pe_done[l], count(PE, j, "turn"))
                    nc.scalar.activation(hT[l][:, :], left[l][:, 0:2 * P], ACT.Relu).then_inc(act_done[l], 1)

                def send(l, j):
                    act.wait_ge(pe_done[l], count(PE, j, "products"))
                    if again(j):
                        act.wait_ge(stored[l], 16 * j)
                    nc.scalar.activation(message[l][:, :], right[l][:, SENT], ACT.Copy).then_inc(act_done[l], 1)

                rounds(act, STAGES, {"hT": relu, "own": send}, N2)

            @block.tensor
            def _(pe):
                def turn(l, j):
                    pe.wait_ge(dve_done[l], count(DV, j, "h"))
                    if again(j):
                        pe.wait_ge(act_done[l], count(AC, j - 1, "hT"))
                    turn_pair(pe, c, left[l], h, l).then_inc(pe_done[l], 1)

                def products(l, j):
                    pe.wait_ge(act_done[l], count(AC, j, "hT"))
                    if again(j):
                        pe.wait_ge(dve_done[l], count(DV, j - 1, "own"))
                    both = c.wout[:, :, :].rearrange("p g d -> p (g d)")
                    pe.matmul(right[l][:, 0:2 * D], c.ones3[:, :], c.bias3[:, B_OUT:B_OUT + 2, :].rearrange("a b d -> a (b d)"),
                              start=True, stop=False)
                    pe.matmul(right[l][:, 0:2 * D], hT[l][:, 0:P], both, start=False, stop=True)
                    o = right[l][:, 2 * D:3 * D]
                    pe.matmul(o, c.ones3[:, :], c.bias3[:, B_OUT, :], start=True, stop=False)
                    pe.matmul(o, hT[l][:, P:2 * P], both[:, 0:D], start=False, stop=True).then_inc(pe_done[l], 1)

                rounds(pe, STAGES, {"turn": turn, "products": products}, N2)


def build(nc, a, out):
    def table(name, rows, cols, dt=F32):
        return nc.dram_tensor(name, [rows, cols], dt, kind="Internal").ap()

    d = {"out": out}
    d["starts"] = table("starts", P * NHI, 2, I32)
    d["by_dst"] = table("by_dst", SLOTS, FIELDS, I32)
    d["by_src"] = table("by_src", SLOTS, FIELDS, I32)
    d["key_rows"] = table("key_rows", 2, SLOTS)
    d["inside"] = nc.dram_tensor("inside", [2, 2, SLOTS], F32, kind="Internal").ap()
    d["carried"] = table("carried", 2, TILES * D)
    d["carried2"] = table("carried2", 2, TILES * 2)
    d["into"] = table("into", SLOTS + P, D)
    d["from"] = table("from", SLOTS + P, D)
    d["message"] = table("message", SLOTS, D)
    d["reverse"] = table("reverse", SLOTS, D)
    d["filter"] = table("filter", SLOTS, D)
    d["kept"] = nc.dram_tensor("kept", [SLOTS, 2, D], F32, kind="Internal").ap()
    with ExitStack() as ctx:
        c = allocate(nc, ctx)
        c.bound = row_bounds(nc.gpsimd)
        phase_setup(nc, c, a)
        with ExitStack() as order:
            e = allocate_order(nc, order)
            phase_order(nc, c, a, d, e)
            phase_dense(nc, c, a["x"], out, d, e)
        allocate_edges(nc, ctx, c)
        phase_keys(nc, c, d)
        phase_degrees(nc, c, d)
        phase_enter(nc, c, d, a)
        for layer in (0, 1):
            phase_sum(nc, c, d, f"sum{layer}", BY_DST, (d["message"], None), D, c.inv[BY_DST][0], "into")
            phase_layer(nc, c, d, layer + 1)
        phase_sum(nc, c, d, "sum2", BY_DST, (d["message"], None), D, c.inv[BY_DST][0], "into")
        phase_join(nc, c, d)
        phase_sum(nc, c, d, "fwd", BY_DST, (d["message"], None), D, c.inv[BY_DST][1], "into")
        phase_sum(nc, c, d, "rev", BY_SRC, (d["reverse"], R_PLACE), D, c.inv[BY_SRC][1], "from")
        phase_edges(nc, c, d, a)
        phase_gru(nc, c, d)
        phase_sum(nc, c, d, "nodes", BY_SRC, (d["reverse"], R_PLACE), D, c.inv[BY_SRC][0], "from")
        phase_filter(nc, c, d)
        phase_sum(nc, c, d, "last", BY_DST, (d["message"], None), D, None, "out")


_INS = ['x', 'src', 'dst', 'edge_attr_128', 'edge_weight', 'L0_gnn_W_l', 'L0_gnn_b_l', 'L0_gnn_W_r', 'L1_gnn_W1',
        'L1_gnn_W2', 'L1_gnn_w_ih', 'L1_gnn_w_hh', 'L1_gnn_b_ih', 'L1_gnn_b_hh', 'L2_gnn_W_node', 'L2_gnn_b_node',
        'L2_gnn_W_gate', 'L2_gnn_b_gate', 'L2_gnn_W_filt', 'L2_gnn_b_filt', 'L2_gnn_bn_gamma', 'L2_gnn_bn_beta',
        'L2_gnn_bn_mean', 'L2_gnn_bn_var', 'L3_gnn_W_neigh', 'L3_gnn_b_neigh', 'L3_gnn_W_self', 'L3_gnn_b_self']


def kernel(**inputs):
    import numpy as np
    import concourse.bacc as bacc
    from concourse.bass_utils import run_bass_kernel_spmd

    nc = bacc.Bacc("TRN2", target_bir_lowering=False, num_devices=1)
    arrays, args = {}, {}
    for name in _INS:
        arrays[name] = np.ascontiguousarray(inputs[name])
        args[name] = nc.dram_tensor(name, arrays[name].shape, mybir.dt.from_np(arrays[name].dtype), kind="ExternalInput").ap()
    out = nc.dram_tensor("out", (N_NODES, D), F32, kind="ExternalOutput").ap()
    build(nc, args, out)
    r = run_bass_kernel_spmd(nc, [arrays], core_ids=[0])
    return r.results[0]["out"]
```

```python
from contextlib import ExitStack

import concourse.bass as bass
from concourse import mybir

F32 = mybir.dt.float32
BF16 = mybir.dt.bfloat16
I32 = mybir.dt.int32
U16 = mybir.dt.uint16
ALU = mybir.AluOpType
ACT = mybir.ActivationFunctionType

P = 128
D = 128
N_NODES = 50000
N_EDGES = 12500
TILES = 100
SLOTS = TILES * P
PAD_NODE = N_NODES
EDGE_ROWS = N_EDGES // TILES
LANES = 5
ROUNDS = TILES // LANES
AT = lambda l, j: LANES * j + l
FEW = 4
LN_EPS = 1e-5
BN_EPS = 1e-3

ND, NU = 125, 4
GROUP = ND * NU
assert N_NODES == GROUP * LANES * ROUNDS
SPLIT = 112

(B_HN, B_R, B_Z, B_IN, B_L0, B_L1, B_L2, B_NODE_MSG, B_NODE, B_OUT, B_ZERO, B_GATE, B_FILT, B_SHIFT) = range(14)
NBIAS = 14
ROW_OF = {B_IN: 0, B_L0: 1, B_L1: 2, B_L2: 3, B_SHIFT: 4}


class Semaphores:

    def __init__(self, nc):
        self.nc, self.all = nc, []

    def __call__(self, name):
        self.all.append(self.nc.alloc_semaphore(name))
        return self.all[-1]

    def __enter__(self):
        return self

    def __exit__(self, *error):
        if error[0] is None:
            self.nc.clear_and_free_semaphores(self.all)
            self.nc.all_engine_barrier()


def rounds(eng, stages, mine, n, lanes=LANES):
    k = len(stages)
    late = [l * k // lanes for l in range(lanes)]

    def one(j, first=False, last=False):
        for slot in range(k):
            for l in range(lanes):
                s = slot - late[l]
                if s >= 0 and not last and stages[s] in mine:
                    mine[stages[s]](l, j)
                elif s < 0 and not first and stages[s + k] in mine:
                    mine[stages[s + k]](l, j - 1)

    one(0, first=True)
    one(1)
    with eng.Fori(2, n) as j:
        one(j)
    one(n, last=True)


def timetable(slots, starts):
    stages = [""] * slots
    for name, slot in starts.items():
        assert stages[slot] == ""
        stages[slot] = name
    return stages


def count(names, j, name):
    return j * len(names) + names.index(name) + 1


def again(j):
    return not (isinstance(j, int) and j == 0)


def bc(ap, n):
    return ap.unsqueeze(1).to_broadcast([ap.shape[0], n, ap.shape[1]])


def col(ap, n):
    return ap.unsqueeze(2).to_broadcast([ap.shape[0], ap.shape[1], n])


class Chip:
    pass


def allocate(nc, ctx):
    c = Chip()

    def sb(name, shape, dt):
        return ctx.enter_context(nc.sbuf_tensor(name, shape, dt))

    c.ident = sb("ident", [P, P], F32)
    c.identb = sb("identb", [P, P], BF16)
    c.wrT = sb("wrT", [P, 3, 2 * D], F32)
    c.whhT = sb("whhT", [P, 3, D], F32)
    c.wfwd = sb("wfwd", [P, 3, D], F32)
    c.wrev = sb("wrev", [P, 3, D], F32)
    c.wnode = sb("wnode", [P, D], F32)
    c.wgf = sb("wgf", [P, 2, D], F32)
    c.wout = sb("wout", [P, 2, D], F32)
    c.bcol = sb("bcol", [P, 2], F32)
    c.bias = sb("bias", [P, len(ROW_OF), D], F32)
    c.bias3 = sb("bias3", [3, NBIAS, D], BF16)
    c.ones3 = sb("ones3", [3, P], BF16)
    c.power = sb("power", [P, P], F32)
    return c


def phase_setup(nc, c, a):
    with ExitStack() as ctx:
        def sb(name, shape, dt):
            return ctx.enter_context(nc.sbuf_tensor(name, shape, dt))

        sem = ctx.enter_context(Semaphores(nc))
        raw = sb("raw", [P, 17, D], F32)
        rows = sb("rows", [P, 18, D], F32)
        w12 = sb("w12", [P, 2, D], F32)
        wihT = sb("wihT", [P, 2, 3, D], F32)
        scale = sb("scale", [P, D], F32)
        rstd = sb("bn_rstd", [P, D], F32)
        shifted = sb("shifted", [P, D], F32)
        bias = sb("bias_all", [P, NBIAS, D], F32)
        part = [sb(f"part{i}", [1, NBIAS * D], BF16) for i in range(3)]
        rest = [sb(f"rest{i}", [1, NBIAS * D], F32) for i in range(2)]
        turned = ctx.enter_context(nc.psum_tensor("turned", [P, 17, P], F32))
        folded = ctx.enter_context(nc.psum_tensor("folded", [P, 2, 512], F32))
        loaded = sem("loaded")
        zeroed = sem("zeroed")
        ones_set = sem("ones_set")
        ident_made = sem("ident_made")
        turns_done = sem("turns_done")
        turned_copied = sem("turned_copied")
        folds_done = sem("folds_done")
        folds_copied = sem("folds_copied")
        vec = sem("vec")
        rstd_made = sem("rstd_made")
        parts_placed = sem("parts_placed")
        block = ctx.enter_context(nc.Block())
        IH, HH, NODE, GATE, FILT, GAMMA, BETA, MEAN, VAR, NEIGH, SELF = 3, 6, 9, 10, 11, 12, 13, 14, 15, 16, 17
        loads = []
        for i in range(3):
            loads.append((raw[:, i, :], a["L0_gnn_W_l"][i]))
            loads.append((raw[:, 3 + i, :], a["L0_gnn_W_r"][i]))
            loads.append((raw[:, 6 + i, :], a["L1_gnn_w_hh"][i * D:(i + 1) * D, :]))
            for h in range(2):
                loads.append((raw[:, 9 + 3 * h + i, :], a["L1_gnn_w_ih"][i * D:(i + 1) * D, h * D:(h + 1) * D]))
        loads.append((raw[:, 15, :], a["L3_gnn_W_self"]))
        loads.append((raw[:, 16, :], a["L3_gnn_W_neigh"]))
        loads.append((w12[:, 0, :], a["L1_gnn_W1"]))
        loads.append((w12[:, 1, :], a["L1_gnn_W2"]))
        loads.append((c.wnode[:, :], a["L2_gnn_W_node"]))
        loads.append((c.wgf[:, 0, :], a["L2_gnn_W_gate"]))
        loads.append((c.wgf[:, 1, :], a["L2_gnn_W_filt"]))
        vectors = [a["L0_gnn_b_l"][i] for i in range(3)]
        for v in ("L1_gnn_b_ih", "L1_gnn_b_hh"):
            vectors += [a[v][i * D:(i + 1) * D] for i in range(3)]
        vectors += [a["L2_gnn_" + v] for v in ("b_node", "b_gate", "b_filt", "bn_gamma", "bn_beta", "bn_mean", "bn_var")]
        vectors += [a["L3_gnn_b_neigh"], a["L3_gnn_b_self"]]
        for i, v in enumerate(vectors):
            loads.append((rows[:, i, :], v.partition_broadcast(P)))
        for i in range(2):
            loads.append((c.bcol[:, i:i + 1], a["L0_gnn_b_l"][i].rearrange("(p x) -> p x", x=1)))

        @block.sync
        def _(sp):
            for out, src in loads:
                sp.dma_start(out, src).then_inc(loaded, 16)
            sp.wait_ge(vec, 22)
            for i in range(3):
                sp.dma_start(c.bias3[i:i + 1, :, :].rearrange("a b d -> a (b d)"), part[i][:, :]).then_inc(parts_placed, 16)
            sp.wait_ge(parts_placed, 48)

        @block.gpsimd
        def _(pool):
            pool.memset(c.ident[:, :], 0.0).then_inc(zeroed, 1)
            pool.memset(c.ones3[:, :], 1.0).then_inc(ones_set, 1)
            pool.wait_ge(zeroed, 1)
            pool.affine_select(out=c.ident[:, :], in_=c.ident[:, :], compare_op=ALU.not_equal, fill=1.0,
                               base=0, pattern=[[-1, P]], channel_multiplier=1).then_inc(ident_made, 1)
            pool.memset(c.power[:, :], -0.5).then_inc(zeroed, 1)
            pool.wait_ge(loaded, 16 * len(loads))
            pool.tensor_scalar(scale[:, :], rows[:, VAR, :], BN_EPS, None, ALU.add).then_inc(zeroed, 1)
            pool.wait_ge(zeroed, 3)
            pool.tensor_tensor(rstd[:, :], scale[:, :], c.power[:, :], ALU.pow).then_inc(rstd_made, 1)

        @block.tensor
        def _(pe):
            pe.wait_ge(ident_made, 1)
            pe.wait_ge(loaded, 16 * len(loads))
            for i in range(17):
                pe.transpose(turned[:, i, :], raw[:, i, :], c.ident[:, :]).then_inc(turns_done, 1)
            pe.wait_ge(turned_copied, 17)
            for h in range(2):
                pe.matmul(folded[:, h, 0:3 * D], w12[:, h, :], wihT[:, h, :, :].rearrange("p g d -> p (g d)"),
                          start=True, stop=True).then_inc(folds_done, 1)

        @block.scalar
        def _(act):
            place = [c.wrT[:, i, D:2 * D] for i in range(3)] + [c.wrT[:, i, 0:D] for i in range(3)]
            place += [c.whhT[:, i, :] for i in (1, 2, 0)]
            place += [wihT[:, h, i, :] for h in range(2) for i in range(3)]
            place += [c.wout[:, 0, :], c.wout[:, 1, :]]
            for i, out in enumerate(place):
                act.wait_ge(turns_done, 17)
                nc.scalar.activation(out, turned[:, i, :], ACT.Copy).then_inc(turned_copied, 1)
            for h, out in enumerate((c.wfwd, c.wrev)):
                act.wait_ge(folds_done, 2)
                nc.scalar.activation(out[:, :, :], folded[:, h, 0:3 * D].rearrange("p (g d) -> p g d", g=3),
                                     ACT.Copy).then_inc(folds_copied, 1)

        @block.vector
        def _(dve):
            dve.wait_ge(ident_made, 1)
            nc.vector.tensor_copy(c.identb[:, :], c.ident[:, :]).then_inc(vec, 1)
            dve.wait_ge(loaded, 16 * len(loads))
            b = bias
            for out, row in ((B_HN, HH + 2), (B_IN, IH + 2), (B_L0, 0), (B_L1, 1), (B_L2, 2), (B_GATE, GATE), (B_FILT, FILT)):
                nc.vector.tensor_copy(b[:, out, :], rows[:, row, :]).then_inc(vec, 1)
            nc.vector.memset(b[:, B_ZERO, :], 0.0)
            for out, x, y in ((B_R, IH, HH), (B_Z, IH + 1, HH + 1), (B_OUT, NEIGH, SELF)):
                nc.vector.tensor_tensor(b[:, out, :], rows[:, x, :], rows[:, y, :], ALU.add).then_inc(vec, 1)
            dve.wait_ge(rstd_made, 1)
            nc.vector.tensor_tensor(scale[:, :], rstd[:, :], rows[:, GAMMA, :], ALU.mult).then_inc(vec, 1)
            dve.wait_ge(vec, 12)
            nc.vector.tensor_tensor(c.wnode[:, :], c.wnode[:, :], scale[:, :], ALU.mult).then_inc(vec, 1)
            nc.vector.tensor_tensor(b[:, B_NODE_MSG, :], rows[:, NODE, :], scale[:, :], ALU.mult).then_inc(vec, 1)
            nc.vector.tensor_tensor(shifted[:, :], rows[:, MEAN, :], scale[:, :], ALU.mult).then_inc(vec, 1)
            dve.wait_ge(vec, 15)
            nc.vector.tensor_tensor(b[:, B_SHIFT, :], rows[:, BETA, :], shifted[:, :], ALU.subtract).then_inc(vec, 1)
            dve.wait_ge(vec, 16)
            nc.vector.tensor_tensor(b[:, B_NODE, :], b[:, B_NODE_MSG, :], b[:, B_SHIFT, :], ALU.add).then_inc(vec, 1)
            dve.wait_ge(vec, 17)
            for row, place in ROW_OF.items():
                nc.vector.tensor_copy(c.bias[:, place, :], b[:, row, :])
            whole = b[0:1, :, :].rearrange("a b d -> a (b d)")
            nc.vector.tensor_copy(part[0][:, :], whole).then_inc(vec, 1)
            dve.wait_ge(vec, 18)
            nc.vector.tensor_tensor(rest[0][:, :], whole, part[0][:, :], ALU.subtract).then_inc(vec, 1)
            dve.wait_ge(vec, 19)
            nc.vector.tensor_copy(part[1][:, :], rest[0][:, :]).then_inc(vec, 1)
            dve.wait_ge(vec, 20)
            nc.vector.tensor_tensor(rest[1][:, :], rest[0][:, :], part[1][:, :], ALU.subtract).then_inc(vec, 1)
            dve.wait_ge(vec, 21)
            nc.vector.tensor_copy(part[2][:, :], rest[1][:, :]).then_inc(vec, 1)


def phase_dense(nc, c, x_dram, out_dram, d, e):
    x_view = x_dram.rearrange("(g p u) d -> g p u d", p=ND, u=NU)
    out_view = out_dram.rearrange("(g p u) d -> g p u d", p=ND, u=NU)
    PE = ["h0T", "h1T", "h2T", "h3", "h4T", "rz low", "rz high", "hn", "h5T", "node", "h6T", "self"]
    AC = ["h0", "h0T", "h1T", "h2T", "h4", "h4T", "rz low", "rz high", "n", "h5", "h5T", "h6", "h6T"]
    DV = ["stats0", "mean0", "var0", "shift0", "x1", "stats1", "mean1", "var1", "shift1", "r hn", "n in", "z mix",
          "x2", "stats2", "mean2", "var2", "shift2", "x3", "stats3", "mean3", "var3", "shift3", "out"]
    PO = ["rstd0", "rstd1", "h4 - n", "n + x1", "rstd2", "rstd3"]
    STAGES = timetable(336, {"load": 0, "ln0": 18, "rstd0": 26, "shift0": 32, "h0": 35, "h0T": 44, "h0T copy": 55,
                             "look up": 60, "h1T": 62, "h1T relu": 68, "h2T": 73, "h2T relu": 78, "h3": 83, "ln1": 91,
                             "rstd1": 101, "record": 105, "shift1": 108, "h4": 113, "h4T": 122, "h4T copy": 126,
                             "gates low": 133, "rz low": 140, "send": 143, "gates high": 145, "rz high": 151, "hn": 156,
                             "n in": 167, "n": 176, "mix": 180, "ln2": 193, "rstd2": 206, "shift2": 212, "h5": 221, "h5T": 230,
                             "h5T copy": 234, "node": 239, "ln3": 246, "rstd3": 257, "shift3": 271, "h6": 295, "h6T": 304,
                             "h6T copy": 312, "self": 317, "out": 324, "store": 329})
    with ExitStack() as ctx:
        w = Work(nc, ctx, "dense")
        x, x1, x2, x3, y, h, h4, u, n, apart, both = (w.sb(s, [ND, NU, D]) for s in (
            "x", "x1", "x2", "x3", "y", "h", "h4", "u", "n", "apart", "both"))
        hT, gT = w.sb("hT", [P, GROUP]), w.sb("gT", [P, GROUP])
        rz = w.sb("rz", [ND, NU, 2 * D])
        norm = Norm(w, ND, NU)
        bank = w.banks("bank")
        loaded, stored = w.sems("x_loaded"), w.sems("out_stored")
        pe_done, act_done, dve_done, pool_done = w.sems("pe_done"), w.sems("act_done"), w.sems("dve_done"), w.sems("pool_done")
        records = Records(nc, w, c, d, e)
        block = ctx.enter_context(nc.Block())

        def rows(t):
            return t[0:ND, 0:NU * D].rearrange("p (u d) -> p u d", u=NU)

        def dv(j, name):
            return count(DV, j, name)

        def ac(j, name):
            return count(AC, j, name)

        def pn(j, name):
            return count(PE, j, name)

        def po(j, name):
            return count(PO, j, name)

        def part(view, g, lo, hi):
            return view[g, lo:hi] if isinstance(g, int) else view[bass.ds(g, 1), lo:hi].rearrange("g p u d -> (g p) u d")

        @block.sync
        def _(sp):
            def load(l, j):
                if again(j):
                    sp.wait_ge(dve_done[l], dv(j - 1, "x1"))
                for lo, hi in ((0, SPLIT), (SPLIT, ND)):
                    sp.dma_start(x[l][lo:hi, :, :], part(x_view, AT(l, j), lo, hi)).then_inc(loaded[l], 16)

            def store(l, j):
                sp.wait_ge(dve_done[l], dv(j, "out"))
                for lo, hi in ((0, SPLIT), (SPLIT, ND)):
                    sp.dma_start(part(out_view, AT(l, j), lo, hi), y[l][lo:hi, :, :]).then_inc(stored[l], 16)

            rounds(sp, STAGES, {"load": load, "store": store}, ROUNDS)
            for l in range(LANES):
                sp.wait_ge(stored[l], 32 * ROUNDS)

        @block.gpsimd
        def _(pool):
            def factors(k):
                def go(l, j):
                    pool.wait_ge(dve_done[l], dv(j, "var" + k))
                    norm.power(pool, c, l).then_inc(pool_done[l], 1)
                return go

            def mix(l, j):
                pool.wait_ge(act_done[l], ac(j, "n"))
                if again(j):
                    pool.wait_ge(dve_done[l], dv(j - 1, "x2"))
                pool.tensor_tensor(apart[l][:, :, :], h4[l][:, :, :], n[l][:, :, :], ALU.subtract).then_inc(pool_done[l], 1)
                pool.tensor_tensor(both[l][:, :, :], n[l][:, :, :], x1[l][:, :, :], ALU.add).then_inc(pool_done[l], 1)

            rounds(pool, STAGES, {"mix": mix, "look up": records.look_up(pool), "send": records.send(pool)}
                   | {"rstd" + k: factors(k) for k in "0123"}, ROUNDS)
            records.finish(pool)

        @block.tensor
        def _(pe):
            def turn(src, l):
                for i in range(NU):
                    last = pe.transpose(bank[l][:, i * ND:(i + 1) * ND], src[l][:, i, :], c.ident[0:ND, 0:ND])
                last.then_inc(pe_done[l], 1)

            def h0T(l, j):
                pe.wait_ge(act_done[l], ac(j, "h0"))
                if again(j):
                    pe.wait_ge(dve_done[l], dv(j - 1, "out"))
                turn(h, l)

            def h1T(l, j):
                pe.wait_ge(act_done[l], ac(j, "h0T"))
                pe.matmul(bank[l][:, 0:GROUP], c.wrT[:, 0, 0:D], hT[l][:, :], start=True, stop=True).then_inc(pe_done[l], 1)

            def h2T(l, j):
                pe.wait_ge(act_done[l], ac(j, "h1T"))
                pe.matmul(bank[l][:, 0:GROUP], c.wrT[:, 1, 0:D], gT[l][:, :], start=True, stop=True).then_inc(pe_done[l], 1)

            def rowwise(l, lhs, rhs, bias):
                for i in range(NU):
                    o = bank[l][0:ND, i * D:(i + 1) * D]
                    pe.matmul(o, c.ones3[:, 0:ND], c.bias3[:, bias, :], start=True, stop=False)
                    last = pe.matmul(o, lhs[l][:, i * ND:(i + 1) * ND], rhs, start=False, stop=True)
                last.then_inc(pe_done[l], 1)

            def h3(l, j):
                pe.wait_ge(act_done[l], ac(j, "h2T"))
                rowwise(l, hT, c.wrT[:, 2, 0:D], B_L2)

            def h4T(l, j):
                pe.wait_ge(act_done[l], ac(j, "h4"))
                turn(h4, l)

            def gates(k, waited):
                def go(l, j):
                    pe.wait_ge(act_done[l], ac(j, waited))
                    for i in range(2):
                        o = bank[l][0:ND, i * 2 * D:(i + 1) * 2 * D]
                        at = 2 * k + i
                        pe.matmul(o, c.ones3[:, 0:ND], c.bias3[:, B_R:B_Z + 1, :].rearrange("a b d -> a (b d)"),
                                  start=True, stop=False)
                        last = pe.matmul(o, gT[l][:, at * ND:(at + 1) * ND], c.whhT[:, 1:3, :].rearrange("p g d -> p (g d)"),
                                         start=False, stop=True)
                    last.then_inc(pe_done[l], 1)
                return go

            def hn(l, j):
                pe.wait_ge(act_done[l], ac(j, "rz high"))
                rowwise(l, gT, c.whhT[:, 0, :], B_HN)

            def h5T(l, j):
                pe.wait_ge(act_done[l], ac(j, "h5"))
                turn(h, l)

            def node(l, j):
                pe.wait_ge(act_done[l], ac(j, "h5T"))
                rowwise(l, hT, c.wnode[:, :], B_NODE)

            def h6T(l, j):
                pe.wait_ge(act_done[l], ac(j, "h6"))
                turn(h, l)

            def own(l, j):
                pe.wait_ge(act_done[l], ac(j, "h6T"))
                rowwise(l, gT, c.wout[:, 0, :], B_OUT)

            rounds(pe, STAGES, {"h0T": h0T, "h1T": h1T, "h2T": h2T, "h3": h3, "h4T": h4T, "gates low": gates(0, "h4T"), "gates high": gates(1, "rz low"), "hn": hn, "h5T": h5T,
                                "node": node, "h6T": h6T, "self": own}, ROUNDS)

        @block.scalar
        def _(act):
            def relu_of(out, name):
                def go(l, j):
                    act.wait_ge(pe_done[l], pn(j, name))
                    nc.scalar.activation(out[l][:, :], bank[l][:, 0:GROUP], ACT.Relu).then_inc(act_done[l], 1)
                return go

            def h0(l, j):
                act.wait_ge(dve_done[l], dv(j, "shift0"))
                if again(j):
                    act.wait_ge(pe_done[l], pn(j - 1, "h6T"))
                norm.apply(h, x, l).then_inc(act_done[l], 1)

            def layer(out, name, i):
                def go(l, j):
                    act.wait_ge(pe_done[l], pn(j, name))
                    nc.scalar.activation(out[l][:, :], bank[l][:, 0:GROUP], ACT.Relu, bias=c.bcol[:, i:i + 1]).then_inc(act_done[l], 1)
                return go

            def h4_(l, j):
                act.wait_ge(dve_done[l], dv(j, "shift1"))
                if again(j):
                    act.wait_ge(pool_done[l], po(j - 1, "h4 - n"))
                norm.apply(h4, x1, l).then_inc(act_done[l], 1)

            def apply(src, k):
                def go(l, j):
                    act.wait_ge(dve_done[l], dv(j, "shift" + k))
                    norm.apply(h, src, l).then_inc(act_done[l], 1)
                return go

            def rz_(k, name):
                def go(l, j):
                    act.wait_ge(pe_done[l], pn(j, name))
                    nc.scalar.activation(rz[l][:, 2 * k:2 * k + 2, :], bank[l][0:ND, :].rearrange("p (u c) -> p u c", u=2),
                                         ACT.Tanh, scale=0.5).then_inc(act_done[l], 1)
                return go

            def n_(l, j):
                act.wait_ge(dve_done[l], dv(j, "n in"))
                nc.scalar.activation(n[l][:, :, :], u[l][:, :, :], ACT.Tanh).then_inc(act_done[l], 1)

            rounds(act, STAGES, {"h0": h0, "h0T copy": relu_of(hT, "h0T"), "h1T relu": layer(gT, "h1T", 0), "h2T relu": layer(hT, "h2T", 1), "h4": h4_,
                                 "h4T copy": relu_of(gT, "h4T"), "rz low": rz_(0, "rz low"), "rz high": rz_(1, "rz high"), "n": n_, "h5T copy": relu_of(hT, "h5T"),
                                 "h5": apply(x2, "2"), "h6": apply(x3, "3"), "h6T copy": relu_of(gT, "h6T")}, ROUNDS)

        @block.vector
        def _(dve):
            def moments(l, j, src, k):
                norm.factor_base(dve, l, src[l], dve_done, lambda s: dv(j, s + k))

            def shift(k):
                def go(l, j):
                    dve.wait_ge(pool_done[l], po(j, "rstd" + k))
                    norm.move(l).then_inc(dve_done[l], 1)
                return go

            def ln0(l, j):
                dve.wait_ge(loaded[l], (j + 1) * 32)
                moments(l, j, x, "0")

            def ln1(l, j):
                dve.wait_ge(pe_done[l], pn(j, "h3"))
                if again(j):
                    dve.wait_ge(pool_done[l], po(j - 1, "n + x1"))
                nc.vector.tensor_tensor(x1[l][:, :, :], rows(bank[l]), x[l][:, :, :], ALU.add).then_inc(dve_done[l], 1)
                dve.wait_ge(dve_done[l], dv(j, "x1"))
                moments(l, j, x1, "1")

            def n_in(l, j):
                dve.wait_ge(pe_done[l], pn(j, "hn"))
                nc.vector.scalar_tensor_tensor(u[l][:, :, :], rz[l][:, :, 0:D], 1.0, rows(bank[l]), ALU.add, ALU.mult)\
                    .then_inc(dve_done[l], 1)
                dve.wait_ge(dve_done[l], dv(j, "r hn"))
                nc.vector.scalar_tensor_tensor(u[l][:, :, :], u[l][:, :, :], 0.5, bc(c.bias[0:ND, ROW_OF[B_IN], :], NU),
                                               ALU.mult, ALU.add).then_inc(dve_done[l], 1)

            def ln2(l, j):
                dve.wait_ge(pool_done[l], po(j, "n + x1"))
                nc.vector.scalar_tensor_tensor(u[l][:, :, :], rz[l][:, :, D:2 * D], 1.0, apart[l][:, :, :], ALU.add, ALU.mult)\
                    .then_inc(dve_done[l], 1)
                dve.wait_ge(dve_done[l], dv(j, "z mix"))
                nc.vector.scalar_tensor_tensor(x2[l][:, :, :], u[l][:, :, :], 0.5, both[l][:, :, :], ALU.mult, ALU.add)\
                    .then_inc(dve_done[l], 1)
                dve.wait_ge(dve_done[l], dv(j, "x2"))
                moments(l, j, x2, "2")

            def ln3(l, j):
                dve.wait_ge(pe_done[l], pn(j, "node"))
                nc.vector.scalar_tensor_tensor(x3[l][:, :, :], rows(bank[l]), 0.0, x2[l][:, :, :], ALU.max, ALU.add)\
                    .then_inc(dve_done[l], 1)
                dve.wait_ge(dve_done[l], dv(j, "x3"))
                moments(l, j, x3, "3")

            def out(l, j):
                dve.wait_ge(pe_done[l], pn(j, "self"))
                if again(j):
                    dve.wait_ge(stored[l], j * 32)
                nc.vector.tensor_tensor(y[l][:, :, :], rows(bank[l]), x3[l][:, :, :], ALU.add).then_inc(dve_done[l], 1)

            rounds(dve, STAGES, {"ln0": ln0, "shift0": shift("0"), "ln1": ln1, "shift1": shift("1"), "n in": n_in,
                                 "ln2": ln2, "shift2": shift("2"), "ln3": ln3, "shift3": shift("3"), "out": out, "record": records.make(dve)}, ROUNDS)


class Work:

    def __init__(self, nc, ctx, name, lanes=LANES):
        self.nc, self.ctx, self.name, self.lanes = nc, ctx, name, lanes
        self.semaphore = ctx.enter_context(Semaphores(nc))

    def sb(self, name, shape, dt=F32):
        return [self.one(f"{name}{l}", shape, dt) for l in range(self.lanes)]

    def one(self, name, shape, dt=F32):
        return self.ctx.enter_context(self.nc.sbuf_tensor(f"{self.name}_{name}", shape, dt))

    def bank(self, name):
        return self.ctx.enter_context(self.nc.psum_tensor(f"{self.name}_{name}", [P, 512], F32))

    def banks(self, name):
        return [self.bank(f"{name}{l}") for l in range(self.lanes)]

    def sem(self, name):
        return self.semaphore(f"{self.name}_{name}")

    def sems(self, name):
        return [self.sem(f"{name}{l}") for l in range(self.lanes)]


def one_of(t, j):
    return t[:, j] if isinstance(j, int) else t[:, bass.ds(j, 1)].rearrange(
        "p a b -> p (a b)" if len(t.shape) == 3 else "p a b c -> p (a b) c")


def tile_of_two(t, j):
    return t[:, :, j] if isinstance(j, int) else t[:, :, bass.ds(j, 1)].rearrange("p a b -> p (a b)")


def column(t, j):
    return t[:, j:j + 1] if isinstance(j, int) else t[:, bass.ds(j, 1)]


def tile_rows(table, j):
    return table[j * P:(j + 1) * P] if isinstance(j, int) else table[bass.ds(j * P, P)]


def row_bounds(pool):
    found = {}
    for row in (P * NHI - 1, SLOTS - 1, SLOTS, N_NODES - 1, N_EDGES - 1):
        found[row] = pool.alloc_register(f"before_bound{row}"), pool.alloc_register(f"bound{row}")
        pool.reg_mov(found[row][0], row - 1)
    return found


def gather(pool, out, table, index, bound):
    kept, bound = bound
    pool.reg_alu(bound, kept, 1, ALU.add)
    return pool.indirect_dma_start(out=out, out_offset=None, in_=table, in_offset=bass.IndirectOffsetOnAxis(ap=index, axis=0),
                                   bounds_check=bound, oob_is_err=False)


def scatter(pool, table, index, src, bound):
    kept, bound = bound
    pool.reg_alu(bound, kept, 1, ALU.add)
    return pool.indirect_dma_start(out=table, out_offset=bass.IndirectOffsetOnAxis(ap=index, axis=0), in_=src, in_offset=None,
                                   bounds_check=bound, oob_is_err=False)


(R_SRC, R_DST, R_EDGE, R_WRITE_DST, R_WEIGHT, R_SRC_KEY, R_DST_KEY, R_DST_OUT, R_SRC_IN, R_SRC_OUT, R_WRITE_SRC,
 R_PLACE) = range(12)
OWN_FIELDS = R_DST_OUT
FIELDS = 12
NHI = -(-(PAD_NODE + 1) // P)
FAR = float(1 << 16)
BY_DST, BY_SRC = 0, 1


def phase_order(nc, c, a, d, e):
    DV = ["lo", "hi", "before", "rank", "kept"]
    AC = ["turned bf16", "turned f32", "histogram"]
    PE = ["turned", "same", "rank"]
    STAGES = ["one-hot", "turn", "turned", "same", "before", "snapshot", "add", "look", "keep"]
    n_rounds = TILES // 2
    with ExitStack() as ctx:
        w = Work(nc, ctx, "order", FEW)
        keys = w.one("keys", [P, 2, TILES], I32)
        parts = w.one("parts", [P, 2, 2, TILES], I32)
        lof = w.one("lof", [P, 2, TILES])
        hif = w.one("hif", [P, 2, TILES])
        keyf = w.one("keyf", [P, 2, TILES])
        weight = w.one("weight", [P, TILES])
        edge = w.one("edge", [P, TILES])
        entry, rank = e.entry, e.rank
        ramp = w.one("ramp", [P, NHI])
        earlier = w.one("earlier", [P, P])
        onlo, onloT = w.sb("onlo", [P, P], BF16), w.sb("onloT", [P, P], BF16)
        onloTf = w.sb("onloTf", [P, P])
        onhi = w.sb("onhi", [P, NHI], BF16)
        lesser = w.sb("lesser", [P, P], BF16)
        history = w.sb("history", [P, NHI])
        product = w.sb("product", [P, NHI])
        found = w.sb("found", [P, 1])
        zero = w.one("zero", [P, NHI])
        zerob = w.one("zerob", [P, NHI], BF16)
        counts = w.one("counts", [P, 2, NHI])
        running = w.one("running", [P, 2, NHI])
        total = w.one("total", [P, 2])
        offset = w.one("offset", [P, 2])
        start = w.one("start", [P, 2, NHI])
        starts = w.one("starts", [P, NHI, 2], I32)
        work = w.banks("work")
        hist = [w.bank("hist0"), w.bank("hist1")]
        loaded, made, prepared, setup = w.sem("loaded"), w.sem("made"), w.sem("prepared"), w.sem("setup")
        pe_done, act_done, dve_done = w.sems("pe_done"), w.sems("act_done"), w.sems("dve_done")
        added = [w.sem("added0"), w.sem("added1")]
        snapped = [w.sem("snapped0"), w.sem("snapped1")]
        table_step, table_stored, sums_done = w.sem("table_step"), w.sem("table_stored"), w.sem("sums_done")

        with nc.Block() as block:
            @block.sync
            def _(sp):
                sp.wait_ge(made, 8)
                for k, name in ((BY_DST, "dst"), (BY_SRC, "src")):
                    sp.dma_start(keys[0:EDGE_ROWS, k, :], a[name].rearrange("(p t) -> p t", t=TILES)).then_inc(loaded, 16)
                sp.dma_start(weight[0:EDGE_ROWS, :], a["edge_weight"].rearrange("(p t) -> p t", t=TILES)).then_inc(loaded, 16)
                sp.wait_ge(table_step, 9)
                sp.dma_start(d["starts"].rearrange("(p h) k -> p h k", p=P), starts[:, :, :]).then_inc(table_stored, 16)
                sp.wait_ge(table_stored, 16)

            @block.gpsimd
            def _(pool):
                pool.memset(keys[:, :, :], PAD_NODE).then_inc(made, 1)
                pool.memset(weight[:, :], 0.0).then_inc(made, 1)
                pool.memset(zero[:, :], 0.0).then_inc(made, 1)
                pool.memset(zerob[:, :], 0.0).then_inc(made, 1)
                pool.memset(earlier[:, :], 1.0).then_inc(made, 1)
                pool.iota(ramp[:, :], pattern=[[1, NHI]], base=0, channel_multiplier=0,
                          allow_small_or_imprecise_dtypes=True).then_inc(made, 1)
                pool.iota(edge[:, :], pattern=[[1, TILES]], base=0, channel_multiplier=TILES,
                          allow_small_or_imprecise_dtypes=True).then_inc(made, 1)
                pool.wait_ge(made, 7)
                pool.affine_select(out=earlier[:, :], in_=earlier[:, :], compare_op=ALU.is_gt, fill=0.0,
                                   base=0, pattern=[[1, P]], channel_multiplier=-1).then_inc(made, 1)

            @block.vector
            def _(dve):
                dve.wait_ge(loaded, 48)
                flat = keys[:, :, :]
                nc.vector.tensor_scalar(parts[:, 0], flat, P - 1, None, ALU.bitwise_and).then_inc(prepared, 1)
                nc.vector.tensor_scalar(parts[:, 1], flat, 7, None, ALU.logical_shift_right).then_inc(prepared, 1)
                nc.vector.tensor_copy(keyf[:, :, :], flat).then_inc(prepared, 1)
                dve.wait_ge(prepared, 3)
                nc.vector.tensor_copy(lof[:, :, :], parts[:, 0]).then_inc(prepared, 1)
                nc.vector.tensor_copy(hif[:, :, :], parts[:, 1]).then_inc(prepared, 1)
                dve.wait_ge(prepared, 5)
                nc.vector.scalar_tensor_tensor(entry[:, :, :], lof[:, :, :], float(NHI), hif[:, :, :], ALU.mult, ALU.add)\
                    .then_inc(prepared, 1)
                dve.wait_ge(prepared, 6)

                def onehot(l, j):
                    k, t = l // 2, 2 * j + l % 2
                    if again(j):
                        dve.wait_ge(pe_done[l], count(PE, j - 1, "rank"))
                    nc.vector.tensor_scalar(onlo[l][:, :], ramp[:, 0:P], column(lof[:, k], t), None, ALU.is_equal)\
                        .then_inc(dve_done[l], 1)
                    nc.vector.tensor_scalar(onhi[l][:, :], ramp[:, :], column(hif[:, k], t), None, ALU.is_equal)\
                        .then_inc(dve_done[l], 1)

                def before(l, j):
                    dve.wait_ge(pe_done[l], count(PE, j, "same"))
                    nc.vector.tensor_tensor(lesser[l][:, :], work[l][:, 0:P], earlier[:, :], ALU.mult).then_inc(dve_done[l], 1)

                def keep(l, j):
                    k, t = l // 2, 2 * j + l % 2
                    dve.wait_ge(pe_done[l], count(PE, j, "rank"))
                    if again(j):
                        dve.wait_ge(dve_done[l], count(DV, j - 1, "kept"))
                    nc.vector.tensor_tensor_reduce(product[l][:, :], work[l][:, 0:NHI], onhi[l][:, :], 1.0, 0.0,
                                                   ALU.mult, ALU.add, found[l][:, :]).then_inc(dve_done[l], 1)
                    dve.wait_ge(dve_done[l], count(DV, j, "rank"))
                    nc.vector.tensor_copy(column(rank[:, k], t), found[l][:, :]).then_inc(dve_done[l], 1)

                rounds(dve, STAGES, {"one-hot": onehot, "before": before, "keep": keep}, n_rounds, FEW)
                dve.wait_ge(sums_done, 1)
                for k in range(2):
                    nc.vector.tensor_tensor_scan(running[:, k, :], counts[:, k, :], zero[:, :], 0.0, ALU.add, ALU.add)\
                        .then_inc(table_step, 1)
                dve.wait_ge(table_step, 2)
                nc.vector.tensor_copy(total[:, :], running[:, :, NHI - 1]).then_inc(table_step, 1)
                dve.wait_ge(sums_done, 2)
                nc.vector.tensor_copy(offset[:, :], work[0][:, 0:2]).then_inc(table_step, 1)
                dve.wait_ge(table_step, 4)
                for k in range(2):
                    nc.vector.scalar_tensor_tensor(start[:, k, :], running[:, k, :], offset[:, k:k + 1], counts[:, k, :],
                                                   ALU.add, ALU.subtract).then_inc(table_step, 1)
                dve.wait_ge(table_step, 6)
                nc.vector.tensor_scalar(counts[:, :, :], counts[:, :, :], 0.0, None, ALU.is_gt).then_inc(table_step, 1)
                dve.wait_ge(table_step, 7)
                nc.vector.scalar_tensor_tensor(running[:, :, :], start[:, :, :], -float(SLOTS), counts[:, :, :], ALU.add, ALU.mult)\
                    .then_inc(table_step, 1)
                dve.wait_ge(table_step, 8)
                nc.vector.tensor_scalar(starts[:, :, :].rearrange("p h k -> p k h"), running[:, :, :], float(SLOTS), None,
                                        ALU.add).then_inc(table_step, 1)

            @block.scalar
            def _(act):
                def turned(l, j):
                    act.wait_ge(pe_done[l], count(PE, j, "turned"))
                    nc.scalar.activation(onloT[l][:, :], work[l][:, 0:P // 2].bitcast(BF16), ACT.Copy).then_inc(act_done[l], 1)
                    nc.scalar.activation(onloTf[l][:, :], work[l][:, 0:P // 2].bitcast(BF16), ACT.Copy).then_inc(act_done[l], 1)

                def snapshot(l, j):
                    k, t = l // 2, 2 * j + l % 2
                    act.wait_ge(added[k], t + 1)
                    if again(j):
                        act.wait_ge(pe_done[l], count(PE, j - 1, "rank"))
                    nc.scalar.activation(history[l][:, :], hist[k][:, 0:NHI], ACT.Copy).then_inc(act_done[l], 1)

                rounds(act, STAGES, {"turned": turned, "snapshot": snapshot}, n_rounds, FEW)
                for k in range(2):
                    act.wait_ge(added[k], TILES + 2)
                    last = nc.scalar.activation(counts[:, k, :], hist[k][:, 0:NHI], ACT.Copy)
                last.then_inc(sums_done, 1)

            @block.tensor
            def _(pe):
                pe.wait_ge(made, 8)
                for k in range(2):
                    pe.matmul(hist[k][:, 0:NHI], zerob[:, 0:P], zerob[:, :], start=True, stop=True).then_inc(added[k], 1)

                def turn(l, j):
                    pe.wait_ge(dve_done[l], count(DV, j, "lo"))
                    if again(j):
                        pe.wait_ge(dve_done[l], count(DV, j - 1, "rank"))
                    pe.transpose(work[l][:, 0:P // 2].bitcast(BF16), onlo[l][:, :], c.identb[:, :]).then_inc(pe_done[l], 1)

                def same(l, j):
                    pe.wait_ge(act_done[l], count(AC, j, "turned f32"))
                    pe.matmul(work[l][:, 0:P], onloT[l][:, :], onloT[l][:, :], start=True, stop=True).then_inc(pe_done[l], 1)

                def add(l, j):
                    k, t = l // 2, 2 * j + l % 2
                    pe.wait_ge(dve_done[l], count(DV, j, "hi"))
                    pe.wait_ge(act_done[l], count(AC, j, "histogram"))
                    pe.matmul(hist[k][:, 0:NHI], onlo[l][:, :], onhi[l][:, :], start=False, stop=True,
                              skip_group_check=True).then_inc(added[k], 1)

                def look(l, j):
                    pe.wait_ge(dve_done[l], count(DV, j, "before"))
                    pe.matmul(work[l][:, 0:NHI], onloTf[l][:, :], history[l][:, :], start=True, stop=False)
                    pe.matmul(work[l][:, 0:NHI], lesser[l][:, :], onhi[l][:, :], start=False, stop=True).then_inc(pe_done[l], 1)

                rounds(pe, STAGES, {"turn": turn, "same": same, "add": add, "look": look}, n_rounds, FEW)
                for k in range(2):
                    pe.matmul(hist[k][:, 0:NHI], zerob[:, 0:P], zerob[:, :], start=False, stop=True,
                              skip_group_check=True).then_inc(added[k], 1)
                pe.wait_ge(table_step, 3)
                pe.matmul(work[0][:, 0:2], earlier[:, :], total[:, :], start=True, stop=True).then_inc(sums_done, 1)

        away = w.one("away", [P, 2, TILES])
        step = w.sem("record_step")
        with nc.Block() as block:
            @block.vector
            def _(dve):
                v = nc.vector
                field = lambda f: e.own[:, :, f]
                v.tensor_scalar(away[:, :, :], rank[:, :, :], 0.0, None, ALU.is_gt).then_inc(step, 1)
                dve.wait_ge(step, 1)
                v.scalar_tensor_tensor(field(R_WRITE_DST), away[:, BY_DST, :], FAR, keyf[:, BY_DST, :], ALU.mult, ALU.add).then_inc(step, 1)
                v.scalar_tensor_tensor(e.write_src[:, :], away[:, BY_SRC, :], FAR, keyf[:, BY_SRC, :], ALU.mult, ALU.add).then_inc(step, 1)
                v.tensor_scalar(field(R_SRC), keyf[:, BY_SRC, :], float(N_NODES - 1), None, ALU.min).then_inc(step, 1)
                v.tensor_scalar(field(R_DST), keyf[:, BY_DST, :], float(N_NODES - 1), None, ALU.min).then_inc(step, 1)
                v.tensor_scalar(field(R_EDGE), edge[:, :], float(N_EDGES - 1), None, ALU.min).then_inc(step, 1)
                for f, values in ((R_WEIGHT, weight[:, :]), (R_SRC_KEY, keyf[:, BY_SRC, :]), (R_DST_KEY, keyf[:, BY_DST, :])):
                    v.tensor_copy(e.own[:, :, f].bitcast(F32), values).then_inc(step, 1)


class Records:
    MADE = ["own", "starts", "places", "away", "place", "write"]

    def __init__(self, nc, w, c, d, e):
        self.nc, self.c, self.d, self.e = nc, c, d, e
        self.near = w.sb("near", [P, 4], I32)
        self.point, self.spot = w.sb("point", [P, 2], I32), w.sb("spot", [P, 2], I32)
        self.sent = w.sb("sent", [P, FIELDS], I32)
        self.away = w.sb("away", [P, 1])
        self.pointed, self.fetched, self.made, self.written = (w.sems(s) for s in ("pointed", "fetched", "made", "written"))

    def look_up(self, pool):
        def go(l, j):
            if again(j):
                pool.wait_ge(self.fetched[l], 32 * j)
            pool.tensor_copy(self.point[l][:, :], tile_of_two(self.e.entry, AT(l, j))).then_inc(self.pointed[l], 1)
            pool.wait_ge(self.pointed[l], j + 1)
            if again(j):
                pool.wait_ge(self.made[l], count(self.MADE, j - 1, "write"))
            for k in range(2):
                gather(pool, self.near[l][:, 2 * k:2 * k + 2], self.d["starts"], self.point[l][:, k:k + 1], self.c.bound[P * NHI - 1])\
                    .then_inc(self.fetched[l], 16)
        return go

    def make(self, dve):
        v = self.nc.vector

        def go(l, j):
            near, sent, spot, made = self.near[l], self.sent[l], self.spot[l], self.made[l]
            dve.wait_ge(self.fetched[l], 32 * (j + 1))
            if again(j):
                dve.wait_ge(self.written[l], 32 * j)
            v.tensor_copy(sent[:, 0:OWN_FIELDS], one_of(self.e.own, AT(l, j))).then_inc(made, 1)
            v.tensor_copy(sent[:, R_DST_OUT:R_SRC_OUT + 1], near[:, 1:4]).then_inc(made, 1)
            v.tensor_tensor(spot[:, :], near[:, 0:4:3], tile_of_two(self.e.rank, AT(l, j)), ALU.add).then_inc(made, 1)
            v.tensor_scalar(self.away[l][:, :], near[:, 2:3], float(SLOTS), FAR, ALU.is_lt, ALU.mult).then_inc(made, 1)
            dve.wait_ge(made, count(self.MADE, j, "places"))
            v.tensor_copy(sent[:, R_PLACE:R_PLACE + 1], spot[:, 0:1]).then_inc(made, 1)
            dve.wait_ge(made, count(self.MADE, j, "away"))
            v.tensor_tensor(sent[:, R_WRITE_SRC:R_WRITE_SRC + 1], self.away[l][:, :], column(self.e.write_src, AT(l, j)), ALU.max)\
                .then_inc(made, 1)
        return go

    def send(self, pool):
        def go(l, j):
            pool.wait_ge(self.made[l], count(self.MADE, j, "write"))
            for k, name in ((BY_DST, "by_dst"), (BY_SRC, "by_src")):
                scatter(pool, self.d[name], self.spot[l][:, k:k + 1], self.sent[l][:, :], self.c.bound[SLOTS - 1]).then_inc(self.written[l], 16)
        return go

    def finish(self, pool):
        for l in range(LANES):
            pool.wait_ge(self.written[l], 32 * ROUNDS)


def allocate_order(nc, ctx):
    e = Chip()
    e.entry = ctx.enter_context(nc.sbuf_tensor("entry", [P, 2, TILES], I32))
    e.rank = ctx.enter_context(nc.sbuf_tensor("rank", [P, 2, TILES], F32))
    e.own = ctx.enter_context(nc.sbuf_tensor("own_fields", [P, TILES, OWN_FIELDS], I32))
    e.write_src = ctx.enter_context(nc.sbuf_tensor("write_src", [P, TILES], F32))
    return e


def allocate_edges(nc, ctx, c):
    def sb(name, shape, dt=F32):
        return ctx.enter_context(nc.sbuf_tensor(name, shape, dt))

    c.rec = [sb("rec_by_dst", [P, TILES, FIELDS], I32), sb("rec_by_src", [P, TILES, FIELDS], I32)]
    c.key = [sb("key_by_dst", [P, TILES]), sb("key_by_src", [P, TILES])]
    c.meets = [[sb(f"meets_{e}_{k}", [TILES, TILES]) for e in ("before", "after")] for k in range(2)]
    c.inv = [[sb(f"inv_{n}_{k}", [P, TILES]) for n in ("count", "weight")] for k in range(2)]
    c.state = sb("state", [P, TILES, 2, D])


def phase_keys(nc, c, d):
    with ExitStack() as ctx:
        w = Work(nc, ctx, "keys", FEW)
        turned = w.sb("turned", [TILES, P])
        short = w.sb("short", [TILES, P], U16)
        inside = [w.one(f"inside{k}", [TILES, 2, P], BF16) for k in range(2)]
        diagonal = [[w.one(f"diagonal{k}{e}", [TILES, TILES]) for e in range(2)] for k in range(2)]
        ones = w.one("ones", [TILES, TILES])
        near = [w.one("near_before", [TILES, TILES]), w.one("near_after", [TILES, TILES])]
        banks = w.banks("bank")
        zeros = w.one("zeros", [P, D])
        loaded, taken, turns, copied, shortened, stored, made, marked, spread, met = (w.sem(s) for s in (
            "loaded", "taken", "turns", "copied", "shortened", "stored", "made", "marked", "spread", "met"))
        with nc.Block() as block:
            @block.sync
            def _(sp):
                for k, name in ((BY_DST, "by_dst"), (BY_SRC, "by_src")):
                    sp.dma_start(c.rec[k][:, :, :], d[name].rearrange("(t p) f -> p t f", p=P)).then_inc(loaded, 16)
                sp.wait_ge(made, 4)
                for name in ("into", "from"):
                    sp.dma_start(d[name][SLOTS:SLOTS + P], zeros[:, :]).then_inc(stored, 16)
                sp.wait_ge(shortened, 2)
                for k in range(2):
                    sp.dma_start(d["key_rows"][k].rearrange("(t p) -> t p", p=P), short[k][:, :]).then_inc(stored, 16)
                sp.wait_ge(marked, 8)
                for k in range(2):
                    for i in range(PARTS):
                        sp.dma_start(d["inside"][k, i].rearrange("e (t p) -> t e p", p=P), inside[k][:, :, :]).then_inc(stored, 16)
                sp.wait_ge(stored, 64 + 32 * PARTS)

            @block.gpsimd
            def _(pool):
                pool.memset(zeros[:, :], 0.0).then_inc(made, 1)
                pool.memset(ones[:, :], 1.0).then_inc(made, 1)
                for m in near:
                    pool.memset(m[:, :], 1.0).then_inc(made, 1)
                pool.wait_ge(made, 4)
                for m, s in zip(near, (-1, 1)):
                    pool.affine_select(out=m[:, :], in_=m[:, :], compare_op=ALU.is_gt, fill=0.0, base=0,
                                       pattern=[[-s, TILES]], channel_multiplier=s).then_inc(made, 1)

            @block.vector
            def _(dve):
                dve.wait_ge(loaded, 32)
                for k, f in ((BY_DST, R_DST_KEY), (BY_SRC, R_SRC_KEY)):
                    nc.vector.tensor_copy(c.key[k][:, :], c.rec[k][:, :, f].bitcast(F32)).then_inc(taken, 1)
                dve.wait_ge(copied, 2)
                for k in range(2):
                    nc.vector.tensor_copy(short[k][:, :], turned[k][:, :]).then_inc(shortened, 1)
                    for e, at in ((0, 0), (1, P - 1)):
                        edge = turned[k][:, at:at + 1]
                        nc.vector.tensor_scalar(inside[k][:, e, :], turned[k][:, :], edge, None, ALU.is_equal).then_inc(marked, 1)
                        nc.vector.tensor_scalar(diagonal[k][e][:, :], c.ident[0:TILES, 0:TILES], edge, None, ALU.mult).then_inc(marked, 1)
                dve.wait_ge(made, 6)
                for k in range(2):
                    dve.wait_ge(spread, 2 * (k + 1))
                    for e, at in ((0, P - 1), (1, 0)):
                        nc.vector.scalar_tensor_tensor(c.meets[k][e][:, :], banks[2 * k + e][0:TILES, 0:TILES], turned[k][:, at:at + 1],
                                                       near[e][:, :], ALU.is_equal, ALU.mult).then_inc(met, 1)

            @block.tensor
            def _(pe):
                pe.wait_ge(taken, 2)
                for k in range(2):
                    pe.transpose(banks[k][0:TILES, 0:P], c.key[k][:, :], c.ident[:, :]).then_inc(turns, 1)
                pe.wait_ge(made, 6)
                pe.wait_ge(marked, 8)
                for k in range(2):
                    for e in range(2):
                        pe.matmul(banks[2 * k + e][0:TILES, 0:TILES], ones[:, :], diagonal[k][e][:, :], start=True, stop=True)\
                            .then_inc(spread, 1)

            @block.scalar
            def _(act):
                for k in range(2):
                    act.wait_ge(turns, k + 1)
                    nc.scalar.activation(turned[k][:, :], banks[k][0:TILES, 0:P], ACT.Copy).then_inc(copied, 1)


SET = 4
PARTS = 3
SUM_ROUNDS = TILES // (SET * LANES)


def set_rows(table, g):
    rows = table[g * SET * P:(g + 1) * SET * P] if isinstance(g, int) else table[bass.ds(g * (SET * P), SET * P)]
    return rows.rearrange("(u p) d -> p u d", p=P)


def set_of(t, g):
    return t[:, g * SET:(g + 1) * SET] if isinstance(g, int) else t[:, bass.ds(g * SET, SET)]


def phase_sum(nc, c, d, tag, order, source, width, inv, target):
    gathered = source is not None and source[1] is not None
    with ExitStack() as ctx:
        w = Work(nc, ctx, tag)
        sums = w.one("sums", [P, TILES, width])
        ends = [w.one(f"ends{e}", [TILES, width]) for e in range(2)]
        msg = w.sb("msg", [P, SET, width])
        keys = w.sb("keys", [P, SET, P], U16)
        equal = w.sb("equal", [P, SET, P])
        index = w.sb("index", [P, SET], I32)
        bank = w.banks("bank")
        ends_moved, joined_made, joined_copied, split = (w.sem(s) for s in ("ends_moved", "joined_made", "joined_copied", "split"))
        key_row = d["key_rows"][order]

        def row_of(g):
            r = key_row[g * SET * P:(g + 1) * SET * P] if isinstance(g, int) else key_row[bass.ds(g * (SET * P), SET * P)]
            return r.partition_broadcast(P)

        loaded, got, pointed = w.sems("loaded"), w.sems("got"), w.sems("pointed")
        compared, multiplied, kept = w.sems("compared"), w.sems("multiplied"), w.sems("kept")
        STAGES = ["load", "", "compare", "multiply", "keep"]
        per = 1 if gathered or source is None else 2
        with nc.Block() as block:
            @block.sync
            def _(sp):
                def load(l, j):
                    if again(j):
                        sp.wait_ge(multiplied[l], j)
                    sp.dma_start(keys[l][:, :, :].rearrange("p u e -> p (u e)"), row_of(AT(l, j))).then_inc(loaded[l], 16)
                    if per == 2:
                        sp.dma_start(msg[l][:, :, :], set_rows(source[0], AT(l, j))).then_inc(loaded[l], 16)

                rounds(sp, STAGES, {"load": load}, SUM_ROUNDS)

            if gathered:
                @block.gpsimd
                def _(pool):
                    def fetch(l, j):
                        if again(j):
                            pool.wait_ge(multiplied[l], j)
                        pool.tensor_copy(index[l][:, :], set_of(c.rec[order], AT(l, j))[:, :, source[1]]).then_inc(pointed[l], 1)
                        pool.wait_ge(pointed[l], j + 1)
                        for u in range(SET):
                            gather(pool, msg[l][:, u, :], source[0], index[l][:, u:u + 1], c.bound[SLOTS - 1]).then_inc(got[l], 16)

                    rounds(pool, STAGES, {"load": fetch}, SUM_ROUNDS)

            @block.vector
            def _(dve):
                def compare(l, j):
                    dve.wait_ge(loaded[l], 16 * per * (j + 1))
                    if again(j):
                        dve.wait_ge(multiplied[l], j)
                    mine = set_of(c.key[order], AT(l, j))
                    for u in range(SET):
                        last = nc.vector.tensor_scalar(equal[l][:, u, :], keys[l][:, u, :], mine[:, u:u + 1], None,
                                                       ALU.is_equal)
                    if source is None:
                        nc.vector.memset(msg[l][:, :, 0], 1.0)
                        last = nc.vector.tensor_copy(msg[l][:, :, 1], set_of(c.rec[order], AT(l, j))[:, :, R_WEIGHT].bitcast(F32))
                    last.then_inc(compared[l], 1)

                rounds(dve, STAGES, {"compare": compare}, SUM_ROUNDS)

            @block.tensor
            def _(pe):
                def multiply(l, j):
                    pe.wait_ge(compared[l], j + 1)
                    if gathered:
                        pe.wait_ge(got[l], 16 * SET * (j + 1))
                    if again(j):
                        pe.wait_ge(kept[l], j)
                    for u in range(SET):
                        last = pe.matmul(bank[l][:, u * width:(u + 1) * width], equal[l][:, u, :], msg[l][:, u, :], start=True, stop=True)
                    last.then_inc(multiplied[l], 1)

                rounds(pe, STAGES, {"multiply": multiply}, SUM_ROUNDS)

            @block.scalar
            def _(act):
                def keep(l, j):
                    act.wait_ge(multiplied[l], j + 1)
                    into = set_of(sums, AT(l, j))
                    if inv is None:
                        last = nc.scalar.activation(into, bank[l][:, 0:SET * width].rearrange("p (u d) -> p u d", u=SET), ACT.Copy)
                    else:
                        scale = set_of(inv, AT(l, j))
                        for u in range(SET):
                            last = nc.scalar.activation(into[:, u, :], bank[l][:, u * width:(u + 1) * width], ACT.Copy,
                                                        scale=scale[:, u:u + 1])
                    last.then_inc(kept[l], 1)

                rounds(act, STAGES, {"keep": keep}, SUM_ROUNDS)

        carried, rest = msg[0][0:TILES, 0:2, :], (msg[2][0:TILES, 0:2, :], msg[3][0:TILES, 0:2, :])
        parts = msg[1][0:TILES, 0:PARTS, :].rearrange("t i d -> t (i d)").bitcast(BF16)\
            .rearrange("t (i e d) -> t i e d", i=PARTS, e=2)
        carry_dram = d["carried2" if width == 2 else "carried"]
        with nc.Block() as block:
            @block.sync
            def _(sp):
                for e, at in ((0, 0), (1, P - 1)):
                    sp.dma_start(ends[e][:, :], sums[at:at + 1, :, :].rearrange("a t d -> a (t d)")).then_inc(ends_moved, 16)
                sp.wait_ge(split, 5)
                for i in range(PARTS):
                    sp.dma_start(carry_dram[2 * i:2 * i + 2].rearrange("e (t d) -> t e d", t=TILES), parts[:, i]).then_inc(ends_moved, 16)
                sp.wait_ge(ends_moved, 32 + 16 * PARTS)

            @block.vector
            def _(dve):
                dve.wait_ge(joined_copied, 1)
                nc.vector.tensor_copy(parts[:, 0], carried).then_inc(split, 1)
                dve.wait_ge(split, 1)
                nc.vector.tensor_tensor(rest[0], carried, parts[:, 0], ALU.subtract).then_inc(split, 1)
                dve.wait_ge(split, 2)
                nc.vector.tensor_copy(parts[:, 1], rest[0]).then_inc(split, 1)
                dve.wait_ge(split, 3)
                nc.vector.tensor_tensor(rest[1], rest[0], parts[:, 1], ALU.subtract).then_inc(split, 1)
                dve.wait_ge(split, 4)
                nc.vector.tensor_copy(parts[:, 2], rest[1]).then_inc(split, 1)

            @block.tensor
            def _(pe):
                pe.wait_ge(ends_moved, 32)
                for e in range(2):
                    last = pe.matmul(bank[0][0:TILES, e * width:(e + 1) * width], c.meets[order][e][:, :], ends[1 - e][:, :],
                                     start=True, stop=True)
                last.then_inc(joined_made, 1)

            @block.scalar
            def _(act):
                act.wait_ge(joined_made, 1)
                nc.scalar.activation(carried, bank[0][0:TILES, 0:2 * width].rearrange("p (e d) -> p e d", e=2), ACT.Copy)\
                    .then_inc(joined_copied, 1)

        loaded, multiplied = w.sems("loaded2"), w.sems("multiplied2")
        summed, owned, stored, pointed = w.sems("summed"), w.sems("owned"), w.sems("stored"), w.sems("pointed2")
        def halves(t):
            return t[0:2 * PARTS, 0:SET // 2, :].rearrange("r u d -> r (u d)").bitcast(BF16)

        carry, inside = [halves(m) for m in msg], [halves(k) for k in equal]
        result = equal
        STAGES = ["load", "", "multiply", "sum", "store"]
        final = target == "out"
        with nc.Block() as block:
            @block.sync
            def _(sp):
                inside_dram = d["inside"][order].rearrange("i e s -> (i e) s")

                def columns(t, g, size):
                    return t[:, g * size:(g + 1) * size] if isinstance(g, int) else t[:, bass.ds(g * size, size)]

                def load(l, j):
                    if again(j) and final:
                        sp.wait_ge(stored[l], 16 * SET * j)
                    elif again(j):
                        sp.wait_ge(multiplied[l], j)
                    sp.dma_start(inside[l], columns(inside_dram, AT(l, j), SET * P))\
                        .then_inc(loaded[l], 16)
                    sp.dma_start(carry[l], columns(carry_dram, AT(l, j), SET * width))\
                        .then_inc(loaded[l], 16)

                rounds(sp, STAGES, {"load": load}, SUM_ROUNDS)

            if target in ("into", "from"):
                @block.scalar
                def _(act):
                    def store(l, j):
                        act.wait_ge(summed[l], j + 1)
                        act.dma_start(set_rows(d[target], AT(l, j)), set_of(sums, AT(l, j))).then_inc(stored[l], 16)

                    rounds(act, STAGES, {"store": store}, SUM_ROUNDS)
                    for l in range(LANES):
                        act.wait_ge(stored[l], 16 * SUM_ROUNDS)

            @block.vector
            def _(dve):
                def add(l, j):
                    dve.wait_ge(multiplied[l], j + 1)
                    out = result[l][:, :, :] if final else set_of(sums if isinstance(target, str) else target, AT(l, j))
                    nc.vector.tensor_tensor(out, bank[l][:, 0:SET * width].rearrange("p (u d) -> p u d", u=SET), set_of(sums, AT(l, j)),
                                            ALU.add).then_inc(summed[l], 1)
                    if final:
                        dve.wait_ge(summed[l], j + 1)
                        own = c.state[:, AT(l, j) * SET:(AT(l, j) + 1) * SET, 1, :] if isinstance(j, int) else \
                            c.state[:, bass.ds(AT(l, j) * SET, SET), 1, :]
                        nc.vector.tensor_tensor(result[l][:, :, :], result[l][:, :, :], own, ALU.add).then_inc(owned[l], 1)

                rounds(dve, STAGES, {"sum": add}, SUM_ROUNDS)

            @block.tensor
            def _(pe):
                def multiply(l, j):
                    pe.wait_ge(loaded[l], 32 * (j + 1))
                    if again(j):
                        pe.wait_ge(summed[l], j)
                    for u in range(SET):
                        last = pe.matmul(bank[l][:, u * width:(u + 1) * width], inside[l][:, u * P:(u + 1) * P],
                                         carry[l][:, u * width:(u + 1) * width], start=True, stop=True)
                    last.then_inc(multiplied[l], 1)

                rounds(pe, STAGES, {"multiply": multiply}, SUM_ROUNDS)

            if final:
                @block.gpsimd
                def _(pool):
                    def store(l, j):
                        if again(j):
                            pool.wait_ge(stored[l], 16 * SET * j)
                        pool.tensor_copy(index[l][:, :], set_of(c.rec[order], AT(l, j))[:, :, R_WRITE_DST]).then_inc(pointed[l], 1)
                        pool.wait_ge(pointed[l], j + 1)
                        pool.wait_ge(owned[l], j + 1)
                        for u in range(SET):
                            scatter(pool, d["out"], index[l][:, u:u + 1], result[l][:, u, :], c.bound[N_NODES - 1])\
                                .then_inc(stored[l], 16)

                    rounds(pool, STAGES, {"store": store}, SUM_ROUNDS)
                    for l in range(LANES):
                        pool.wait_ge(stored[l], 16 * SET * SUM_ROUNDS)


def phase_degrees(nc, c, d):
    with ExitStack() as outer:
        totals = [outer.enter_context(nc.sbuf_tensor(f"totals{k}", [P, TILES, 2], F32)) for k in range(2)]
        for k in range(2):
            phase_sum(nc, c, d, f"deg{k}", k, None, 2, None, totals[k])
        with ExitStack() as ctx:
            w = Work(nc, ctx, "degrees")
            present, safe, counted = (w.one(s, [P, TILES]) for s in ("present", "safe", "counted"))
            step = w.sem("step")
            with nc.Block() as block:
                @block.vector
                def _(dve):
                    v = nc.vector
                    for k in range(2):
                        base = 7 * k
                        if k:
                            dve.wait_ge(step, base)
                        v.tensor_scalar(counted[:, :], totals[k][:, :, 0], 1.0, None, ALU.max).then_inc(step, 1)
                        v.tensor_scalar(present[:, :], totals[k][:, :, 1], 0.0, None, ALU.is_gt).then_inc(step, 1)
                        dve.wait_ge(step, base + 2)
                        v.reciprocal(c.inv[k][0][:, :], counted[:, :]).then_inc(step, 1)
                        v.scalar_tensor_tensor(safe[:, :], totals[k][:, :, 1], 1.0, present[:, :], ALU.subtract, ALU.mult).then_inc(step, 1)
                        dve.wait_ge(step, base + 4)
                        v.tensor_scalar(safe[:, :], safe[:, :], 1.0, None, ALU.add).then_inc(step, 1)
                        dve.wait_ge(step, base + 5)
                        v.reciprocal(safe[:, :], safe[:, :]).then_inc(step, 1)
                        dve.wait_ge(step, base + 6)
                        v.tensor_tensor(c.inv[k][1][:, :], safe[:, :], present[:, :], ALU.mult).then_inc(step, 1)


class Norm:

    def __init__(self, w, p, u):
        self.nc, self.p, self.u = w.nc, p, u
        self.stats = w.sb("stats", [p, u, 6])
        self.mv = w.sb("mv", [p, u, 2])
        self.var = w.sb("var", [p, u])
        self.rstd = w.sb("rstd", [p, u])
        self.shift = w.sb("shift", [p, u])
        self.pause = w.one("pause", [p, 1])

    def moments(self, dve, l, src, done, at):
        v = self.nc.vector
        for i in range(self.u):
            last = v.bn_stats(self.stats[l][:, i, :], src[:, i, :])
        last.then_inc(done[l], 1)
        dve.wait_ge(done[l], at("stats"))
        v.memset(self.pause[:, :], 0.0)
        for i in range(self.u):
            last = v.bn_aggr(self.mv[l][:, i, :], self.stats[l][:, i, :])
        last.then_inc(done[l], 1)

    def factor_base(self, dve, l, src, done, at):
        self.moments(dve, l, src, done, at)
        dve.wait_ge(done[l], at("mean"))
        self.variance(l).then_inc(done[l], 1)

    def variance(self, l):
        return self.nc.vector.tensor_scalar(self.var[l][:, :], self.mv[l][:, :, 1], LN_EPS, None, ALU.add)

    def power(self, pool, c, l):
        return pool.tensor_tensor(self.rstd[l][:, :], self.var[l][:, :], c.power[0:self.p, 0:self.u], ALU.pow)

    def move(self, l):
        return self.nc.vector.scalar_tensor_tensor(self.shift[l][:, :], self.mv[l][:, :, 0], -1.0, self.rstd[l][:, :],
                                                   ALU.mult, ALU.mult)

    def apply_here(self, out, src, l):
        for i in range(self.u):
            last = self.nc.vector.tensor_scalar(out[l][:, i, :], src[:, i, :], self.mv[l][:, i, 0:1],
                                                self.rstd[l][:, i:i + 1], ALU.subtract, ALU.mult)
        return last

    def apply(self, out, src, l):
        for i in range(self.u):
            last = self.nc.scalar.activation(out[l][:, i, :], src[l][:, i, :], ACT.Relu, bias=self.shift[l][:, i:i + 1],
                                             scale=self.rstd[l][:, i:i + 1])
        return last


def pair(t, j):
    return t[:, j] if isinstance(j, int) else t[:, bass.ds(j, 1)].rearrange("p a u d -> p (a u) d")


def fields(rec, j, lo, hi):
    return rec[:, j, lo:hi] if isinstance(j, int) else rec[:, bass.ds(j, 1), lo:hi].rearrange("p a f -> p (a f)")


SELF = lambda bank: bank[:, 0:512].rearrange("p (u c) -> p u c", u=2)[:, :, 0:D]
SENT = slice(D, 2 * D)


def turn_pair(pe, c, out, src, l):
    for i in range(2):
        last = pe.transpose(out[:, i * P:(i + 1) * P], src[l][:, i, :], c.ident[:, :])
    return last


def layer_products(pe, bank, hT, both):
    pe.matmul(bank[:, 0:2 * D], hT[:, 0:P], both, start=True, stop=True)
    return pe.matmul(bank[:, 2 * D:3 * D], hT[:, P:2 * P], both[:, 0:D], start=True, stop=True)


def phase_enter(nc, c, d, a):
    DV = ["stats", "mean", "var", "h", "own"]
    PO = ["index", "rstd"]
    AC = ["hT", "message"]
    PE = ["turn", "products"]
    STAGES = ["load", "", "", "norm", "", "rstd", "h", "turn", "hT", "products", "", "own", "store"]
    with ExitStack() as ctx:
        w = Work(nc, ctx, "enter")
        index, x, h, hT, message = w.sb("index", [P, 2], I32), w.sb("x", [P, 2, D]), w.sb("h", [P, 2, D]), w.sb("hT", [P, 2 * P]), w.sb("message", [P, D])
        norm = Norm(w, P, 2)
        bank = w.banks("bank")
        loaded, stored, kept = w.sems("loaded"), w.sems("stored"), w.sems("kept")
        pe_done, act_done, dve_done, pool_done = w.sems("pe_done"), w.sems("act_done"), w.sems("dve_done"), w.sems("pool_done")
        with nc.Block() as block:
            @block.gpsimd
            def _(pool):
                def load(l, j):
                    if again(j):
                        pool.wait_ge(loaded[l], 32 * j)
                        pool.wait_ge(dve_done[l], count(DV, j - 1, "h"))
                        pool.wait_ge(kept[l], 16 * j)
                    pool.tensor_copy(index[l][:, :], fields(c.rec[BY_DST], AT(l, j), R_SRC, R_DST + 1)).then_inc(pool_done[l], 1)
                    pool.wait_ge(pool_done[l], count(PO, j, "index"))
                    for i in range(2):
                        gather(pool, x[l][:, i, :], a["x"], index[l][:, i:i + 1], c.bound[N_NODES - 1]).then_inc(loaded[l], 16)

                def factors(l, j):
                    pool.wait_ge(dve_done[l], count(DV, j, "var"))
                    norm.power(pool, c, l).then_inc(pool_done[l], 1)

                rounds(pool, STAGES, {"load": load, "rstd": factors}, ROUNDS)

            @block.sync
            def _(sp):
                def keep(l, j):
                    sp.wait_ge(loaded[l], 32 * (j + 1))
                    sp.dma_start(tile_rows(d["kept"], AT(l, j)), x[l][:, :, :]).then_inc(kept[l], 16)

                def store(l, j):
                    sp.wait_ge(act_done[l], count(AC, j, "message"))
                    sp.dma_start(tile_rows(d["message"], AT(l, j)), message[l][:, :]).then_inc(stored[l], 16)

                rounds(sp, STAGES, {"norm": keep, "store": store}, ROUNDS)
                for l in range(LANES):
                    sp.wait_ge(stored[l], 16 * ROUNDS)
                    sp.wait_ge(kept[l], 16 * ROUNDS)

            @block.vector
            def _(dve):
                def moments(l, j):
                    dve.wait_ge(loaded[l], 32 * (j + 1))
                    norm.factor_base(dve, l, x[l], dve_done, lambda s: count(DV, j, s))

                def apply(l, j):
                    dve.wait_ge(pool_done[l], count(PO, j, "rstd"))
                    if again(j):
                        dve.wait_ge(pe_done[l], count(PE, j - 1, "turn"))
                    norm.apply_here(h, x[l], l).then_inc(dve_done[l], 1)

                def own(l, j):
                    dve.wait_ge(pe_done[l], count(PE, j, "products"))
                    dve.wait_ge(act_done[l], count(AC, j, "message"))
                    nc.vector.tensor_tensor(pair(c.state, AT(l, j)), SELF(bank[l]), bc(c.bias[:, ROW_OF[B_L0], :], 2), ALU.add)\
                        .then_inc(dve_done[l], 1)

                rounds(dve, STAGES, {"norm": moments, "h": apply, "own": own}, ROUNDS)

            @block.scalar
            def _(act):
                def relu(l, j):
                    act.wait_ge(pe_done[l], count(PE, j, "turn"))
                    nc.scalar.activation(hT[l][:, :], bank[l][:, 0:2 * P], ACT.Relu).then_inc(act_done[l], 1)

                def send(l, j):
                    act.wait_ge(pe_done[l], count(PE, j, "products"))
                    if again(j):
                        act.wait_ge(stored[l], 16 * j)
                    nc.scalar.activation(message[l][:, :], bank[l][:, SENT], ACT.Copy).then_inc(act_done[l], 1)

                rounds(act, STAGES, {"hT": relu, "own": send}, ROUNDS)

            @block.tensor
            def _(pe):
                def turn(l, j):
                    pe.wait_ge(dve_done[l], count(DV, j, "h"))
                    if again(j):
                        pe.wait_ge(dve_done[l], count(DV, j - 1, "own"))
                    turn_pair(pe, c, bank[l], h, l).then_inc(pe_done[l], 1)

                def products(l, j):
                    pe.wait_ge(act_done[l], count(AC, j, "hT"))
                    layer_products(pe, bank[l], hT[l], c.wrT[:, 0, :]).then_inc(pe_done[l], 1)

                rounds(pe, STAGES, {"turn": turn, "products": products}, ROUNDS)


def phase_layer(nc, c, d, layer):
    DV = ["sum", "own"]
    AC = ["hT", "message"]
    PE = ["turn", "products"]
    STAGES = ["load", "sum", "", "turn", "hT", "products", "own", "", "", "store"]
    with ExitStack() as ctx:
        w = Work(nc, ctx, f"layer{layer}")
        index, near, s, hT, message = w.sb("index", [P, 1], I32), w.sb("near", [P, 2, D]), w.sb("s", [P, 2, D]), w.sb("hT", [P, 2 * P]), w.sb("message", [P, D])
        bank = w.banks("bank")
        loaded, gathered, stored, pointed = w.sems("loaded"), w.sems("gathered"), w.sems("stored"), w.sems("pointed")
        pe_done, act_done, dve_done = w.sems("pe_done"), w.sems("act_done"), w.sems("dve_done")
        with nc.Block() as block:
            @block.gpsimd
            def _(pool):
                def load(l, j):
                    if again(j):
                        pool.wait_ge(gathered[l], 16 * j)
                        pool.wait_ge(dve_done[l], count(DV, j - 1, "sum"))
                    pool.tensor_copy(index[l][:, :], fields(c.rec[BY_DST], AT(l, j), R_SRC_IN, R_SRC_IN + 1)).then_inc(pointed[l], 1)
                    pool.wait_ge(pointed[l], j + 1)
                    gather(pool, near[l][:, 0, :], d["into"], index[l][:, :], c.bound[SLOTS]).then_inc(gathered[l], 16)

                rounds(pool, STAGES, {"load": load}, ROUNDS)

            @block.sync
            def _(sp):
                def load(l, j):
                    if again(j):
                        sp.wait_ge(dve_done[l], count(DV, j - 1, "sum"))
                    sp.dma_start(near[l][:, 1, :], tile_rows(d["into"], AT(l, j))).then_inc(loaded[l], 16)

                def store(l, j):
                    sp.wait_ge(act_done[l], count(AC, j, "message"))
                    sp.dma_start(tile_rows(d["message"], AT(l, j)), message[l][:, :]).then_inc(stored[l], 16)

                rounds(sp, STAGES, {"load": load, "store": store}, ROUNDS)
                for l in range(LANES):
                    sp.wait_ge(stored[l], 16 * ROUNDS)

            @block.vector
            def _(dve):
                def add(l, j):
                    dve.wait_ge(loaded[l], 16 * (j + 1))
                    dve.wait_ge(gathered[l], 16 * (j + 1))
                    if again(j):
                        dve.wait_ge(pe_done[l], count(PE, j - 1, "turn"))
                    nc.vector.tensor_tensor(s[l][:, :, :], near[l][:, :, :], pair(c.state, AT(l, j)), ALU.add).then_inc(dve_done[l], 1)

                def own(l, j):
                    dve.wait_ge(pe_done[l], count(PE, j, "products"))
                    dve.wait_ge(act_done[l], count(AC, j, "message"))
                    nc.vector.tensor_tensor(pair(c.state, AT(l, j)), SELF(bank[l]), bc(c.bias[:, ROW_OF[B_L0 + layer], :], 2), ALU.add)\
                        .then_inc(dve_done[l], 1)

                rounds(dve, STAGES, {"sum": add, "own": own}, ROUNDS)

            @block.scalar
            def _(act):
                def relu(l, j):
                    act.wait_ge(pe_done[l], count(PE, j, "turn"))
                    if again(j):
                        act.wait_ge(pe_done[l], count(PE, j - 1, "products"))
                    nc.scalar.activation(hT[l][:, :], bank[l][:, 0:2 * P], ACT.Relu).then_inc(act_done[l], 1)

                def send(l, j):
                    act.wait_ge(pe_done[l], count(PE, j, "products"))
                    if again(j):
                        act.wait_ge(stored[l], 16 * j)
                    nc.scalar.activation(message[l][:, :], bank[l][:, SENT], ACT.Copy).then_inc(act_done[l], 1)

                rounds(act, STAGES, {"hT": relu, "own": send}, ROUNDS)

            @block.tensor
            def _(pe):
                def turn(l, j):
                    pe.wait_ge(dve_done[l], count(DV, j, "sum"))
                    if again(j):
                        pe.wait_ge(dve_done[l], count(DV, j - 1, "own"))
                    turn_pair(pe, c, bank[l], s, l).then_inc(pe_done[l], 1)

                def products(l, j):
                    pe.wait_ge(act_done[l], count(AC, j, "hT"))
                    layer_products(pe, bank[l], hT[l], c.wrT[:, layer, :]).then_inc(pe_done[l], 1)

                rounds(pe, STAGES, {"turn": turn, "products": products}, ROUNDS)


def phase_join(nc, c, d):
    DV = ["sum", "x", "stats", "mean", "var", "kept", "shift"]
    PO = ["index", "rstd"]
    AC = ["h", "message"]
    STAGES = timetable(120, {"load": 0, "sum": 45, "x": 63, "rstd": 82, "shift": 92, "h": 96, "message": 107, "store": 115})
    with ExitStack() as ctx:
        w = Work(nc, ctx, "join")
        index, near, s, x0, x = w.sb("index", [P, 1], I32), w.sb("near", [P, 2, D]), w.sb("s", [P, 2, D]), w.sb("x0", [P, 2, D]), w.sb("x", [P, 2, D])
        h, message = w.sb("h", [P, 2, D]), w.sb("message", [P, 2, D])
        norm = Norm(w, P, 2)
        loaded, gathered, stored = w.sems("loaded"), w.sems("gathered"), w.sems("stored")
        act_done, dve_done, pool_done = w.sems("act_done"), w.sems("dve_done"), w.sems("pool_done")
        with nc.Block() as block:
            @block.gpsimd
            def _(pool):
                def load(l, j):
                    if again(j):
                        pool.wait_ge(gathered[l], 16 * j)
                        pool.wait_ge(dve_done[l], count(DV, j - 1, "x"))
                    pool.tensor_copy(index[l][:, :], fields(c.rec[BY_DST], AT(l, j), R_SRC_IN, R_SRC_IN + 1)).then_inc(pool_done[l], 1)
                    pool.wait_ge(pool_done[l], count(PO, j, "index"))
                    gather(pool, near[l][:, 0, :], d["into"], index[l][:, :], c.bound[SLOTS]).then_inc(gathered[l], 16)

                def factors(l, j):
                    pool.wait_ge(dve_done[l], count(DV, j, "var"))
                    norm.power(pool, c, l).then_inc(pool_done[l], 1)

                rounds(pool, STAGES, {"load": load, "rstd": factors}, ROUNDS)

            @block.sync
            def _(sp):
                def load(l, j):
                    if again(j):
                        sp.wait_ge(dve_done[l], count(DV, j - 1, "x"))
                    sp.dma_start(near[l][:, 1, :], tile_rows(d["into"], AT(l, j))).then_inc(loaded[l], 16)
                    sp.dma_start(x0[l][:, :, :], tile_rows(d["kept"], AT(l, j))).then_inc(loaded[l], 16)

                def store(l, j):
                    sp.wait_ge(act_done[l], count(AC, j, "message"))
                    sp.dma_start(tile_rows(d["message"], AT(l, j)), message[l][:, 0, :]).then_inc(stored[l], 16)
                    sp.dma_start(tile_rows(d["reverse"], AT(l, j)), message[l][:, 1, :]).then_inc(stored[l], 16)

                rounds(sp, STAGES, {"load": load, "store": store}, ROUNDS)
                for l in range(LANES):
                    sp.wait_ge(stored[l], 32 * ROUNDS)

            @block.vector
            def _(dve):
                def own(l, j):
                    dve.wait_ge(loaded[l], 32 * (j + 1))
                    nc.vector.tensor_tensor(s[l][:, :, :], x0[l][:, :, :], pair(c.state, AT(l, j)), ALU.add).then_inc(dve_done[l], 1)

                def add(l, j):
                    dve.wait_ge(loaded[l], 32 * (j + 1))
                    dve.wait_ge(gathered[l], 16 * (j + 1))
                    dve.wait_ge(dve_done[l], count(DV, j, "sum"))
                    if again(j):
                        dve.wait_ge(act_done[l], count(AC, j - 1, "h"))
                    nc.vector.tensor_tensor(x[l][:, :, :], near[l][:, :, :], s[l][:, :, :], ALU.add).then_inc(dve_done[l], 1)
                    dve.wait_ge(dve_done[l], count(DV, j, "x"))
                    norm.factor_base(dve, l, x[l], dve_done, lambda s: count(DV, j, s))
                    nc.vector.tensor_copy(pair(c.state, AT(l, j)), x[l][:, :, :]).then_inc(dve_done[l], 1)

                def shift(l, j):
                    dve.wait_ge(pool_done[l], count(PO, j, "rstd"))
                    norm.move(l).then_inc(dve_done[l], 1)

                rounds(dve, STAGES, {"sum": own, "x": add, "shift": shift}, ROUNDS)

            @block.scalar
            def _(act):
                def apply(l, j):
                    act.wait_ge(dve_done[l], count(DV, j, "shift"))
                    norm.apply(h, x, l).then_inc(act_done[l], 1)

                def send(l, j):
                    act.wait_ge(act_done[l], count(AC, j, "h"))
                    if again(j):
                        act.wait_ge(stored[l], 32 * j)
                    nc.scalar.activation(message[l][:, :, :], h[l][:, :, :], ACT.Copy,
                                         scale=fields(c.rec[BY_DST], AT(l, j), R_WEIGHT, R_WEIGHT + 1).bitcast(F32)).then_inc(act_done[l], 1)

                rounds(act, STAGES, {"h": apply, "message": send}, ROUNDS)


def phase_edges(nc, c, d, a):
    DV = ["filter", "product"]
    AC = ["eT", "tanh"]
    PE = ["turn", "products"]
    STAGES = ["load", "", "turn", "eT", "", "products", "tanh", "filter", "store"]
    with ExitStack() as ctx:
        w = Work(nc, ctx, "edges")
        index, e, eT, g, f = w.sb("index", [P, 1], I32), w.sb("e", [P, D]), w.sb("eT", [P, P]), w.sb("g", [P, D]), w.sb("f", [P, D])
        bank = w.banks("bank")
        gathered, stored, pointed = w.sems("gathered"), w.sems("stored"), w.sems("pointed")
        pe_done, act_done, dve_done = w.sems("pe_done"), w.sems("act_done"), w.sems("dve_done")
        with nc.Block() as block:
            @block.gpsimd
            def _(pool):
                def load(l, j):
                    if again(j):
                        pool.wait_ge(gathered[l], 16 * j)
                        pool.wait_ge(pe_done[l], count(PE, j - 1, "turn"))
                    pool.tensor_copy(index[l][:, :], fields(c.rec[BY_DST], AT(l, j), R_EDGE, R_EDGE + 1)).then_inc(pointed[l], 1)
                    pool.wait_ge(pointed[l], j + 1)
                    gather(pool, e[l][:, :], a["edge_attr_128"], index[l][:, :], c.bound[N_EDGES - 1]).then_inc(gathered[l], 16)

                rounds(pool, STAGES, {"load": load}, ROUNDS)

            @block.sync
            def _(sp):
                def store(l, j):
                    sp.wait_ge(dve_done[l], count(DV, j, "product"))
                    sp.dma_start(tile_rows(d["filter"], AT(l, j)), f[l][:, :]).then_inc(stored[l], 16)

                rounds(sp, STAGES, {"store": store}, ROUNDS)
                for l in range(LANES):
                    sp.wait_ge(stored[l], 16 * ROUNDS)

            @block.vector
            def _(dve):
                def go(l, j):
                    dve.wait_ge(act_done[l], count(AC, j, "tanh"))
                    if again(j):
                        dve.wait_ge(stored[l], 16 * j)
                    nc.vector.scalar_tensor_tensor(f[l][:, :], g[l][:, :], 1.0, bank[l][:, D:2 * D], ALU.add, ALU.mult)\
                        .then_inc(dve_done[l], 1)
                    dve.wait_ge(dve_done[l], count(DV, j, "filter"))
                    nc.vector.tensor_scalar(f[l][:, :], f[l][:, :], 0.5, None, ALU.mult).then_inc(dve_done[l], 1)

                rounds(dve, STAGES, {"filter": go}, ROUNDS)

            @block.scalar
            def _(act):
                def copy(l, j):
                    act.wait_ge(pe_done[l], count(PE, j, "turn"))
                    nc.scalar.activation(eT[l][:, :], bank[l][:, 0:P], ACT.Copy).then_inc(act_done[l], 1)

                def tanh(l, j):
                    act.wait_ge(pe_done[l], count(PE, j, "products"))
                    if again(j):
                        act.wait_ge(dve_done[l], count(DV, j - 1, "filter"))
                    nc.scalar.activation(g[l][:, :], bank[l][:, 0:D], ACT.Tanh, scale=0.5).then_inc(act_done[l], 1)

                rounds(act, STAGES, {"eT": copy, "tanh": tanh}, ROUNDS)

            @block.tensor
            def _(pe):
                def turn(l, j):
                    pe.wait_ge(gathered[l], 16 * (j + 1))
                    if again(j):
                        pe.wait_ge(dve_done[l], count(DV, j - 1, "filter"))
                    pe.transpose(bank[l][:, 0:P], e[l][:, :], c.ident[:, :]).then_inc(pe_done[l], 1)

                def products(l, j):
                    pe.wait_ge(act_done[l], count(AC, j, "eT"))
                    o = bank[l][:, 0:2 * D]
                    pe.matmul(o, c.ones3[:, :], c.bias3[:, B_GATE:B_FILT + 1, :].rearrange("a b d -> a (b d)"), start=True, stop=False)
                    pe.matmul(o, eT[l][:, :], c.wgf[:, :, :].rearrange("p g d -> p (g d)"), start=False, stop=True)\
                        .then_inc(pe_done[l], 1)

                rounds(pe, STAGES, {"turn": turn, "products": products}, ROUNDS)


def phase_gru(nc, c, d):
    DV = ["stats1", "mean1", "var1", "h", "r hn src", "r hn dst", "n in src", "n in dst", "h - n", "z mix", "x", "stats2", "mean2",
          "var2", "h5", "own", "message"]
    PO = ["index", "rstd1", "n + x1", "rstd2"]
    AC = ["hT", "intoT", "outT", "rz src", "rz dst", "n", "h5T"]
    PE = ["turn h", "turn out", "gates src", "gates dst", "turn h5", "node"]
    STAGES = ["load", "", "norm1", "rstd1", "h", "turn h", "hT", "gates src", "", "gates dst", "", "rz", "n in", "n", "",
              "mix", "norm2", "rstd2", "h5", "turn h5", "h5T", "node", "", "own", "store"]
    with ExitStack() as ctx:
        w = Work(nc, ctx, "gru", FEW)
        index = w.sb("index", [P, 3], I32)
        h, h5 = w.sb("h", [P, 2, D]), w.sb("h5", [P, 2, D])
        into, out = w.sb("into", [P, 2, D]), w.sb("out", [P, 2, D])
        hT, outT = w.sb("hT", [P, 4 * P]), w.sb("outT", [P, 2 * P])
        rz = w.sb("rz", [P, 2, 2 * D])
        u, n, apart, both, own = (w.sb(s, [P, 2, D]) for s in ("u", "n", "apart", "both", "own"))
        filt, message = w.sb("filt", [P, 1, D]), w.sb("message", [P, 1, D])
        norm = Norm(w, P, 2)
        left, right = w.banks("left"), w.banks("right")
        loaded, gathered, stored = w.sems("loaded"), w.sems("gathered"), w.sems("stored")
        pe_done, act_done, dve_done, pool_done = w.sems("pe_done"), w.sems("act_done"), w.sems("dve_done"), w.sems("pool_done")
        with nc.Block() as block:
            @block.gpsimd
            def _(pool):
                def load(l, j):
                    if again(j):
                        pool.wait_ge(gathered[l], 48 * j)
                        pool.wait_ge(pe_done[l], count(PE, j - 1, "turn out"))
                    pool.tensor_copy(index[l][:, :], fields(c.rec[BY_DST], FEW * j + l, R_DST_OUT, R_SRC_OUT + 1)).then_inc(pool_done[l], 1)
                    pool.wait_ge(pool_done[l], count(PO, j, "index"))
                    gather(pool, into[l][:, 0, :], d["into"], index[l][:, 1:2], c.bound[SLOTS]).then_inc(gathered[l], 16)
                    gather(pool, out[l][:, 0, :], d["from"], index[l][:, 2:3], c.bound[SLOTS]).then_inc(gathered[l], 16)
                    gather(pool, out[l][:, 1, :], d["from"], index[l][:, 0:1], c.bound[SLOTS]).then_inc(gathered[l], 16)

                def factors(k):
                    def go(l, j):
                        pool.wait_ge(dve_done[l], count(DV, j, "var" + k))
                        norm.power(pool, c, l).then_inc(pool_done[l], 1)
                    return go

                def mix(l, j):
                    pool.wait_ge(act_done[l], count(AC, j, "n"))
                    if again(j):
                        pool.wait_ge(dve_done[l], count(DV, j - 1, "x"))
                    pool.tensor_tensor(both[l][:, :, :], n[l][:, :, :], pair(c.state, FEW * j + l), ALU.add).then_inc(pool_done[l], 1)

                rounds(pool, STAGES, {"load": load, "rstd1": factors("1"), "rstd2": factors("2"), "mix": mix}, TILES // FEW, FEW)

            @block.sync
            def _(sp):
                def load(l, j):
                    if again(j):
                        sp.wait_ge(pe_done[l], count(PE, j - 1, "turn h"))
                        sp.wait_ge(dve_done[l], count(DV, j - 1, "message"))
                    sp.dma_start(into[l][:, 1, :], tile_rows(d["into"], FEW * j + l)).then_inc(loaded[l], 16)
                    sp.dma_start(filt[l][:, 0, :], tile_rows(d["filter"], FEW * j + l)).then_inc(loaded[l], 16)

                def store(l, j):
                    sp.wait_ge(dve_done[l], count(DV, j, "message"))
                    sp.dma_start(tile_rows(d["kept"], FEW * j + l), own[l][:, :, :]).then_inc(stored[l], 16)
                    sp.dma_start(tile_rows(d["reverse"], FEW * j + l), message[l][:, 0, :]).then_inc(stored[l], 16)

                rounds(sp, STAGES, {"load": load, "store": store}, TILES // FEW, FEW)
                for l in range(FEW):
                    sp.wait_ge(stored[l], 32 * TILES // FEW)

            @block.vector
            def _(dve):
                def norm1(l, j):
                    norm.factor_base(dve, l, pair(c.state, FEW * j + l), dve_done, lambda s: count(DV, j, s + "1"))

                def apply1(l, j):
                    dve.wait_ge(pool_done[l], count(PO, j, "rstd1"))
                    if again(j):
                        dve.wait_ge(pe_done[l], count(PE, j - 1, "turn h"))
                    norm.apply_here(h, pair(c.state, FEW * j + l), l).then_inc(dve_done[l], 1)

                def n_in(l, j):
                    dve.wait_ge(act_done[l], count(AC, j, "rz dst"))
                    for i, bank in enumerate((left, right)):
                        nc.vector.scalar_tensor_tensor(u[l][:, i, :], rz[l][:, i, 0:D], 1.0, bank[l][:, 0:D], ALU.add, ALU.mult)\
                            .then_inc(dve_done[l], 1)
                    dve.wait_ge(dve_done[l], count(DV, j, "r hn dst"))
                    for i, bank in enumerate((left, right)):
                        nc.vector.scalar_tensor_tensor(u[l][:, i, :], u[l][:, i, :], 0.5, bank[l][:, 3 * D:4 * D], ALU.mult, ALU.add)\
                            .then_inc(dve_done[l], 1)

                def norm2(l, j):
                    dve.wait_ge(act_done[l], count(AC, j, "n"))
                    nc.vector.scalar_tensor_tensor(apart[l][:, :, :], h[l][:, :, :], 0.0, n[l][:, :, :], ALU.max, ALU.subtract)\
                        .then_inc(dve_done[l], 1)
                    dve.wait_ge(dve_done[l], count(DV, j, "h - n"))
                    nc.vector.scalar_tensor_tensor(u[l][:, :, :], rz[l][:, :, D:2 * D], 1.0, apart[l][:, :, :], ALU.add, ALU.mult)\
                        .then_inc(dve_done[l], 1)
                    dve.wait_ge(dve_done[l], count(DV, j, "z mix"))
                    dve.wait_ge(pool_done[l], count(PO, j, "n + x1"))
                    nc.vector.scalar_tensor_tensor(pair(c.state, FEW * j + l), u[l][:, :, :], 0.5, both[l][:, :, :], ALU.mult, ALU.add)\
                        .then_inc(dve_done[l], 1)
                    dve.wait_ge(dve_done[l], count(DV, j, "x"))
                    nc.vector.memset(norm.pause[:, :], 0.0)
                    norm.factor_base(dve, l, pair(c.state, FEW * j + l), dve_done, lambda s: count(DV, j, s + "2"))

                def apply2(l, j):
                    dve.wait_ge(pool_done[l], count(PO, j, "rstd2"))
                    norm.apply_here(h5, pair(c.state, FEW * j + l), l).then_inc(dve_done[l], 1)

                def node(l, j):
                    dve.wait_ge(pe_done[l], count(PE, j, "node"))
                    dve.wait_ge(loaded[l], 32 * (j + 1))
                    if again(j):
                        dve.wait_ge(stored[l], 32 * j)
                    nc.vector.tensor_tensor(own[l][:, :, :], right[l][:, 0:2 * D].rearrange("p (u d) -> p u d", u=2),
                                            bc(c.bias[:, ROW_OF[B_SHIFT], :], 2), ALU.add).then_inc(dve_done[l], 1)
                    nc.vector.tensor_tensor(message[l][:, 0, :], right[l][:, D:2 * D], filt[l][:, 0, :], ALU.mult).then_inc(dve_done[l], 1)

                rounds(dve, STAGES, {"norm1": norm1, "h": apply1, "n in": n_in, "norm2": norm2, "h5": apply2, "own": node}, TILES // FEW, FEW)

            @block.scalar
            def _(act):
                def copy(l, j):
                    act.wait_ge(pe_done[l], count(PE, j, "turn h"))
                    nc.scalar.activation(hT[l][:, 0:2 * P], left[l][:, 0:2 * P], ACT.Relu).then_inc(act_done[l], 1)
                    nc.scalar.activation(hT[l][:, 2 * P:4 * P], left[l][:, 2 * P:4 * P], ACT.Copy).then_inc(act_done[l], 1)
                    act.wait_ge(pe_done[l], count(PE, j, "turn out"))
                    nc.scalar.activation(outT[l][:, :], right[l][:, 0:2 * P], ACT.Copy).then_inc(act_done[l], 1)

                def rz_(l, j):
                    for i, (bank, side) in enumerate(((left, "gates src"), (right, "gates dst"))):
                        act.wait_ge(pe_done[l], count(PE, j, side))
                        nc.scalar.activation(rz[l][:, i, :], bank[l][:, D:3 * D], ACT.Tanh, scale=0.5).then_inc(act_done[l], 1)

                def n_(l, j):
                    act.wait_ge(dve_done[l], count(DV, j, "n in dst"))
                    nc.scalar.activation(n[l][:, :, :], u[l][:, :, :], ACT.Tanh).then_inc(act_done[l], 1)

                def copy5(l, j):
                    act.wait_ge(pe_done[l], count(PE, j, "turn h5"))
                    nc.scalar.activation(hT[l][:, 0:2 * P], left[l][:, 0:2 * P], ACT.Relu).then_inc(act_done[l], 1)

                rounds(act, STAGES, {"hT": copy, "rz": rz_, "n": n_, "h5T": copy5}, TILES // FEW, FEW)

            @block.tensor
            def _(pe):
                def turn(l, j):
                    pe.wait_ge(dve_done[l], count(DV, j, "h"))
                    pe.wait_ge(loaded[l], 32 * (j + 1))
                    pe.wait_ge(gathered[l], 48 * (j + 1))
                    if again(j):
                        pe.wait_ge(act_done[l], count(AC, j - 1, "h5T"))
                        pe.wait_ge(dve_done[l], count(DV, j - 1, "message"))
                    turn_pair(pe, c, left[l], h, l)
                    turn_pair(pe, c, left[l][:, 2 * P:4 * P], into, l).then_inc(pe_done[l], 1)
                    turn_pair(pe, c, right[l], out, l).then_inc(pe_done[l], 1)

                def gates(i, bank):
                    def go(l, j):
                        pe.wait_ge(act_done[l], count(AC, j, "outT"))
                        o, cols = bank[l], slice(i * P, (i + 1) * P)
                        pe.matmul(o[:, :], c.ones3[:, :], c.bias3[:, B_HN:B_IN + 1, :].rearrange("a b d -> a (b d)"), start=True, stop=False)
                        pe.matmul(o[:, 0:3 * D], hT[l][:, cols], c.whhT[:, :, :].rearrange("p g d -> p (g d)"), start=False, stop=False)
                        pe.matmul(o[:, D:4 * D], hT[l][:, 2 * P + i * P:2 * P + (i + 1) * P], c.wfwd[:, :, :].rearrange("p g d -> p (g d)"),
                                  start=False, stop=False)
                        last = pe.matmul(o[:, D:4 * D], outT[l][:, cols], c.wrev[:, :, :].rearrange("p g d -> p (g d)"), start=False, stop=True)
                        last.then_inc(pe_done[l], 1)
                    return go

                def turn5(l, j):
                    pe.wait_ge(dve_done[l], count(DV, j, "h5"))
                    turn_pair(pe, c, left[l], h5, l).then_inc(pe_done[l], 1)

                def node(l, j):
                    pe.wait_ge(act_done[l], count(AC, j, "h5T"))
                    for i in range(2):
                        o = right[l][:, i * D:(i + 1) * D]
                        pe.matmul(o, c.ones3[:, :], c.bias3[:, B_NODE_MSG, :], start=True, stop=False)
                        last = pe.matmul(o, hT[l][:, i * P:(i + 1) * P], c.wnode[:, :], start=False, stop=True)
                    last.then_inc(pe_done[l], 1)

                rounds(pe, STAGES, {"turn h": turn, "gates src": gates(0, left), "gates dst": gates(1, right), "turn h5": turn5, "node": node}, TILES // FEW, FEW)


def phase_filter(nc, c, d):
    DV = ["sum", "x", "stats", "mean", "var", "h", "out", "own"]
    PO = ["index", "rstd"]
    AC = ["hT", "message"]
    PE = ["turn", "products"]
    STAGES = ["load", "", "", "", "", "sum", "rstd", "h", "turn", "hT", "products", "own", "store", "", "", "", "", "", ""]
    with ExitStack() as ctx:
        w = Work(nc, ctx, "filter")
        index = w.sb("index", [P, 4], I32)
        near, s, own, x, h, y = (w.sb(n, [P, 2, D]) for n in ("near", "s", "own", "x", "h", "y"))
        hT, message = w.sb("hT", [P, 2 * P]), w.sb("message", [P, D])
        norm = Norm(w, P, 2)
        bank = w.banks("bank")
        loaded, gathered, stored, written = w.sems("loaded"), w.sems("gathered"), w.sems("stored"), w.sems("written")
        pe_done, act_done, dve_done, pool_done = w.sems("pe_done"), w.sems("act_done"), w.sems("dve_done"), w.sems("pool_done")
        with nc.Block() as block:
            @block.gpsimd
            def _(pool):
                def load(l, j):
                    if again(j):
                        pool.wait_ge(written[l], 16 * j)
                        pool.wait_ge(dve_done[l], count(DV, j - 1, "sum"))
                    pool.tensor_copy(index[l][:, :], fields(c.rec[BY_DST], AT(l, j), R_DST_OUT, R_WRITE_SRC + 1)).then_inc(pool_done[l], 1)
                    pool.wait_ge(pool_done[l], count(PO, j, "index"))
                    for i, at in ((0, 2), (1, 0)):
                        gather(pool, near[l][:, i, :], d["from"], index[l][:, at:at + 1], c.bound[SLOTS]).then_inc(gathered[l], 16)

                def factors(l, j):
                    pool.wait_ge(dve_done[l], count(DV, j, "var"))
                    norm.power(pool, c, l).then_inc(pool_done[l], 1)

                def write(l, j):
                    pool.wait_ge(dve_done[l], count(DV, j, "out"))
                    scatter(pool, d["out"], index[l][:, 3:4], y[l][:, 0, :], c.bound[N_NODES - 1]).then_inc(written[l], 16)

                rounds(pool, STAGES, {"load": load, "rstd": factors, "store": write}, ROUNDS)
                for l in range(LANES):
                    pool.wait_ge(written[l], 16 * ROUNDS)

            @block.sync
            def _(sp):
                def load(l, j):
                    if again(j):
                        sp.wait_ge(dve_done[l], count(DV, j - 1, "sum"))
                    sp.dma_start(own[l][:, :, :], tile_rows(d["kept"], AT(l, j))).then_inc(loaded[l], 16)

                def store(l, j):
                    sp.wait_ge(act_done[l], count(AC, j, "message"))
                    sp.dma_start(tile_rows(d["message"], AT(l, j)), message[l][:, :]).then_inc(stored[l], 16)

                rounds(sp, STAGES, {"load": load, "store": store}, ROUNDS)
                for l in range(LANES):
                    sp.wait_ge(stored[l], 16 * ROUNDS)

            @block.vector
            def _(dve):
                def add(l, j):
                    dve.wait_ge(loaded[l], 16 * (j + 1))
                    dve.wait_ge(gathered[l], 32 * (j + 1))
                    nc.vector.tensor_tensor(s[l][:, :, :], near[l][:, :, :], own[l][:, :, :], ALU.add).then_inc(dve_done[l], 1)
                    dve.wait_ge(dve_done[l], count(DV, j, "sum"))
                    nc.vector.scalar_tensor_tensor(x[l][:, :, :], s[l][:, :, :], 0.0, pair(c.state, AT(l, j)), ALU.max, ALU.add).then_inc(dve_done[l], 1)
                    dve.wait_ge(dve_done[l], count(DV, j, "x"))
                    norm.factor_base(dve, l, x[l], dve_done, lambda s: count(DV, j, s))

                def apply(l, j):
                    dve.wait_ge(pool_done[l], count(PO, j, "rstd"))
                    norm.apply_here(h, x[l], l).then_inc(dve_done[l], 1)

                def out(l, j):
                    dve.wait_ge(pe_done[l], count(PE, j, "products"))
                    dve.wait_ge(act_done[l], count(AC, j, "message"))
                    if again(j):
                        dve.wait_ge(written[l], 16 * j)
                    nc.vector.tensor_tensor(y[l][:, 0, :], bank[l][:, 0:D], x[l][:, 0, :], ALU.add).then_inc(dve_done[l], 1)
                    t = AT(l, j)
                    mine = c.state[:, t, 1, :] if isinstance(t, int) else c.state[:, bass.ds(t, 1), 1, :].rearrange("p a d -> p (a d)")
                    nc.vector.tensor_tensor(mine, bank[l][:, 2 * D:3 * D], x[l][:, 1, :], ALU.add).then_inc(dve_done[l], 1)

                rounds(dve, STAGES, {"sum": add, "h": apply, "own": out}, ROUNDS)

            @block.scalar
            def _(act):
                def relu(l, j):
                    act.wait_ge(pe_done[l], count(PE, j, "turn"))
                    nc.scalar.activation(hT[l][:, :], bank[l][:, 0:2 * P], ACT.Relu).then_inc(act_done[l], 1)

                def send(l, j):
                    act.wait_ge(pe_done[l], count(PE, j, "products"))
                    if again(j):
                        act.wait_ge(stored[l], 16 * j)
                    nc.scalar.activation(message[l][:, :], bank[l][:, SENT], ACT.Copy).then_inc(act_done[l], 1)

                rounds(act, STAGES, {"hT": relu, "own": send}, ROUNDS)

            @block.tensor
            def _(pe):
                def turn(l, j):
                    pe.wait_ge(dve_done[l], count(DV, j, "h"))
                    if again(j):
                        pe.wait_ge(dve_done[l], count(DV, j - 1, "own"))
                    turn_pair(pe, c, bank[l], h, l).then_inc(pe_done[l], 1)

                def products(l, j):
                    pe.wait_ge(act_done[l], count(AC, j, "hT"))
                    both = c.wout[:, :, :].rearrange("p g d -> p (g d)")
                    pe.matmul(bank[l][:, 0:2 * D], c.ones3[:, :], c.bias3[:, B_OUT:B_OUT + 2, :].rearrange("a b d -> a (b d)"),
                              start=True, stop=False)
                    pe.matmul(bank[l][:, 0:2 * D], hT[l][:, 0:P], both, start=False, stop=True)
                    o = bank[l][:, 2 * D:3 * D]
                    pe.matmul(o, c.ones3[:, :], c.bias3[:, B_OUT, :], start=True, stop=False)
                    pe.matmul(o, hT[l][:, P:2 * P], both[:, 0:D], start=False, stop=True).then_inc(pe_done[l], 1)

                rounds(pe, STAGES, {"turn": turn, "products": products}, ROUNDS)


def build(nc, a, out):
    def table(name, rows, cols, dt=F32):
        return nc.dram_tensor(name, [rows, cols], dt, kind="Internal").ap()

    d = {"out": out}
    d["starts"] = table("starts", P * NHI, 2, I32)
    d["by_dst"] = table("by_dst", SLOTS, FIELDS, I32)
    d["by_src"] = table("by_src", SLOTS, FIELDS, I32)
    d["key_rows"] = table("key_rows", 2, SLOTS, U16)
    d["inside"] = nc.dram_tensor("inside", [2, PARTS, 2, SLOTS], BF16, kind="Internal").ap()
    d["carried"] = table("carried", PARTS * 2, TILES * D, BF16)
    d["carried2"] = table("carried2", PARTS * 2, TILES * 2, BF16)
    d["into"] = table("into", SLOTS + P, D)
    d["from"] = table("from", SLOTS + P, D)
    d["message"] = table("message", SLOTS, D)
    d["reverse"] = table("reverse", SLOTS, D)
    d["filter"] = table("filter", SLOTS, D)
    d["kept"] = nc.dram_tensor("kept", [SLOTS, 2, D], F32, kind="Internal").ap()
    with ExitStack() as ctx:
        c = allocate(nc, ctx)
        c.bound = row_bounds(nc.gpsimd)
        phase_setup(nc, c, a)
        with ExitStack() as order:
            e = allocate_order(nc, order)
            phase_order(nc, c, a, d, e)
            phase_dense(nc, c, a["x"], out, d, e)
        allocate_edges(nc, ctx, c)
        phase_keys(nc, c, d)
        phase_degrees(nc, c, d)
        phase_enter(nc, c, d, a)
        for layer in (0, 1):
            phase_sum(nc, c, d, f"sum{layer}", BY_DST, (d["message"], None), D, c.inv[BY_DST][0], "into")
            phase_layer(nc, c, d, layer + 1)
        phase_sum(nc, c, d, "sum2", BY_DST, (d["message"], None), D, c.inv[BY_DST][0], "into")
        phase_join(nc, c, d)
        phase_sum(nc, c, d, "fwd", BY_DST, (d["message"], None), D, c.inv[BY_DST][1], "into")
        phase_sum(nc, c, d, "rev", BY_SRC, (d["reverse"], R_PLACE), D, c.inv[BY_SRC][1], "from")
        phase_edges(nc, c, d, a)
        phase_gru(nc, c, d)
        phase_sum(nc, c, d, "nodes", BY_SRC, (d["reverse"], R_PLACE), D, c.inv[BY_SRC][0], "from")
        phase_filter(nc, c, d)
        phase_sum(nc, c, d, "last", BY_DST, (d["message"], None), D, None, "out")


_INS = ['x', 'src', 'dst', 'edge_attr_128', 'edge_weight', 'L0_gnn_W_l', 'L0_gnn_b_l', 'L0_gnn_W_r', 'L1_gnn_W1',
        'L1_gnn_W2', 'L1_gnn_w_ih', 'L1_gnn_w_hh', 'L1_gnn_b_ih', 'L1_gnn_b_hh', 'L2_gnn_W_node', 'L2_gnn_b_node',
        'L2_gnn_W_gate', 'L2_gnn_b_gate', 'L2_gnn_W_filt', 'L2_gnn_b_filt', 'L2_gnn_bn_gamma', 'L2_gnn_bn_beta',
        'L2_gnn_bn_mean', 'L2_gnn_bn_var', 'L3_gnn_W_neigh', 'L3_gnn_b_neigh', 'L3_gnn_W_self', 'L3_gnn_b_self']


def kernel(**inputs):
    import numpy as np
    import concourse.bacc as bacc
    from concourse.bass_utils import run_bass_kernel_spmd

    nc = bacc.Bacc("TRN2", target_bir_lowering=False, num_devices=1)
    arrays, args = {}, {}
    for name in _INS:
        arrays[name] = np.ascontiguousarray(inputs[name])
        args[name] = nc.dram_tensor(name, arrays[name].shape, mybir.dt.from_np(arrays[name].dtype), kind="ExternalInput").ap()
    out = nc.dram_tensor("out", (N_NODES, D), F32, kind="ExternalOutput").ap()
    build(nc, args, out)
    r = run_bass_kernel_spmd(nc, [arrays], core_ids=[0])
    return r.results[0]["out"]
```
